# Optimizing a Trainium2 kernel written in Bass

```python
import numpy as np
import jax
import jax.numpy as jnp

def _softmax(x, axis=-1):
    return jax.nn.softmax(x, axis=axis)

def _gelu(x):
    return jax.nn.gelu(x, approximate=True)

def _silu(x):
    return jax.nn.silu(x)

def _sigmoid(x):
    return jax.nn.sigmoid(x)

def _layernorm(x, axis=-1, eps=1e-05):
    m = jnp.mean(x, axis=axis, keepdims=True)
    v = jnp.var(x, axis=axis, keepdims=True)
    return (x - m) / jnp.sqrt(v + eps)

def _scatter_add(tgt, idx, src, axis=0):
    return tgt.at[idx].add(src)

def _segment_sum(src, seg, n):
    return jax.ops.segment_sum(src, seg, n)
kernel_name = 'mk_xattn_ffn_d4_seqx_r4_81590e'

def setup_inputs(seed: int=0):
    np.random.seed(seed)
    _w = jnp.asarray

    def _rec_inputs():
        import jax
        import jax.numpy as jnp
        _rk = jax.random.key(seed)
        x = -0.000125 + 0.9999 * jax.random.normal(jax.random.fold_in(_rk, 1), (2, 1024, 256), jnp.float32)
        _lenS = 1024 - jax.random.randint(jax.random.fold_in(_rk, 7), (2,), 0, max(1, 1024 // 4) + 1, jnp.int32)
        _lenS2 = 77 - jax.random.randint(jax.random.fold_in(_rk, 8), (2,), 0, max(1, 77 // 4) + 1, jnp.int32)
        _ctx_1024P = jax.random.normal(jax.random.fold_in(_rk, 11), (2, 16, 256), jnp.float32)
        _ctx_1024c = jax.random.dirichlet(jax.random.fold_in(_rk, 511), 0.3 * jnp.ones((16,), jnp.float32), (2, 77))
        _ctx_1024t = jnp.einsum('bsk,bkd->bsd', _ctx_1024c, _ctx_1024P)
        _ctx_1024t = _ctx_1024t * jax.lax.rsqrt(jnp.mean(jnp.square(_ctx_1024t)) + 1e-12) * 0.953939
        ctx_1024 = -4.4511e-05 + 0.999885 * (_ctx_1024t + 0.3 * jax.random.normal(jax.random.fold_in(_rk, 611), (2, 77, 256), jnp.float32))
        _validS = jnp.arange(1024)[None, :] < _lenS[:, None]
        _validS2 = jnp.arange(77)[None, :] < _lenS2[:, None]
        _causal = jnp.tril(jnp.ones((1024, 1024), dtype=bool))
        mask_BxSxS2_bk0 = jnp.logical_not(jnp.broadcast_to(_validS2[:, None, :], (2, 1024, 77)))
        return (x, ctx_1024, mask_BxSxS2_bk0)
    x, ctx_1024, mask_BxSxS2_bk0 = _rec_inputs()

    def _L0_xattn_setup():
        import jax, jax.numpy as jnp
        import numpy as np
        H = 16
        D = 64
        SCALE = D ** (-0.5)
        TEXT = 77
        IMG = 16
        AUD = 32
        MAXREL = 16
        B, NQ, QD = (32, 256, 256)
        INNER = H * D

        def _heads(t):
            return t.reshape(t.shape[0], t.shape[1], H, D)
        key = jax.random.key(seed)
        ks = jax.random.split(key, 14)
        w = lambda k, s: jax.random.normal(k, s, jnp.float32) * 0.02
        return {'x': jax.random.normal(ks[0], (B, NQ, QD), jnp.float32), 'context': jax.random.normal(ks[1], (B, TEXT + IMG + AUD, QD), jnp.float32), 'Wq': w(ks[2], (QD, INNER)), 'Wk': w(ks[3], (QD, INNER)), 'Wv': w(ks[4], (QD, INNER)), 'Wk_ip': w(ks[5], (QD, INNER)), 'Wv_ip': w(ks[6], (QD, INNER)), 'Wk_ap': w(ks[7], (QD, INNER)), 'Wv_ap': w(ks[8], (QD, INNER)), 'Wo': w(ks[9], (INNER, QD)), 'bo': jnp.zeros((QD,), jnp.float32), 'rel_k': w(ks[10], (2 * MAXREL + 1, D)), 'rel_v': w(ks[11], (2 * MAXREL + 1, D)), 'alpha': jnp.zeros((), jnp.float32), 'beta': jnp.zeros((), jnp.float32)}
    _L0_xattn_all = _L0_xattn_setup()
    _L0_xattn_in = {k: v for k, v in _L0_xattn_all.items() if k in ('Wq', 'Wk', 'Wv', 'Wk_ip', 'Wv_ip', 'Wk_ap', 'Wv_ap', 'Wo', 'bo', 'rel_k', 'rel_v', 'alpha', 'beta')}
    del _L0_xattn_all

    def _L0_ffn_setup():
        import jax, jax.numpy as jnp
        import numpy as np
        H = 256
        I = 512
        E = 32
        B, S = (4, 512)

        def _grouped_mm(a, w, group_sizes):
            return jax.lax.ragged_dot(a, w, group_sizes)

        def _swiglu(x, gw, uw, dw):
            return jax.nn.silu(x @ gw) * (x @ uw) @ dw
        key = jax.random.key(seed)
        ks = jax.random.split(key, 8)
        scale = 0.02
        inp = {'hidden_states': jax.random.normal(ks[0], (B, S, H), dtype=jnp.float32), 'gate_w': jax.random.normal(ks[1], (H, E), dtype=jnp.float32) * scale, 'shared_gate_w': jax.random.normal(ks[2], (H, I), dtype=jnp.float32) * scale, 'shared_up_w': jax.random.normal(ks[3], (H, I), dtype=jnp.float32) * scale, 'shared_down_w': jax.random.normal(ks[4], (I, H), dtype=jnp.float32) * scale, 'routed_gate_w': jax.random.normal(ks[5], (E, H, I), dtype=jnp.float32) * scale, 'routed_up_w': jax.random.normal(ks[6], (E, H, I), dtype=jnp.float32) * scale, 'routed_down_w': jax.random.normal(ks[7], (E, I, H), dtype=jnp.float32) * scale}
        return inp
    _L0_ffn_all = _L0_ffn_setup()
    _L0_ffn_in = {k: v for k, v in _L0_ffn_all.items() if k in ('gate_w', 'shared_gate_w', 'shared_up_w', 'shared_down_w', 'routed_gate_w', 'routed_up_w', 'routed_down_w')}
    del _L0_ffn_all

    def _L1_xattn_setup():
        import jax, jax.numpy as jnp
        import numpy as np
        B, T, D, H = (4, 512, 256, 16)
        DK = D // H

        def _split_heads(x):
            b, t, _ = x.shape
            return x.reshape(b, t, H, DK).transpose(0, 2, 1, 3)
        key = jax.random.key(seed)
        ks = jax.random.split(key, 8)
        std = 1.0 / np.sqrt(2.0 * D)
        inp = {'q': jax.random.normal(ks[0], (B, T, D), jnp.float32), 'k': jax.random.normal(ks[1], (B, T, D), jnp.float32), 'v': jax.random.normal(ks[2], (B, T, D), jnp.float32), 'Wq': jax.random.normal(ks[3], (D, D), jnp.float32) * std, 'Wk': jax.random.normal(ks[4], (D, D), jnp.float32) * std, 'Wv': jax.random.normal(ks[5], (D, D), jnp.float32) * std, 'Wo': jax.random.normal(ks[6], (D, D), jnp.float32) * std, 'bq': jnp.zeros((D,), jnp.float32), 'bk': jnp.zeros((D,), jnp.float32), 'bv': jnp.zeros((D,), jnp.float32), 'bo': jnp.zeros((D,), jnp.float32)}
        return inp
    _L1_xattn_all = _L1_xattn_setup()
    _L1_xattn_in = {k: v for k, v in _L1_xattn_all.items() if k in ('Wq', 'Wk', 'Wv', 'Wo', 'bq', 'bk', 'bv', 'bo')}
    del _L1_xattn_all

    def _L1_ffn_setup():
        import jax, jax.numpy as jnp
        import numpy as np
        D_MODEL, D_FF, RANK = (256, 1024, 64)
        B, S = (4, 1024)
        key = jax.random.key(seed)
        ks = jax.random.split(key, 7)
        return {'x': jax.random.normal(ks[0], (B, S, D_MODEL), dtype=jnp.float32), 'U1': jax.random.normal(ks[1], (D_MODEL, RANK), dtype=jnp.float32) * 0.02, 'V1': jax.random.normal(ks[2], (RANK, D_FF), dtype=jnp.float32) * 0.02, 'b1': jnp.zeros((D_FF,), dtype=jnp.float32), 'U2': jax.random.normal(ks[3], (D_FF, RANK), dtype=jnp.float32) * 0.02, 'V2': jax.random.normal(ks[4], (RANK, D_MODEL), dtype=jnp.float32) * 0.02, 'b2': jnp.zeros((D_MODEL,), dtype=jnp.float32)}
    _L1_ffn_all = _L1_ffn_setup()
    _L1_ffn_in = {k: v for k, v in _L1_ffn_all.items() if k in ('U1', 'V1', 'b1', 'U2', 'V2', 'b2')}
    del _L1_ffn_all

    def _L2_xattn_setup():
        import jax, jax.numpy as jnp
        import numpy as np
        HIDDEN = 256
        HEADS = 16
        HEAD_DIM = HIDDEN // HEADS
        key = jax.random.key(seed)
        ks = jax.random.split(key, 11)
        B, S = (2, 512)
        s = 1.0 / np.sqrt(HIDDEN)
        return {'query': jax.random.normal(ks[0], (B, S, HIDDEN), jnp.float32), 'key': jax.random.normal(ks[1], (B, S, HIDDEN), jnp.float32), 'value': jax.random.normal(ks[2], (B, S, HIDDEN), jnp.float32), 'Wq': jax.random.uniform(ks[3], (HIDDEN, HIDDEN), jnp.float32, -s, s), 'bq': jax.random.uniform(ks[4], (HIDDEN,), jnp.float32, -s, s), 'Wk': jax.random.uniform(ks[5], (HIDDEN, HIDDEN), jnp.float32, -s, s), 'bk': jax.random.uniform(ks[6], (HIDDEN,), jnp.float32, -s, s), 'Wv': jax.random.uniform(ks[7], (HIDDEN, HIDDEN), jnp.float32, -s, s), 'bv': jax.random.uniform(ks[8], (HIDDEN,), jnp.float32, -s, s), 'Wo': jax.random.uniform(ks[9], (HIDDEN, HIDDEN), jnp.float32, -s, s), 'bo': jax.random.uniform(ks[10], (HIDDEN,), jnp.float32, -s, s)}
    _L2_xattn_all = _L2_xattn_setup()
    _L2_xattn_in = {k: v for k, v in _L2_xattn_all.items() if k in ('Wq', 'bq', 'Wk', 'bk', 'Wv', 'bv', 'Wo', 'bo')}
    del _L2_xattn_all

    def _L2_ffn_setup():
        import jax, jax.numpy as jnp
        import numpy as np
        INT8_MAX = 127.0

        def _absmax_scale(x, axes):
            amax = jnp.max(jnp.abs(x), axis=axes, keepdims=True)
            return jnp.maximum(amax, 1e-12) / INT8_MAX
        key = jax.random.key(seed)
        k1, k2 = jax.random.split(key)
        lhs = jax.random.normal(k1, (4, 2048, 256), dtype=jnp.float32)
        rhs = jax.random.normal(k2, (256, 256), dtype=jnp.float32)
        return {'lhs': lhs, 'rhs': rhs}
    _L2_ffn_all = _L2_ffn_setup()
    _L2_ffn_in = {k: v for k, v in _L2_ffn_all.items() if k in ('rhs',)}
    del _L2_ffn_all

    def _L3_xattn_setup():
        import jax, jax.numpy as jnp
        import numpy as np
        D_MODEL = 256
        N_HEADS = 16
        HEAD_DIM = D_MODEL // N_HEADS
        BATCH = 2
        SEQ = 512
        key = jax.random.key(seed)
        ks = jax.random.split(key, 8)
        scale = 1.0 / np.sqrt(D_MODEL)
        q = jax.random.normal(ks[0], (BATCH, SEQ, D_MODEL), dtype=jnp.float32)
        k = jax.random.normal(ks[1], (BATCH, SEQ, D_MODEL), dtype=jnp.float32)
        v = jax.random.normal(ks[2], (BATCH, SEQ, D_MODEL), dtype=jnp.float32)
        mask = jax.random.bernoulli(ks[3], 0.1, (BATCH, SEQ, SEQ))
        w_q = jax.random.normal(ks[4], (D_MODEL, D_MODEL), dtype=jnp.float32) * scale
        w_k = jax.random.normal(ks[5], (D_MODEL, D_MODEL), dtype=jnp.float32) * scale
        w_v = jax.random.normal(ks[6], (D_MODEL, D_MODEL), dtype=jnp.float32) * scale
        w_o = jax.random.normal(ks[7], (D_MODEL, D_MODEL), dtype=jnp.float32) * scale
        return {'q': q, 'k': k, 'v': v, 'mask': mask, 'w_q': w_q, 'w_k': w_k, 'w_v': w_v, 'w_o': w_o}
    _L3_xattn_all = _L3_xattn_setup()
    _L3_xattn_in = {k: v for k, v in _L3_xattn_all.items() if k in ('w_q', 'w_k', 'w_v', 'w_o')}
    del _L3_xattn_all

    def _L3_ffn_setup():
        import jax, jax.numpy as jnp
        import numpy as np
        B, S, H = (4, 512, 256)
        F = 1024
        E = 8
        JITTER_EPS = 0.01

        def _sparse_mixer_top2(scores, jitter_eps):
            vals, idx = jax.lax.top_k(scores, 2)
            neg_inf = -jnp.inf
            m1 = vals[:, :1]
            factor1 = jnp.maximum(jnp.abs(scores), m1)
            mask1 = (m1 - scores) / factor1 > 2 * jitter_eps
            p1 = jax.nn.softmax(jnp.where(mask1, neg_inf, scores), axis=-1)
            mult1 = jnp.take_along_axis(p1, idx[:, :1], axis=-1)[:, 0]
            m2 = vals[:, 1:2]
            factor2 = jnp.maximum(jnp.abs(scores), m2)
            mask2 = (m2 - scores) / factor2 > 2 * jitter_eps
            top1_onehot = jnp.arange(scores.shape[-1])[None, :] == idx[:, :1]
            s2 = jnp.where(top1_onehot, neg_inf, scores)
            p2 = jax.nn.softmax(jnp.where(mask2, neg_inf, s2), axis=-1)
            mult2 = jnp.take_along_axis(p2, idx[:, 1:2], axis=-1)[:, 0]
            return (mult1, mult2, idx)
        key = jax.random.key(seed)
        k0, k1, k2, k3, k4 = jax.random.split(key, 5)
        hidden_states = jax.random.normal(k0, (B, S, H), dtype=jnp.float32)
        gate_w = jax.random.normal(k1, (E, H), dtype=jnp.float32) * 0.02
        w1 = jax.random.normal(k2, (E, F, H), dtype=jnp.float32) * 0.02
        w2 = jax.random.normal(k3, (E, H, F), dtype=jnp.float32) * 0.02
        w3 = jax.random.normal(k4, (E, F, H), dtype=jnp.float32) * 0.02
        return {'hidden_states': hidden_states, 'gate_w': gate_w, 'w1': w1, 'w2': w2, 'w3': w3}
    _L3_ffn_all = _L3_ffn_setup()
    _L3_ffn_in = {k: v for k, v in _L3_ffn_all.items() if k in ('gate_w', 'w1', 'w2', 'w3')}
    del _L3_ffn_all
    return {'x': x, 'ctx_1024': ctx_1024, 'mask_BxSxS2_bk0': mask_BxSxS2_bk0, 'L0_xattn_Wq': _L0_xattn_in['Wq'], 'L0_xattn_Wk': _L0_xattn_in['Wk'], 'L0_xattn_Wv': _L0_xattn_in['Wv'], 'L0_xattn_Wk_ip': _L0_xattn_in['Wk_ip'], 'L0_xattn_Wv_ip': _L0_xattn_in['Wv_ip'], 'L0_xattn_Wk_ap': _L0_xattn_in['Wk_ap'], 'L0_xattn_Wv_ap': _L0_xattn_in['Wv_ap'], 'L0_xattn_Wo': _L0_xattn_in['Wo'], 'L0_xattn_bo': _L0_xattn_in['bo'], 'L0_xattn_rel_k': _L0_xattn_in['rel_k'], 'L0_xattn_rel_v': _L0_xattn_in['rel_v'], 'L0_xattn_alpha': _L0_xattn_in['alpha'], 'L0_xattn_beta': _L0_xattn_in['beta'], 'L0_ffn_gate_w': _L0_ffn_in['gate_w'], 'L0_ffn_shared_gate_w': _L0_ffn_in['shared_gate_w'], 'L0_ffn_shared_up_w': _L0_ffn_in['shared_up_w'], 'L0_ffn_shared_down_w': _L0_ffn_in['shared_down_w'], 'L0_ffn_routed_gate_w': _L0_ffn_in['routed_gate_w'], 'L0_ffn_routed_up_w': _L0_ffn_in['routed_up_w'], 'L0_ffn_routed_down_w': _L0_ffn_in['routed_down_w'], 'L1_xattn_Wq': _L1_xattn_in['Wq'], 'L1_xattn_Wk': _L1_xattn_in['Wk'], 'L1_xattn_Wv': _L1_xattn_in['Wv'], 'L1_xattn_Wo': _L1_xattn_in['Wo'], 'L1_xattn_bq': _L1_xattn_in['bq'], 'L1_xattn_bk': _L1_xattn_in['bk'], 'L1_xattn_bv': _L1_xattn_in['bv'], 'L1_xattn_bo': _L1_xattn_in['bo'], 'L1_ffn_U1': _L1_ffn_in['U1'], 'L1_ffn_V1': _L1_ffn_in['V1'], 'L1_ffn_b1': _L1_ffn_in['b1'], 'L1_ffn_U2': _L1_ffn_in['U2'], 'L1_ffn_V2': _L1_ffn_in['V2'], 'L1_ffn_b2': _L1_ffn_in['b2'], 'L2_xattn_Wq': _L2_xattn_in['Wq'], 'L2_xattn_bq': _L2_xattn_in['bq'], 'L2_xattn_Wk': _L2_xattn_in['Wk'], 'L2_xattn_bk': _L2_xattn_in['bk'], 'L2_xattn_Wv': _L2_xattn_in['Wv'], 'L2_xattn_bv': _L2_xattn_in['bv'], 'L2_xattn_Wo': _L2_xattn_in['Wo'], 'L2_xattn_bo': _L2_xattn_in['bo'], 'L2_ffn_rhs': _L2_ffn_in['rhs'], 'L3_xattn_w_q': _L3_xattn_in['w_q'], 'L3_xattn_w_k': _L3_xattn_in['w_k'], 'L3_xattn_w_v': _L3_xattn_in['w_v'], 'L3_xattn_w_o': _L3_xattn_in['w_o'], 'L3_ffn_gate_w': _L3_ffn_in['gate_w'], 'L3_ffn_w1': _L3_ffn_in['w1'], 'L3_ffn_w2': _L3_ffn_in['w2'], 'L3_ffn_w3': _L3_ffn_in['w3']}

def reference(x, ctx_1024, mask_BxSxS2_bk0, L0_xattn_Wq, L0_xattn_Wk, L0_xattn_Wv, L0_xattn_Wk_ip, L0_xattn_Wv_ip, L0_xattn_Wk_ap, L0_xattn_Wv_ap, L0_xattn_Wo, L0_xattn_bo, L0_xattn_rel_k, L0_xattn_rel_v, L0_xattn_alpha, L0_xattn_beta, L0_ffn_gate_w, L0_ffn_shared_gate_w, L0_ffn_shared_up_w, L0_ffn_shared_down_w, L0_ffn_routed_gate_w, L0_ffn_routed_up_w, L0_ffn_routed_down_w, L1_xattn_Wq, L1_xattn_Wk, L1_xattn_Wv, L1_xattn_Wo, L1_xattn_bq, L1_xattn_bk, L1_xattn_bv, L1_xattn_bo, L1_ffn_U1, L1_ffn_V1, L1_ffn_b1, L1_ffn_U2, L1_ffn_V2, L1_ffn_b2, L2_xattn_Wq, L2_xattn_bq, L2_xattn_Wk, L2_xattn_bk, L2_xattn_Wv, L2_xattn_bv, L2_xattn_Wo, L2_xattn_bo, L2_ffn_rhs, L3_xattn_w_q, L3_xattn_w_k, L3_xattn_w_v, L3_xattn_w_o, L3_ffn_gate_w, L3_ffn_w1, L3_ffn_w2, L3_ffn_w3):
    import jax
    import jax.numpy as jnp

    def _L0_xattn_ref(x, context, Wq, Wk, Wv, Wk_ip, Wv_ip, Wk_ap, Wv_ap, Wo, bo, rel_k, rel_v, alpha, beta):
        import jax, jax.numpy as jnp
        import numpy as np
        H = 16
        D = 64
        SCALE = D ** (-0.5)
        TEXT = 77
        IMG = 16
        AUD = 32
        MAXREL = 16
        B, NQ, QD = (32, 256, 256)
        INNER = H * D

        def _heads(t):
            return t.reshape(t.shape[0], t.shape[1], H, D)
        b, nq, _ = x.shape
        q = _heads(x @ Wq)
        ctx_t = context[:, :TEXT]
        ctx_i = context[:, TEXT:TEXT + IMG]
        ctx_a = context[:, TEXT + IMG:]
        k = _heads(ctx_t @ Wk)
        v = _heads(ctx_t @ Wv)
        sim = jnp.einsum('bihd,bjhd->bhij', q, k) * SCALE
        dist = jnp.clip(jnp.arange(TEXT)[None, :] - jnp.arange(nq)[:, None], -MAXREL, MAXREL) + MAXREL
        k2 = rel_k[dist]
        sim = sim + jnp.einsum('bihd,ijd->bhij', q, k2) * SCALE
        attn = jax.nn.softmax(sim, axis=-1)
        out = jnp.einsum('bhij,bjhd->bihd', attn, v)
        out = out + jnp.einsum('bhij,ijd->bihd', attn, rel_v[dist])

        def stream(W_k, W_v, ctx):
            kh = _heads(ctx @ W_k)
            vh = _heads(ctx @ W_v)
            a = jax.nn.softmax(jnp.einsum('bihd,bjhd->bhij', q, kh) * SCALE, axis=-1)
            return jnp.einsum('bhij,bjhd->bihd', a, vh)
        out = out + stream(Wk_ip, Wv_ip, ctx_i) * (jnp.tanh(alpha) + 1.0)
        out = out + stream(Wk_ap, Wv_ap, ctx_a) * (jnp.tanh(beta) + 1.0)
        out = out.reshape(b, nq, INNER)
        return out @ Wo + bo

    def _L0_ffn_ref(hidden_states, gate_w, shared_gate_w, shared_up_w, shared_down_w, routed_gate_w, routed_up_w, routed_down_w):
        import jax, jax.numpy as jnp
        import numpy as np
        H = 256
        I = 512
        E = 32
        B, S = (4, 512)

        def _grouped_mm(a, w, group_sizes):
            return jax.lax.ragged_dot(a, w, group_sizes)

        def _swiglu(x, gw, uw, dw):
            return jax.nn.silu(x @ gw) * (x @ uw) @ dw
        b, s, h = hidden_states.shape
        x = hidden_states.reshape(-1, h)
        shared_out = _swiglu(x, shared_gate_w, shared_up_w, shared_down_w)
        logits = x @ gate_w
        topk_ids = jnp.argmax(logits, axis=-1)
        topk_val = jnp.max(logits, axis=-1)
        scores = jax.nn.sigmoid(topk_val)[:, None]
        xs = x * scores
        tokens_per_expert = jnp.zeros((E,), jnp.int32).at[topk_ids].add(1)
        order = jnp.argsort(topk_ids)
        sorted_x = xs[order]
        g = _grouped_mm(sorted_x, routed_gate_w, tokens_per_expert)
        u = _grouped_mm(sorted_x, routed_up_w, tokens_per_expert)
        d = _grouped_mm(jax.nn.silu(g) * u, routed_down_w, tokens_per_expert)
        inv = jnp.argsort(order)
        routed_out = d[inv]
        return (shared_out + routed_out).reshape(b, s, h)

    def _L1_xattn_ref(q, k, v, Wq, Wk, Wv, Wo, bq, bk, bv, bo):
        import jax, jax.numpy as jnp
        import numpy as np
        B, T, D, H = (4, 512, 256, 16)
        DK = D // H

        def _split_heads(x):
            b, t, _ = x.shape
            return x.reshape(b, t, H, DK).transpose(0, 2, 1, 3)
        qh = _split_heads(q @ Wq.T + bq)
        kh = _split_heads(k @ Wk.T + bk)
        vh = _split_heads(v @ Wv.T + bv)
        scores = jnp.einsum('bhqd,bhkd->bhqk', qh, kh) / jnp.sqrt(jnp.float32(DK))
        tq, tk = (scores.shape[-2], scores.shape[-1])
        causal = jnp.tril(jnp.ones((tq, tk), dtype=bool))
        scores = jnp.where(causal, scores, jnp.float32(-jnp.inf))
        attn = jax.nn.softmax(scores, axis=-1)
        ctx = jnp.einsum('bhqk,bhkd->bhqd', attn, vh)
        merged = ctx.transpose(0, 2, 1, 3).reshape(q.shape[0], tq, D)
        return merged @ Wo.T + bo

    def _L1_ffn_ref(x, U1, V1, b1, U2, V2, b2):
        import jax, jax.numpy as jnp
        import numpy as np
        D_MODEL, D_FF, RANK = (256, 1024, 64)
        B, S = (4, 1024)
        P = jnp.einsum('bsd,dr->bsr', x, U1)
        H = jax.nn.gelu(jnp.einsum('bsr,rf->bsf', P, V1) + b1)
        Q = jnp.einsum('bsf,fr->bsr', H, U2)
        return jnp.einsum('bsr,rd->bsd', Q, V2) + b2

    def _L2_xattn_ref(query, key, value, Wq, bq, Wk, bk, Wv, bv, Wo, bo):
        import jax, jax.numpy as jnp
        import numpy as np
        HIDDEN = 256
        HEADS = 16
        HEAD_DIM = HIDDEN // HEADS
        B, Sq, _ = query.shape
        Sk = key.shape[1]
        Q = (query @ Wq.T + bq).reshape(B, Sq, HEADS, HEAD_DIM).transpose(0, 2, 1, 3)
        K = (key @ Wk.T + bk).reshape(B, Sk, HEADS, HEAD_DIM).transpose(0, 2, 1, 3)
        V = (value @ Wv.T + bv).reshape(B, Sk, HEADS, HEAD_DIM).transpose(0, 2, 1, 3)
        scale = jnp.sqrt(jnp.float32(HEAD_DIM))
        scores = jnp.einsum('bhqd,bhkd->bhqk', Q, K) / scale
        causal = jnp.tril(jnp.ones((Sq, Sk), dtype=bool))
        scores = jnp.where(causal[None, None], scores, -jnp.inf)
        attn = jax.nn.softmax(scores, axis=-1)
        out = jnp.einsum('bhqk,bhkd->bhqd', attn, V)
        out = out.transpose(0, 2, 1, 3).reshape(B, Sq, HIDDEN)
        return out @ Wo.T + bo

    def _L2_ffn_ref(lhs, rhs):
        import jax, jax.numpy as jnp
        import numpy as np
        INT8_MAX = 127.0

        def _absmax_scale(x, axes):
            amax = jnp.max(jnp.abs(x), axis=axes, keepdims=True)
            return jnp.maximum(amax, 1e-12) / INT8_MAX
        lhs_scale = _absmax_scale(lhs, (2,))
        rhs_scale = _absmax_scale(rhs, (0,))
        q_lhs = jnp.clip(jnp.round(lhs / lhs_scale), -INT8_MAX, INT8_MAX).astype(jnp.int8)
        q_rhs = jnp.clip(jnp.round(rhs / rhs_scale), -INT8_MAX, INT8_MAX).astype(jnp.int8)
        acc = jax.lax.dot_general(q_lhs, q_rhs, (((2,), (0,)), ((), ())), preferred_element_type=jnp.int32)
        return acc.astype(jnp.float32) * lhs_scale * rhs_scale

    def _L3_xattn_ref(q, k, v, mask, w_q, w_k, w_v, w_o):
        import jax, jax.numpy as jnp
        import numpy as np
        D_MODEL = 256
        N_HEADS = 16
        HEAD_DIM = D_MODEL // N_HEADS
        BATCH = 2
        SEQ = 512
        B, S, _ = q.shape

        def split_heads(x, w):
            y = x @ w.T
            return y.reshape(B, -1, N_HEADS, HEAD_DIM).transpose(0, 2, 1, 3)
        query = split_heads(q, w_q)
        key_ = split_heads(k, w_k)
        value = split_heads(v, w_v)
        scores = jnp.einsum('bhqd,bhkd->bhqk', query, key_) / np.sqrt(HEAD_DIM)
        scores = jnp.where(mask[:, None, :, :], jnp.float32(-1000000000.0), scores)
        attention = jax.nn.softmax(scores, axis=-1)
        out = jnp.einsum('bhqk,bhkd->bhqd', attention, value)
        out = out.transpose(0, 2, 1, 3).reshape(B, -1, N_HEADS * HEAD_DIM)
        return out @ w_o.T

    def _L3_ffn_ref(hidden_states, gate_w, w1, w2, w3):
        import jax, jax.numpy as jnp
        import numpy as np
        B, S, H = (4, 512, 256)
        F = 1024
        E = 8
        JITTER_EPS = 0.01

        def _sparse_mixer_top2(scores, jitter_eps):
            vals, idx = jax.lax.top_k(scores, 2)
            neg_inf = -jnp.inf
            m1 = vals[:, :1]
            factor1 = jnp.maximum(jnp.abs(scores), m1)
            mask1 = (m1 - scores) / factor1 > 2 * jitter_eps
            p1 = jax.nn.softmax(jnp.where(mask1, neg_inf, scores), axis=-1)
            mult1 = jnp.take_along_axis(p1, idx[:, :1], axis=-1)[:, 0]
            m2 = vals[:, 1:2]
            factor2 = jnp.maximum(jnp.abs(scores), m2)
            mask2 = (m2 - scores) / factor2 > 2 * jitter_eps
            top1_onehot = jnp.arange(scores.shape[-1])[None, :] == idx[:, :1]
            s2 = jnp.where(top1_onehot, neg_inf, scores)
            p2 = jax.nn.softmax(jnp.where(mask2, neg_inf, s2), axis=-1)
            mult2 = jnp.take_along_axis(p2, idx[:, 1:2], axis=-1)[:, 0]
            return (mult1, mult2, idx)
        Bv, Sv, Hv = hidden_states.shape
        x = hidden_states.reshape(-1, Hv)
        scores = x @ gate_w.T
        mult1, mult2, idx = _sparse_mixer_top2(scores, JITTER_EPS)
        out = jnp.zeros_like(x)
        for e in range(E):
            w_tok = mult1 * (idx[:, 0] == e) + mult2 * (idx[:, 1] == e)
            h = jax.nn.silu(x @ w1[e].T) * (x @ w3[e].T)
            out = out + w_tok[:, None] * (h @ w2[e].T)
        return out.reshape(Bv, Sv, Hv)
    x = x + _L0_xattn_ref(_layernorm(x, axis=-1), ctx_1024, L0_xattn_Wq, L0_xattn_Wk, L0_xattn_Wv, L0_xattn_Wk_ip, L0_xattn_Wv_ip, L0_xattn_Wk_ap, L0_xattn_Wv_ap, L0_xattn_Wo, L0_xattn_bo, L0_xattn_rel_k, L0_xattn_rel_v, L0_xattn_alpha, L0_xattn_beta)
    x = x + _L0_ffn_ref(_layernorm(x, axis=-1), L0_ffn_gate_w, L0_ffn_shared_gate_w, L0_ffn_shared_up_w, L0_ffn_shared_down_w, L0_ffn_routed_gate_w, L0_ffn_routed_up_w, L0_ffn_routed_down_w)
    x = x + _L1_xattn_ref(_layernorm(x, axis=-1), ctx_1024, ctx_1024, L1_xattn_Wq, L1_xattn_Wk, L1_xattn_Wv, L1_xattn_Wo, L1_xattn_bq, L1_xattn_bk, L1_xattn_bv, L1_xattn_bo)
    x = x + _L1_ffn_ref(_layernorm(x, axis=-1), L1_ffn_U1, L1_ffn_V1, L1_ffn_b1, L1_ffn_U2, L1_ffn_V2, L1_ffn_b2)
    x = x + _L2_xattn_ref(_layernorm(x, axis=-1), ctx_1024, ctx_1024, L2_xattn_Wq, L2_xattn_bq, L2_xattn_Wk, L2_xattn_bk, L2_xattn_Wv, L2_xattn_bv, L2_xattn_Wo, L2_xattn_bo)
    x = x + _L2_ffn_ref(_layernorm(x, axis=-1), L2_ffn_rhs)
    x = x + _L3_xattn_ref(_layernorm(x, axis=-1), ctx_1024, ctx_1024, mask_BxSxS2_bk0, L3_xattn_w_q, L3_xattn_w_k, L3_xattn_w_v, L3_xattn_w_o)
    x = x + _L3_ffn_ref(_layernorm(x, axis=-1), L3_ffn_gate_w, L3_ffn_w1, L3_ffn_w2, L3_ffn_w3)
    return x

_drawn_inputs = setup_inputs


def setup_inputs(seed=0):
    import zlib

    import numpy as np

    out = dict(_drawn_inputs(seed))
    spreads = {'L0_xattn_bo': (0.0, 0.1),
     'L1_xattn_bq': (0.0, 0.714),
     'L1_xattn_bk': (0.0, 0.8),
     'L1_xattn_bv': (0.0, 0.1),
     'L1_xattn_bo': (0.0, 0.1),
     'L1_ffn_b1': (0.0, 0.8),
     'L1_ffn_b2': (0.0, 0.1)}
    factors = {'L0_xattn_Wq': 7.69,
     'L0_xattn_Wk': 7.704,
     'L0_xattn_rel_k': 8.0,
     'L0_xattn_rel_v': 3.652,
     'L0_ffn_gate_w': 4.852,
     'L0_ffn_routed_gate_w': 4.823,
     'L0_ffn_routed_up_w': 4.812,
     'L0_ffn_routed_down_w': 4.805,
     'L1_ffn_U1': 8.0,
     'L1_ffn_V1': 8.0,
     'L1_ffn_U2': 6.665,
     'L1_ffn_V2': 6.813,
     'L2_xattn_bq': 8.0,
     'L2_xattn_bk': 8.0,
     'L2_xattn_bv': 2.911,
     'L3_xattn_w_q': 4.192,
     'L3_xattn_w_k': 4.218,
     'L3_ffn_gate_w': 8.0,
     'L3_ffn_w1': 8.0,
     'L3_ffn_w2': 8.0,
     'L3_ffn_w3': 8.0}
    for name, (base, spread) in spreads.items():
        noise = np.random.default_rng([zlib.crc32(name.encode()), seed]).standard_normal(out[name].shape)
        drawn = base * np.exp(spread * noise) if base else spread * noise
        out[name] = jnp.asarray(drawn.astype(out[name].dtype))
    for name, factor in factors.items():
        out[name] = (out[name] * factor).astype(out[name].dtype)
    return out
```

```python
import numpy as np
import concourse.bass as bass
from concourse import mybir
from contextlib import ExitStack

P = 128
B, T, D = 2, 1024, 256
J = 77
H = 16
KC = D // P
D0 = 64
INNER = H * D0
C0 = INNER // P
MAXREL = 16
TILES = T // P
STREAMS = 4
ROUNDS = TILES // STREAMS
HJ = H * J
HALF = HJ // 2
QUART = HALF // 2
NCH = -(-HJ // P)
LAST_CH = HJ - P * (NCH - 1)
EXT = P + J - 1
BAND = 2 * MAXREL - 1
PADW = (MAXREL - 1) + J + (P + MAXREL - 1 - J)
NREL = BAND + 1
F0 = 512
FC0 = F0 // P
E0 = 32
EPS = 1e-5
F32 = mybir.dt.float32
BF16 = mybir.dt.bfloat16
I32 = mybir.dt.int32
U32 = mybir.dt.uint32
U8 = mybir.dt.uint8
ALU = mybir.AluOpType
ACT = mybir.ActivationFunctionType
X = mybir.AxisListType.X
STEPS1 = ("stats1", "apply1", "rel", "half0", "half1", "norm", "pT0", "pT1", "band", "out1",
          "stats2", "apply2", "gate_up", "out2")
LAYERS = (1, 2, 3)
STEPS2 = tuple(f"{step}{l}" for l in LAYERS for step in
               ("stats", "apply", "q", "half0_", "half1_", "pT0_", "pT1_", "av", "oT", "out", "fstats", "fapply")
               + (("low", "gelu", "low2", "fout"), ("quant", "fout"), ("gate",))[l - 1])

PE, AC, DV, PO = "pe", "act", "dve", "pool"
STAGES = dict(
    stats=((DV, 0.6), (PO, 0.4)), apply=((DV, 0.4), (PE, 0.2), (AC, 0.4)), half0=((PE, 1.1), (DV, 1.5), (AC, 0, 0.7)),
    fapply3=((DV, 0.4), (PO, 0, 0.1), (PE, 0.2), (AC, 0.4)), q=((PE, 0.9), (PO, 0, 0.2), (AC, 0.5)),
    q3=((PE, 0.9), (PO, 0, 1.5), (AC, 0.5)), half1=((PE, 1.1), (DV, 1.5), (AC, 0.7)), pT=((PE, 0.4), (AC, 0.9)),
    av=((PE, 1.0), (DV, 0.5)), oT=((PE, 0.2), (AC, 0.4)), out=((PE, 1.0), (DV, 0.4)), low=((PE, 0.4), (AC, 0.3)),
    gelu=((PE, 1.7), (AC, 1.5)), down=((PE, 1.7), (AC, 0.3)), fout=((PE, 0.4), (DV, 0.4)),
    quant=((DV, 1.8), (PE, 0.1), (AC, 0.4)), gate=((PE, 0.2), (DV, 0.2)),
    wide_half0=((PE, 2.1), (DV, 1.5), (AC, 0, 0.7)), wide_half1=((PE, 2.1), (DV, 1.5), (AC, 0.7)), norm=((DV, 2.8),),
    out1=((PE, 4.4), (DV, 0.4)), gate_up=((PE, 3.5), (AC, 0.7), (DV, 0.7)), out2=((PE, 2.0), (DV, 0.5)),
    rel=((PE, 0, 6.0), (AC, 6.0)), band=((PE, 1.0), (AC, 0.6)), apply2=((DV, 0.4), (PO, 0, 0.1), (PE, 0.2), (AC, 0.4)))
KIND1 = dict(stats1="stats", apply1="apply", half0="wide_half0", half1="wide_half1", pT0="pT", pT1="pT", stats2="stats")
KIND2 = dict(fstats="stats", fapply="apply", half0_="half0", half1_="half1", pT0_="pT", pT1_="pT", low2="down")
HOP = 0.15


def plan(steps):
    chains = []
    for s in range(STREAMS):
        chain = []
        for r in range(ROUNDS):
            for step in steps:
                if step in ("rel", "band") and (s or r):
                    continue
                kind = KIND1.get(step, step) if steps is STEPS1 else (
                    step if step in STAGES else KIND2.get(step[:-1], step[:-1]))
                chain += [(stage[0], step, s, r, stage[1], stage[-1]) for stage in STAGES[kind]]
        chains.append(chain)
    free, ready, at = dict.fromkeys((PE, AC, DV, PO), 0.0), [OFFSET * s for s in range(STREAMS)], [0] * STREAMS
    found = []
    while any(a < len(c) for a, c in zip(at, chains)):
        options = []
        for s in range(STREAMS):
            if at[s] < len(chains[s]):
                engine = chains[s][at[s]][0]
                options.append((max(free[engine], ready[s]), PRIO * at[s], ready[s], s))
        start, _, _, s = min(options)
        engine, step, _, r, time, held = chains[s][at[s]]
        free[engine] = start + held
        ready[s] = start + time + (HOP if time else 0)
        at[s] += 1
        found.append((engine, step, s, r))
    return found


OFFSET, PRIO = 0.0, 0
POOL_LINKS1, POOL_LINKS2 = 16, 48
DVE_LINKS1, DVE_LINKS2 = 52, 188

ATT = 16
SLOTS = 3
VW = ATT + 1
FIRST = [min(P * k // J, H - SLOTS) for k in range(NCH)]
REPS = -(-P * NCH // J)
LOW, F1 = 64, 1024
F3 = 1024
E3 = 8
JITTER = 0.01
NEVER, MASKED = -3.0e38, -1.0e9
MAGIC = 1.5 * 2.0 ** 23
QMAX = 127.0
BLK0, BLK3 = P, 2 * P
NB0 = B * T // BLK0 + E0
NB3 = 2 * B * T // BLK3 + E3
MS3 = 2
PASSES = (B, NB0 // STREAMS, B, NB3 // MS3)
ROWS = NB0 * BLK0
assert NB3 * BLK3 == ROWS
NT = B * TILES
PLAN = {steps: plan(steps) for steps in (STEPS1, STEPS2)}


def window(c):
    return 2 * J * c // P * P


class Count:

    def __init__(self, sem, per_pass, start=0):
        self.sem, self.per_pass = sem, per_pass
        self.base = [start + sum(m * n for m, n in zip(PASSES[:i], per_pass)) for i in range(len(per_pass))]

    def at(self, phase, i, k):
        return i * self.per_pass[phase] + (self.base[phase] + k)


class Links:

    def __init__(self, eng, sem):
        self.eng, self.sem, self.done, self.n, self.i, self.per_pass = eng, sem, 0, 0, 0, 0

    def enter(self, i, per_pass):
        self.done, self.n, self.i, self.per_pass = self.done + self.n, 0, i, per_pass

    def leave(self, passes):
        assert self.n == self.per_pass, ("links in a pass:", self.n)
        self.done, self.n, self.i, self.per_pass = self.done + passes * self.n, 0, 0, 0

    def __call__(self, ins):
        self.n += 1
        ins.then_inc(self.sem, 1)
        self.eng.wait_ge(self.sem, self.i * self.per_pass + (self.done + self.n))


def build(nc, t, out):
    ctx = ExitStack()
    with ctx:
        offset = [nc.sbuf_base + 31 & ~31]

        def sb(name, shape, dt=F32, at=None):
            size = int(np.prod(shape[1:])) * mybir.dt.size(dt)
            size = size + 31 & ~31
            if at is None:
                at = offset[0]
                offset[0] += size
                assert offset[0] <= nc.sbuf_usable_end, (name, offset[0])
            return nc.alloc_sbuf_tensor_at(name, shape, dt, offset=at), at + size

        def keep(name, shape, dt=F32):
            return sb(name, shape, dt)[0]

        def sem(name):
            return ctx.enter_context(nc.semaphore(name))

        x_all = keep("x_all", [P, B * TILES, D])
        ident = keep("ident", [P, P])
        ones = keep("ones", [1, P])
        minus_half = keep("minus_half", [P, 1])
        ctx_all = keep("ctx_all", [P, KC, B, J])
        ctx_b = keep("ctx_b", [P, KC, J])
        logits0 = keep("logits0", [P, B * TILES, E0])
        stats = [keep(f"stats{s}", [P, 6]) for s in range(STREAMS)]
        mean_var = [keep(f"mean_var{s}", [P, 2]) for s in range(STREAMS)]
        rstd = [keep(f"rstd{s}", [P, 2]) for s in range(STREAMS)]
        xn = [keep(f"xn{s}", [P, D]) for s in range(STREAMS)]
        xnT = [keep(f"xnT{s}", [P, KC, P]) for s in range(STREAMS)]
        probs = [keep(f"probs{s}", [P, HJ]) for s in range(STREAMS)]
        probsT = [keep(f"probsT{s}", [P, NCH, P]) for s in range(STREAMS)]
        mx = [keep(f"mx{s}", [P, H]) for s in range(STREAMS)]
        qT = [keep(f"qT{s}", [P, KC, P]) for s in range(STREAMS)]
        low_T = [keep(f"low_T{s}", [P, P]) for s in range(STREAMS)]
        filled_mask = [keep(f"filled_mask{s}", [P, J], U8) for s in range(STREAMS)]
        scale = [keep(f"scale{s}", [P, 2]) for s in range(STREAMS)]
        identb, squareb, onesb = (keep(n, [P, P], BF16) for n in ("identb", "squareb", "onesb"))
        onesq = keep("onesq", [P, P])
        causal_f, causal = keep("causal_f", [P, J]), keep("causal", [P, J], U8)
        logits3 = keep("logits3", [P, NT, E3])
        rev, kstep = keep("rev", [P, E0]), keep("kstep", [P, 2, 16])
        blks, row = keep("blks", [P, NB0]), keep("row", [P, 1])
        low_tri = keep("low_tri", [P, E0, E0])
        one_hot = keep("one_hot", [P, NT * E0], BF16)
        route = keep("route", [P, 8, NT])
        blocks_of = keep("blocks_of", [P, 4, E0])
        slot = keep("slot", [P, 2, NT], I32)
        zeros = keep("zeros", [P, D])
        expert = keep("expert", [P, NB0])
        load_f, load = keep("load_f", [P, NB0]), keep("load", [P, NB0], U32)
        load_now = keep("load_now", [P, 2, STREAMS], U32)
        phase_start = offset[0]

        wq0 = keep("wq0", [P, KC, INNER])
        wqT0 = keep("wqT0", [P, C0, D])
        wk0 = keep("wk0", [P, KC, INNER])
        wv0 = keep("wv0", [P, KC, INNER])
        wo0 = keep("wo0", [P, C0, D])
        bo0 = keep("bo0", [1, D])
        kT0 = keep("kT0", [P, C0, J])
        qk0 = keep("qk0", [P, KC, HJ])
        vT0 = keep("vT0", [P, C0 * 3 * P + 104])
        vo0 = keep("vo0", [P, NCH, D])
        diag_f = keep("diag_f", [P, P])
        relk_ext = keep("relk_ext", [P, EXT])
        relk_0 = keep("relk_0", [P, 1])
        relv_0 = keep("relv_0", [P, 1])
        relv_T = keep("relv_T", [P, NREL])
        relv_m = keep("relv_m", [P, 2, P])
        relvo = keep("relvo", [P, H // 4, D])
        tail_mask = keep("tail_mask", [P, J])
        rel_q = keep("rel_q", [P, H, EXT])
        band_src = rel_q[:].rearrange("p h e -> p (h e)")[:, 0:H * PADW].rearrange("p (h e) -> p h e", h=H)
        rel_s = keep("rel_s", [P, HJ])
        band = keep("band", [P, H, NREL])
        bandT = keep("bandT", [P, 4, P])
        qT0 = probsT[0][:, 0:C0, :]
        sgw = keep("sgw", [P, KC, F0])
        suw = keep("suw", [P, KC, F0])
        sdw = keep("sdw", [P, FC0, D])
        gate0 = keep("gate0", [P, KC, E0])
        hid = [probs[s][:, 0:2 * F0].rearrange("p (a f) -> p a f", a=2) for s in range(STREAMS)]

        offset[0] = phase_start
        k_bd = {l: keep(f"k_bd{l}", [P, KC, 4 * J]) for l in LAYERS}
        v_bd = {l: keep(f"v_bd{l}", [P, NCH, SLOTS * VW]) for l in LAYERS}
        ctx_rep = keep("ctx_rep", [P, KC, REPS * J])
        computed_end = offset[0]
        w2 = {(n, l): keep(f"{n}_{l}", [P, KC, D]) for l in LAYERS for n in ("wq", "wk", "wv", "wo")}
        bq2 = {l: keep(f"bq_{l}", [P, KC]) for l in (1, 2)}
        bk2 = {l: keep(f"bk_{l}", [P, KC]) for l in (1, 2)}
        bv2 = {l: keep(f"bv_{l}", [1, D]) for l in (1, 2)}
        bo2 = {l: keep(f"bo_{l}", [1, D]) for l in (1, 2)}
        head_mask, slot_mask = keep("head_mask", [P, 4]), keep("slot_mask", [P, NCH, SLOTS])
        u1, v1 = keep("u1", [P, KC, LOW]), keep("v1", [LOW + 1, F1])
        u2, v2 = keep("u2", [P, F1 // P, LOW]), keep("v2", [LOW + 1, D])
        rhs_T, rhs_q = keep("rhs_T", [P, KC, D]), keep("rhs_q", [P, KC, D], BF16)
        rhs_qT = keep("rhs_qT", [P, KC, D], BF16)
        rhs_scale, rhs_scale_row = keep("rhs_scale", [P, 2 * KC]), keep("rhs_scale_row", [P, D])
        diag = keep("diag", [P, KC, P])
        x_q = [keep(f"x_q{s}", [P, D], BF16) for s in range(STREAMS)]
        x_qT = [keep(f"x_qT{s}", [P, D], BF16) for s in range(STREAMS)]
        mask_in, unmasked = keep("mask_in", [P, NT * J // 4], I32), keep("unmasked", [P, NT, J], U8)
        gate3 = keep("gate3", [P, KC, E3])
        moe_start = offset[0]
        w_in0 = [keep(f"w_in0{s}", [P, 2, KC, F0]) for s in range(STREAMS)]
        w_out0 = [keep(f"w_out0{s}", [P, FC0, D]) for s in range(STREAMS)]
        y_sb = [qT[s][:].rearrange("p c n -> p (c n)") for s in range(STREAMS)]
        rows0, rows0_end = sb("rows0", [P, NT, D], at=phase_start)
        assert rows0_end <= computed_end
        offset[0] = moe_start
        w_in3 = [keep(f"w_in3{s}", [P, 2, KC, F3]) for s in range(MS3)]
        w_out3 = [keep(f"w_out3{s}", [P, F3 // P, D]) for s in range(MS3)]
        offset[0] = phase_start
        rows3 = [keep(f"rows3{n}", [P, NT, D]) for n in range(2)]
        x_in = [keep(f"x_in{s}", [P, 2, D]) for s in range(MS3)]
        x_inT = [keep(f"x_inT{s}", [P, KC, BLK3]) for s in range(MS3)]
        act3 = [keep(f"act3{s}", [P, 2 * BLK3]) for s in range(MS3)]
        hid3 = [keep(f"hid3{s}", [P, F3 // P, BLK3]) for s in range(MS3)]
        y3 = [keep(f"y3{s}", [P, 2, D]) for s in range(MS3)]
        assert offset[0] <= moe_start, (offset[0], moe_start)

        sorted_dram = nc.dram_tensor("sorted_dram", [ROWS, D], F32)
        y_dram = nc.dram_tensor("y_dram", [ROWS, D], F32)
        xn3_dram = nc.dram_tensor("xn3_dram", [B * T, D], F32)
        rel_dram = nc.dram_tensor("rel_dram", [P * H * EXT + P], F32)
        band_dram = nc.dram_tensor("band_dram", [P * H * PADW + P], F32)
        xn0_dram = nc.dram_tensor("xn0_dram", [B * T, D], F32)

        ps = [ctx.enter_context(nc.psum_tensor(f"ps{s}", [P, 2, 512], F32)) for s in range(STREAMS)]

        class Stream:
            def __init__(self, s):
                def count(name, *per_pass, start=0):
                    return Count(sem(f"{name}{s}"), per_pass, start)

                first = s == 0
                self.aggr, self.rstd = count("aggr", 4, 0, 12, 0), count("rstd", 4, 0, 12, 0)
                self.xn, self.xn_stored = count("xn", 4, 0, 12, 0), sem(f"xn_stored{s}")
                self.xnT_ps, self.xnT = count("xnT_ps", 4, 1, 10, 1), count("xnT", 4, 1, 10, 1)
                self.q_ps = count("q_ps", 6 * first, 0, 6, 0)
                self.q = count("q", 6 * first, 0, 6, 0)
                self.s_ps, self.filled = count("s_ps", 4, 0, 12, 0), count("filled", 0, 0, 2 + 2 * first, 0)
                self.p_sub, self.p_exp = count("p_sub", 4, 0, 12, 0), count("p_exp", 4, 0, 12, 0)
                self.pT_ps, self.pT = count("pT_ps", 4, 0, 12, 0), count("pT", 4, 0, 12, 0)
                self.o_ps, self.o = count("o_ps", 0, 0, 6, 0), count("o", 2, 0, 6, 0)
                self.oT_ps, self.oT = count("oT_ps", 0, 0, 6, 0), count("oT", 0, 0, 6, 0)
                self.f_ps, self.f, self.fm = count("f_ps", 2, 1, 8, 4), count("f", 2, 1, 8, 4), count("fm", 2, 1, 2, 4)
                self.y_ps, self.x_new = count("y_ps", 4, 1, 12, 1), count("x_new", 4, 1, 12, 1, start=1)
                self.in_loaded, self.out_loaded, self.rows_loaded, self.y_out = (
                    sem(f"{name}{s}") for name in ("in_loaded", "out_loaded", "rows_loaded", "y_out"))

        streams = [Stream(s) for s in range(STREAMS)]
        loaded = {n: sem(f"loaded_{n}") for n in ("x0", "x1", "ctx", "k", "v", "qT", "o", "q", "rel", "rest",
                                                 "shape", "p2", "xn", "mask")}
        zeroed, const2, rhs_ps, rhs_sb = sem("zeroed"), sem("const2"), sem("rhs_ps"), sem("rhs_sb")
        top_ready, score_exp = sem("top_ready"), sem("score_exp")
        one_hot_ready, rank_ready, routed, scaled = sem("one_hot_ready"), sem("rank_ready"), sem("routed"), sem("scaled")
        zero_out, combined, rhs_ready = sem("zero_out"), sem("combined"), sem("rhs_ready")
        scattered, gathered, rep_ready = sem("scattered"), sem("gathered"), sem("rep_ready")
        gathered3 = [sem(f"gathered3_{n}") for n in range(2)]
        consts = sem("consts")
        ctx_ready = sem("ctx_ready")
        prep_ps = Count(sem("prep_ps"), (9, 0, 3, 0), start=1)
        prep_sb = Count(sem("prep_sb"), (9, 0, 3, 0))
        v_ps, vT_ready = sem("v_ps"), sem("vT_ready")
        rel_const = sem("rel_const")
        rel_out, rel_in = sem("rel_out"), sem("rel_in")
        band_ready, band_out, band_in = sem("band_ready"), sem("band_out"), sem("band_in")
        band_tail = sem("band_tail")
        dve_link, pool_link = sem("dve_link"), sem("pool_link")
        stored = sem("stored")
        block = ctx.enter_context(nc.Block())

        def order(steps, own):
            for engine, step, s, r in PLAN[steps]:
                if engine == own["engine"] and step in own:
                    yield own[step], s, r

        def tile(b, s, r):
            return b * TILES + (r * STREAMS + s)

        def x_tile(b, s, r):
            return x_all[:, bass.ds(tile(b, s, r), 1), :].rearrange("p a d -> p (a d)")

        def rep(ap, n):
            return ap.unsqueeze(len(ap.shape)).to_broadcast([*ap.shape, n])

        def heads4(ap):
            return ap.rearrange("p r (q j) -> p r q j", j=J)

        def psum_scores(s):
            return heads4(ps[s][:, :, 0:QUART])

        def sbuf_scores(s, half):
            return heads4(probs[s][:, half * HALF:(half + 1) * HALF].rearrange("p (r n) -> p r n", r=2))

        @block.sync
        def _(sp):
            sp.dma_start(ctx_all[:], t["ctxT"].rearrange("(c p) b j -> p c b j", p=P)).then_inc(loaded["ctx"], 16)
            sp.dma_start(wk0[:], t["Wk0"].rearrange("(c p) n -> p c n", p=P)).then_inc(loaded["k"], 16)
            sp.dma_start(relk_0[:], t["relk_0"]).then_inc(loaded["k"], 16)
            sp.dma_start(wv0[:], t["Wv0"].rearrange("(c p) n -> p c n", p=P)).then_inc(loaded["v"], 16)
            sp.dma_start(relv_0[:], t["relv_0"]).then_inc(loaded["v"], 16)
            sp.dma_start(wqT0[:], t["WqT0"].rearrange("(c p) n -> p c n", p=P)).then_inc(loaded["qT"], 16)
            sp.dma_start(wo0[:], t["Wo0"].rearrange("(c p) n -> p c n", p=P)).then_inc(loaded["o"], 16)
            sp.dma_start(relk_ext[:], t["relk_ext"]).then_inc(loaded["rel"], 16)
            sp.dma_start(relv_T[:], t["relv_T"]).then_inc(loaded["rel"], 16)
            sp.dma_start(x_all[:, 0:TILES, :], t["x"][0].rearrange("(n p) d -> p n d", p=P)).then_inc(loaded["x0"], 16)
            sp.dma_start(wq0[:], t["Wq0"].rearrange("(c p) n -> p c n", p=P)).then_inc(loaded["q"], 16)
            sp.dma_start(bo0[:], t["bo0"]).then_inc(loaded["rest"], 16)
            for dst, src in ((sgw, "sgw"), (suw, "suw"), (sdw, "sdw"), (gate0, "gate0")):
                sp.dma_start(dst[:], t[src].rearrange("(c p) n -> p c n", p=P)).then_inc(loaded["rest"], 16)
            sp.dma_start(x_all[:, TILES:, :], t["x"][1].rearrange("(n p) d -> p n d", p=P)).then_inc(loaded["x1"], 16)
            for dst, src in ((rev, "rev"), (kstep, "kstep"), (blks, "blks"), (row, "row"), (low_tri, "low_tri")):
                sp.dma_start(dst[:], t[src]).then_inc(loaded["shape"], 16)
            sp.wait_ge(zeroed, 1)
            for n in range(ROWS // (8 * P)):
                sp.dma_start(sorted_dram[n * 8 * P:(n + 1) * 8 * P, :].rearrange("(p a) d -> p a d", a=8),
                             zeros[:].unsqueeze(1).to_broadcast([P, 8, D])).then_inc(zero_out, 16)
            with sp.Fori(0, B) as b:
                s0 = streams[0]
                sp.wait_ge(s0.q.sem, s0.q.at(0, b, 5))
                sp.dma_start(rel_dram[0:P * H * EXT].rearrange("(p n) -> p n", p=P),
                             rel_q[:].rearrange("p h e -> p (h e)")).then_inc(rel_out, 16)
                sp.wait_ge(rel_out, 16 * b + 16)
                sp.dma_start(rel_s[:].rearrange("p (h j) -> p h j", h=H),
                             bass.AP(rel_dram, P - 1, [[H * EXT - 1, P], [EXT, H], [1, J]])).then_inc(rel_in, 16)
                sp.wait_ge(band_ready, b + 1)
                sp.dma_start(band_dram[0:P * H * PADW].rearrange("(p n) -> p n", p=P),
                             band_src.rearrange("p h e -> p (h e)")).then_inc(band_out, 16)
                sp.wait_ge(band_out, 16 * b + 16)
                sp.dma_start(band[:, :, 0:BAND],
                             bass.AP(band_dram, 0, [[H * PADW + 1, P], [PADW, H], [1, BAND]])).then_inc(band_in, 16)
            for s in range(STREAMS):
                sp.wait_ge(streams[s].x_new.sem, streams[s].x_new.at(0, B - 1, 4))
            for s in range(STREAMS):
                sp.wait_ge(streams[s].xn_stored, 16 * ROUNDS * B)
            sp.dma_start(rows0[:], xn0_dram[:].rearrange("(n p) d -> p n d", p=P)).then_inc(loaded["xn"], 16)

            def rows_in(phase, s, i, value):
                st = streams[s]
                sp.wait_ge(st.xnT_ps.sem, value)
                if phase == 1:
                    sp.dma_start(xn[s][:], sorted_dram[bass.ds((i + s * PASSES[1]) * BLK0, BLK0), :])\
                        .then_inc(st.rows_loaded, 16)
                else:
                    sp.dma_start(x_in[s][:], sorted_dram[bass.ds((i + s * PASSES[3]) * BLK3, BLK3), :]
                                 .rearrange("(a p) d -> p a d", p=P)).then_inc(st.rows_loaded, 16)

            def results_out(phase, s, i):
                st = streams[s]
                sp.wait_ge(st.x_new.sem, st.x_new.at(phase, i, 1))
                if phase == 1:
                    sp.dma_start(y_dram[bass.ds((i + s * PASSES[1]) * BLK0, BLK0), :], y_sb[s]).then_inc(st.y_out, 16)
                else:
                    sp.dma_start(y_dram[bass.ds((i + s * PASSES[3]) * BLK3, BLK3), :]
                                 .rearrange("(a p) d -> p a d", p=P), y3[s][:]).then_inc(st.y_out, 16)

            def blocks(phase, n_streams):
                for s in range(n_streams):
                    rows_in(phase, s, 0, streams[s].xnT_ps.at(phase, 0, 0))
                with sp.Fori(0, PASSES[phase] - 1) as i:
                    for s in range(n_streams):
                        rows_in(phase, s, i + 1, streams[s].xnT_ps.at(phase, i, 1))
                    for s in range(n_streams):
                        results_out(phase, s, i)
                for s in range(n_streams):
                    results_out(phase, s, PASSES[phase] - 1)

            sp.wait_ge(scattered, 16 * NT)
            blocks(1, STREAMS)
            for l in LAYERS:
                for n in ("wq", "wk", "wv", "wo"):
                    sp.dma_start(w2[n, l][:], t[f"{n}{l}"].rearrange("(c p) n -> p c n", p=P)).then_inc(loaded["p2"], 16)
                if l < 3:
                    for n, d in (("bq", bq2), ("bk", bk2), ("bv", bv2), ("bo", bo2)):
                        sp.dma_start(d[l][:], t[f"{n}{l}"]).then_inc(loaded["p2"], 16)
            sp.dma_start(head_mask[:], t["head_mask"]).then_inc(loaded["p2"], 16)
            sp.dma_start(slot_mask[:], t["slot_mask"]).then_inc(loaded["p2"], 16)
            sp.dma_start(u1[:], t["u1"].rearrange("(c p) n -> p c n", p=P)).then_inc(loaded["p2"], 16)
            sp.dma_start(v1[:], t["v1"]).then_inc(loaded["p2"], 16)
            sp.dma_start(u2[:], t["u2"].rearrange("(c p) n -> p c n", p=P)).then_inc(loaded["p2"], 16)
            sp.dma_start(v2[:], t["v2"]).then_inc(loaded["p2"], 16)
            sp.dma_start(rhs_T[:], t["rhsT"].rearrange("(c p) n -> p c n", p=P)).then_inc(loaded["p2"], 16)
            sp.dma_start(gate3[:], t["gate3"].rearrange("(c p) n -> p c n", p=P)).then_inc(loaded["p2"], 16)
            sp.dma_start(mask_in[:], t["mask"]).then_inc(loaded["mask"], 16)
            for s in range(STREAMS):
                sp.wait_ge(streams[s].x_new.sem, streams[s].x_new.at(2, B - 1, 12))
            for s in range(STREAMS):
                sp.wait_ge(streams[s].xn_stored, 16 * 2 * ROUNDS * B)
            sp.wait_ge(gathered, 16 * NT)
            sp.dma_start(rows3[0][:], xn3_dram[:].rearrange("(n p) d -> p n d", p=P)).then_inc(loaded["xn"], 16)
            sp.wait_ge(scattered, 16 * 3 * NT)
            blocks(3, MS3)
            sp.wait_ge(combined, 1)
            for b in range(B):
                sp.dma_start(out[b].rearrange("(n p) d -> p n d", p=P), x_all[:, b * TILES:(b + 1) * TILES, :])\
                    .then_inc(stored, 16)
            sp.wait_ge(stored, 32)

        @block.gpsimd
        def _(pool):
            link = Links(pool, pool_link)
            nc.gpsimd.memset(zeros[:], 0.0).then_inc(zeroed, 1)
            link(nc.gpsimd.memset(ident[:], 0.0))
            nc.gpsimd.affine_select(out=ident[:], in_=ident[:], compare_op=ALU.not_equal, fill=1.0, base=0,
                                    pattern=[[-1, P]], channel_multiplier=1).then_inc(consts, 1)
            nc.gpsimd.memset(ones[:], 1.0).then_inc(consts, 1)
            nc.gpsimd.memset(minus_half[:], -0.5).then_inc(consts, 1)
            nc.gpsimd.memset(vT0[:], 0.0).then_inc(consts, 1)
            link(nc.gpsimd.memset(tail_mask[:], 1.0))
            nc.gpsimd.affine_select(out=tail_mask[:], in_=tail_mask[:], compare_op=ALU.is_ge, fill=0.0,
                                    base=-MAXREL, pattern=[[1, J]], channel_multiplier=-1).then_inc(consts, 1)

            for m, op, base in ((causal_f, ALU.is_ge, 0),):
                link(nc.gpsimd.memset(m[:], 1.0))
                nc.gpsimd.affine_select(out=m[:], in_=m[:], compare_op=op, fill=0.0, base=base,
                                        pattern=[[-1, J]], channel_multiplier=1).then_inc(const2, 1)
            link(nc.gpsimd.memset(diag_f[:], 1.0))
            nc.gpsimd.affine_select(out=diag_f[:], in_=diag_f[:], compare_op=ALU.is_gt, fill=0.0, base=0,
                                    pattern=[[1, P]], channel_multiplier=-1).then_inc(const2, 1)
            nc.gpsimd.memset(onesq[:], 1.0).then_inc(const2, 1)
            for s in range(STREAMS):
                nc.gpsimd.memset(low_T[s][:], 1.0).then_inc(const2, 1)

            def ln_rstd(s, phase, k):
                st = streams[s]
                pool.wait_ge(st.aggr.sem, st.aggr.at(phase, b, k))
                pool.nop(nofuse=True)
                link(nc.gpsimd.tensor_scalar(rstd[s][:, 1:2], mean_var[s][:, 1:2], EPS, None, ALU.add))
                nc.gpsimd.tensor_tensor(rstd[s][:, 0:1], rstd[s][:, 1:2], minus_half[:], ALU.pow)\
                    .then_inc(st.rstd.sem, 1)

            def ln1(s, r):
                ln_rstd(s, 0, 2 * r + 1)

            def ln2(s, r):
                ln_rstd(s, 0, 2 * r + 2)

            def xn_store(s, r):
                st = streams[s]
                pool.wait_ge(st.xn.sem, st.xn.at(0, b, 2 * r + 2))
                pool.dma_start(xn0_dram[bass.ds(tile(b, s, r) * P, P), :], xn[s][:]).then_inc(st.xn_stored, 16)

            pool.wait_ge(loaded["ctx"], 16)
            with pool.Fori(0, B) as b:
                link.enter(b, POOL_LINKS1)
                pool.wait_ge(prep_ps.sem, prep_ps.at(0, b, 0))
                pool.nop(nofuse=True)
                nc.gpsimd.tensor_copy(ctx_b[:].rearrange("p c j -> p c j"),
                                      ctx_all[:, :, bass.ds(b, 1), :].rearrange("p c a j -> p c (a j)"))\
                    .then_inc(ctx_ready, 1)
                for f, s, r in order(STEPS1, dict(engine=PO, stats1=ln1, stats2=ln2, apply2=xn_store)):
                    f(s, r)
            link.leave(B)

            def scatter(rows, n, done):
                for tl in range(NT):
                    pool.indirect_dma_start(out=sorted_dram[:], out_offset=bass.IndirectOffsetOnAxis(
                        ap=slot[:, n, tl:tl + 1], axis=0), in_=rows[:, tl, :], in_offset=None).then_inc(done, 16)

            def gather(rows, n, done):
                for tl in range(NT):
                    pool.indirect_dma_start(out=rows[:, tl, :], out_offset=None, in_=y_dram[:],
                                            in_offset=bass.IndirectOffsetOnAxis(ap=slot[:, n, tl:tl + 1], axis=0))\
                        .then_inc(done, 16)

            def load_weights(phase, n_streams, w_in, w_out, src_in, src_out, n_exp):
                with pool.Fori(0, PASSES[phase]) as i:
                    link.enter(i, 2 * n_streams)
                    for n, (w, src) in enumerate(((w_in, src_in), (w_out, src_out))):
                        for s in range(n_streams):
                            st = streams[s]
                            last = (st.f_ps, st.y_ps)[n]
                            pool.wait_ge(last.sem, last.at(phase, i, 0))
                            pool.nop(nofuse=True)
                            link(nc.gpsimd.tensor_copy(load_now[:, n, s:s + 1],
                                                       load[:, bass.ds(i + s * PASSES[phase], 1)]))
                            pool.nop(nofuse=True)
                            pool.indirect_dma_start(
                                out=w[s][:].rearrange("p a c n -> p (a c n)" if n == 0 else "p c n -> p (c n)"),
                                out_offset=None, in_=t[src],
                                in_offset=bass.IndirectOffsetOnAxis(ap=load_now[:, n, s:s + 1], axis=0),
                                bounds_check=n_exp * P - 1, oob_is_err=False)\
                                .then_inc((st.in_loaded, st.out_loaded)[n], 16)
                link.leave(PASSES[phase])

            pool.wait_ge(zero_out, 16 * (ROWS // (8 * P)))
            pool.wait_ge(scaled, 1)
            scatter(rows0, 0, scattered)
            load_weights(1, STREAMS, w_in0, w_out0, "w_in0", "w_out0", E0)
            for s in range(STREAMS):
                pool.wait_ge(streams[s].y_out, 16 * PASSES[1])
            gather(rows0, 0, gathered)

            def rstd2(k):
                return lambda s, r: ln_rstd(s, 2, 6 * r + k)

            def fill(l):
                def step(s, r):
                    st = streams[s]
                    if l < 3 and (s or r):
                        return
                    pool.wait_ge(st.q_ps.sem, st.q_ps.at(2, b, 3 * r + l))
                    pool.nop(nofuse=True)
                    ins = nc.gpsimd.memset(probs[s][:], NEVER if l < 3 else MASKED * 4)
                    if l == 3:
                        ins = nc.gpsimd.tensor_copy(
                            filled_mask[s][:], unmasked[:, bass.ds(tile(b, s, r), 1), :].rearrange("p a j -> p (a j)"))
                    ins.then_inc(st.filled.sem, 1)
                return step

            def xn_store2(s, r):
                st = streams[s]
                pool.wait_ge(st.xn.sem, st.xn.at(2, b, 6 * r + 6))
                pool.dma_start(xn3_dram[bass.ds(tile(b, s, r) * P, P), :], xn[s][:]).then_inc(st.xn_stored, 16)

            own = {f"stats{l}": rstd2(2 * l - 1) for l in LAYERS}
            own |= {f"fstats{l}": rstd2(2 * l) for l in LAYERS} | {f"q{l}": fill(l) for l in LAYERS}
            pool.wait_ge(rhs_sb, 1)
            with pool.Fori(0, B) as b:
                link.enter(b, POOL_LINKS2)
                pool.wait_ge(prep_ps.sem, prep_ps.at(2, b, 0))
                pool.nop(nofuse=True)
                nc.gpsimd.tensor_copy(ctx_b[:], ctx_all[:, :, bass.ds(b, 1), :].rearrange("p c a j -> p c (a j)"))\
                    .then_inc(ctx_ready, 1)
                pool.wait_ge(ctx_ready, B + b + 1)
                pool.nop(nofuse=True)
                for kc in range(KC):
                    last = nc.gpsimd.tensor_copy(ctx_rep[:, kc, :].rearrange("p (n j) -> p n j", j=J),
                                                 ctx_b[:, kc:kc + 1, :].to_broadcast([P, REPS, J]))
                last.then_inc(rep_ready, 1)
                for f, s, r in order(STEPS2, own | dict(engine=PO, fapply3=xn_store2)):
                    f(s, r)
            link.leave(B)

            pool.wait_ge(routed, 2)
            pool.wait_ge(loaded["xn"], 32)
            for n in range(2):
                scatter(rows3[0], n, scattered)
            load_weights(3, MS3, w_in3, w_out3, "w_in3", "w_out3", E3)
            for s in range(MS3):
                pool.wait_ge(streams[s].y_out, 16 * (PASSES[1] + PASSES[3]))
            for n in range(2):
                gather(rows3[n], n, gathered3[n])

        def act_copy(dst, src):
            return nc.scalar.activation(dst, src, ACT.Copy)

        @block.scalar
        def _(act):
            def prep(b):
                act.wait_ge(prep_ps.sem, prep_ps.at(0, b, 1))
                for a in range(2):
                    last = nc.scalar.activation(kT0[:, 4 * a:4 * a + 4, :],
                                                ps[0][:, a, 0:4 * J].rearrange("p (c j) -> p c j", j=J),
                                                ACT.Identity, bias=relk_0[:])
                last.then_inc(prep_sb.sem, 1)
                for n, (kc, half) in enumerate(((0, 0), (0, 1), (1, 0), (1, 1))):
                    act.wait_ge(prep_ps.sem, prep_ps.at(0, b, 2 + n))
                    pair = (2 + n) % 4
                    for par in range(2):
                        last = act_copy(
                            qk0[:, kc, half * HALF:(half + 1) * HALF].rearrange("p (c r j) -> p r c j", r=2, j=J)[:, par],
                            ps[pair][:, par, 0:QUART].rearrange("p (c j) -> p c j", j=J))
                    last.then_inc(prep_sb.sem, 1)
                for n in range(3):
                    act.wait_ge(prep_ps.sem, prep_ps.at(0, b, 6 + n))
                    pair = (2 + n) % 4
                    if n < 2:
                        last = act_copy(vo0[:, 4 * n:4 * n + 4, :].rearrange("p (a g) n -> p a (g n)", a=2), ps[pair][:])
                    else:
                        act_copy(vo0[:, 8, :], ps[pair][:, 0, 0:D])
                        last = act_copy(vo0[0:LAST_CH, 9, :], ps[pair][0:LAST_CH, 0, D:2 * D])
                    last.then_inc(prep_sb.sem, 1)
                act.wait_ge(prep_ps.sem, prep_ps.at(0, b, 9))
                act_copy(relvo[:].rearrange("p g n -> p (g n)"), ps[1][:].rearrange("p a n -> p (a n)"))\
                    .then_inc(prep_sb.sem, 1)

            def xn_T(s, phase, i, k):
                st = streams[s]
                act.wait_ge(st.xnT_ps.sem, st.xnT_ps.at(phase, i, k))
                act_copy(xnT[s][:].rearrange("p c n -> p (c n)"), ps[s][:, 0, 0:D]).then_inc(st.xnT.sem, 1)

            def xnT1(s, r):
                xn_T(s, 0, b, 2 * r + 1)

            def xnT2(s, r):
                xn_T(s, 0, b, 2 * r + 2)

            def rel_scores(s, r):
                if s or r:
                    return
                st = streams[0]
                act.wait_ge(st.q_ps.sem, st.q_ps.at(0, b, 1))
                act_copy(qT0.rearrange("p (a c) n -> p a (c n)", a=2), ps[0][:]).then_inc(st.q.sem, 1)
                for g in range(4):
                    act.wait_ge(st.q_ps.sem, st.q_ps.at(0, b, 2 + g))
                    for par in range(2):
                        last = act_copy(rel_q[:, 4 * g:4 * g + 4, :].rearrange("p (c r) e -> p r c e", r=2)[:, par],
                                        ps[0][:, par, 0:2 * EXT].rearrange("p (c e) -> p c e", e=EXT))
                    last.then_inc(st.q.sem, 1)

            def exp(s, phase, k, half):
                st = streams[s]
                act.wait_ge(st.p_sub.sem, st.p_sub.at(phase, b, k))
                part = probs[s][:, half * HALF:(half + 1) * HALF]
                nc.scalar.activation(part, part, ACT.Exp, scale=(D0 if phase == 0 else ATT) ** -0.5)\
                    .then_inc(st.p_exp.sem, 1)

            def exp0(s, r):
                exp(s, 0, 2 * r + 1, 0)

            def exp1(s, r):
                exp(s, 0, 2 * r + 2, 1)

            def probs_T(s, phase, k, part):
                st = streams[s]
                act.wait_ge(st.pT_ps.sem, st.pT_ps.at(phase, b, k))
                flat = probsT[s][:, 5 * part:5 * part + 5, :].rearrange("p c n -> p (c n)")
                m = P if part == 0 else LAST_CH
                act_copy(flat[:, 0:512], ps[s][:, 0, :])
                act_copy(flat[0:m, 512:640], ps[s][0:m, 1, 0:P]).then_inc(st.pT.sem, 1)

            def pT0(s, r):
                probs_T(s, 0, 2 * r + 1, 0)

            def pT1(s, r):
                probs_T(s, 0, 2 * r + 2, 1)

            def band_T(s, r):
                if s or r:
                    return
                st = streams[0]
                act.wait_ge(st.q_ps.sem, st.q_ps.at(0, b, 6))
                act_copy(bandT[:].rearrange("p c n -> p (c n)"), ps[0][:, 0, :]).then_inc(st.q.sem, 1)

            def gate_act(s, phase, i, k):
                st = streams[s]
                act.wait_ge(st.f_ps.sem, st.f_ps.at(phase, i, k))
                nc.scalar.activation(hid[s][:, 0, :], ps[s][:, 0, :], ACT.Silu).then_inc(st.f.sem, 1)

            act.wait_ge(consts, 5)
            act.wait_ge(loaded["k"], 32)
            with act.Fori(0, B) as b:
                prep(b)
                for f, s, r in order(STEPS1, dict(engine=AC, apply1=xnT1, rel=rel_scores, half0=exp0, half1=exp1, pT0=pT0, pT1=pT1,
                                                  band=band_T, apply2=xnT2, gate_up=lambda s, r: gate_act(s, 0, b, r + 1))):
                    f(s, r)

            act.wait_ge(top_ready, 1)
            nc.scalar.activation(route[:, 1, :], route[:, 0, :], ACT.Exp, scale=-1.0).then_inc(score_exp, 1)
            with act.Fori(0, PASSES[1]) as i:
                for s in range(STREAMS):
                    xn_T(s, 1, i, 1)
                for s in range(STREAMS):
                    gate_act(s, 1, i, 1)

            act.wait_ge(rhs_ps, 1)
            act_copy(rhs_qT[:].rearrange("p c n -> p (c n)"), ps[0][:, 0, 0:D].bitcast(BF16))
            act_copy(rhs_scale_row[:], ps[0][:, 1, 0:D]).then_inc(rhs_sb, 1)

            def xnT_of(n):
                return lambda s, r: xn_T(s, 2, b, 5 * r + n)

            def q_T(l):
                def step(s, r):
                    st = streams[s]
                    act.wait_ge(st.q_ps.sem, st.q_ps.at(2, b, 3 * r + l))
                    if l == 3:
                        last = act_copy(qT[s][:].rearrange("p c n -> p (c n)"), ps[s][:, 0, 0:D])
                    else:
                        for c in range(KC):
                            last = nc.scalar.activation(qT[s][:, c, :], ps[s][:, 0, c * P:c * P + P], ACT.Identity,
                                                        bias=bq2[l][:, c:c + 1])
                    last.then_inc(st.q.sem, 1)
                return step

            def out_T(l):
                def step(s, r):
                    st = streams[s]
                    act.wait_ge(st.oT_ps.sem, st.oT_ps.at(2, b, 3 * r + l))
                    act_copy(xnT[s][:].rearrange("p c n -> p (c n)"), ps[s][:, 1, 0:D]).then_inc(st.oT.sem, 1)
                return step

            def low_copy(n):
                def step(s, r):
                    st = streams[s]
                    act.wait_ge(st.f_ps.sem, st.f_ps.at(2, b, 4 * r + n))
                    act_copy(low_T[s][0:LOW, :], ps[s][0:LOW, 0, 0:P]).then_inc(st.f.sem, 1)
                return step

            def gelu(s, r):
                st = streams[s]
                act.wait_ge(st.f_ps.sem, st.f_ps.at(2, b, 4 * r + 2))
                nc.scalar.activation(probs[s][:, 0:F1], ps[s][:].rearrange("p a n -> p (a n)"), ACT.Gelu_apprx_tanh)\
                    .then_inc(st.f.sem, 1)

            def quant_T(s, r):
                st = streams[s]
                act.wait_ge(st.f_ps.sem, st.f_ps.at(2, b, 4 * r + 4))
                act_copy(x_qT[s][:], ps[s][:, 0, 0:P].bitcast(BF16)).then_inc(st.f.sem, 1)

            own = {"engine": AC}
            for l in LAYERS:
                own |= {f"apply{l}": xnT_of({1: 1, 2: 3, 3: 4}[l]), f"q{l}": q_T(l), f"oT{l}": out_T(l)}
                own |= {f"half{h}_{l}": (lambda s, r, l=l, h=h: exp(s, 2, 6 * r + 2 * l - 1 + h, h)) for h in range(2)}
                own |= {f"pT{h}_{l}": (lambda s, r, l=l, h=h: probs_T(s, 2, 6 * r + 2 * l - 1 + h, h)) for h in range(2)}
            own |= dict(fapply1=xnT_of(2), fapply3=xnT_of(5), low1=low_copy(1), gelu1=gelu, low21=low_copy(3), quant2=quant_T)
            with act.Fori(0, B) as b:
                for f, s, r in order(STEPS2, own):
                    f(s, r)

            act.wait_ge(top_ready, 2)
            e1, e2 = (probs[n][:, 0:NT * E3] for n in (2, 3))
            nc.scalar.activation(e1, e1, ACT.Exp, scale=-1.0)
            nc.scalar.activation(e2, e2, ACT.Exp).then_inc(score_exp, 1)
            with act.Fori(0, PASSES[3]) as i:
                for s in range(MS3):
                    st = streams[s]
                    act.wait_ge(st.xnT_ps.sem, st.xnT_ps.at(3, i, 1))
                    act_copy(x_inT[s][:].rearrange("p c n -> p (c n)"), ps[2 * s][:, 0, :]).then_inc(st.xnT.sem, 1)
                for n in range(F3 // P // 2):
                    for s in range(MS3):
                        st = streams[s]
                        act.wait_ge(st.f_ps.sem, st.f_ps.at(3, i, n + 1))
                        if n:
                            act.wait_ge(st.fm.sem, st.fm.at(3, i, n))
                        nc.scalar.activation(act3[s][:], ps[2 * s + (n + 1) % 2][:, 0, :], ACT.Silu).then_inc(st.f.sem, 1)

        @block.vector
        def _(dve):
            link = Links(dve, dve_link)
            for s in range(STREAMS):
                dve.sem_inc(streams[s].x_new.sem, 1)
            dve.wait_ge(loaded["k"], 32)
            dve.wait_ge(loaded["v"], 32)
            dve.wait_ge(loaded["rel"], 32)
            nc.vector.tensor_scalar(relk_ext[:], relk_ext[:], relk_0[:], None, ALU.subtract)
            link(nc.vector.memset(relv_m[:], 0.0))
            for par in range(2):
                for r in range(2):
                    at = (2 * par + r) * NREL
                    last = nc.vector.tensor_scalar(relv_m[D0 * r:D0 * r + D0, par, at:at + NREL],
                                                   relv_T[D0 * r:D0 * r + D0, :], relv_0[D0 * r:D0 * r + D0, :],
                                                   None, ALU.subtract)
            last.then_inc(rel_const, 1)
            dve.wait_ge(const2, 7)
            nc.vector.tensor_copy(causal[:], causal_f[:])
            nc.vector.tensor_copy(squareb[:], diag_f[:])
            nc.vector.tensor_copy(onesb[:], onesq[:])

            def ln_stats(s, r):
                if s == 0:
                    dve.wait_ge(loaded["x1" if r else "x0"], 16)
                dve.nop(nofuse=True)
                link(nc.vector.bn_stats(stats[s][:], x_tile(b, s, r)))
                dve.nop(nofuse=True)
                nc.vector.bn_aggr(mean_var[s][:], stats[s][:]).then_inc(streams[s].aggr.sem, 1)

            def ln_apply(s, r, phase, k):
                st = streams[s]
                dve.wait_ge(st.rstd.sem, st.rstd.at(phase, b, k))
                nc.vector.tensor_scalar(xn[s][:], x_tile(b, s, r), mean_var[s][:, 0:1], rstd[s][:, 0:1],
                                        ALU.subtract, ALU.mult).then_inc(st.xn.sem, 1)

            def ln1a(s, r):
                ln_stats(s, r)

            def ln1b(s, r):
                if r:
                    dve.wait_ge(streams[s].xn_stored, 16 * (b * ROUNDS + r))
                ln_apply(s, r, 0, 2 * r + 1)

            def ln2a(s, r):
                ln_stats(s, r)

            def ln2b(s, r):
                ln_apply(s, r, 0, 2 * r + 2)

            def softmax_half(s, r, half):
                st = streams[s]
                dve.wait_ge(st.s_ps.sem, st.s_ps.at(0, b, 2 * r + half + 1))
                src, dst = psum_scores(s), sbuf_scores(s, half)
                if s == 0 and r == 0:
                    if half == 0:
                        dve.wait_ge(rel_in, 16 * b + 16)
                    rel = heads4(rel_s[:, half * HALF:(half + 1) * HALF].rearrange("p (r n) -> p r n", r=2))
                    link(nc.vector.tensor_tensor(dst, src, rel, ALU.add))
                    src = dst
                m = mx[s][:, 8 * half:8 * half + 8].rearrange("p (r q) -> p r q", r=2)
                link(nc.vector.tensor_reduce(out=m, in_=src, axis=X, op=ALU.max))
                nc.vector.tensor_tensor(dst, src, rep(m, J), ALU.subtract).then_inc(st.p_sub.sem, 1)

            def soft0(s, r):
                softmax_half(s, r, 0)

            def soft1(s, r):
                softmax_half(s, r, 1)

            def normalise(s, r):
                st = streams[s]
                dve.wait_ge(st.p_exp.sem, st.p_exp.at(0, b, 2 * r + 2))
                p3 = probs[s][:].rearrange("p (h j) -> p h j", j=J)
                link(nc.vector.tensor_reduce(out=mx[s][:], in_=p3, axis=X, op=ALU.add))
                link(nc.vector.reciprocal(mx[s][:], mx[s][:]))
                ins = nc.vector.tensor_tensor(p3, p3, rep(mx[s][:], J), ALU.mult)
                ins.then_inc(st.o.sem, 1)
                if s == 0 and r == 0:
                    dve.wait_ge(st.o.sem, st.o.at(0, b, 1))
                    link(nc.vector.memset(band_src, 0.0))
                    nc.vector.tensor_copy(band_src[:, :, MAXREL - 1:MAXREL - 1 + J], p3).then_inc(band_ready, 1)
                    tail = rel_s[:].rearrange("p (h j) -> p h j", j=J)
                    link(nc.vector.tensor_tensor(tail, p3, tail_mask[:].unsqueeze(1).to_broadcast([P, H, J]), ALU.mult))
                    nc.vector.tensor_reduce(out=band[:, :, BAND], in_=tail, axis=X, op=ALU.add).then_inc(band_tail, 1)

            def residual(s, r, u):
                st = streams[s]
                dve.wait_ge(st.y_ps.sem, st.y_ps.at(0, b, 2 * r + u + 1))
                if u:
                    nc.vector.tensor_copy(logits0[:, bass.ds(tile(b, s, r), 1), :].rearrange("p a d -> p (a d)"),
                                          ps[s][:, 1, 0:E0])
                ins = nc.vector.tensor_tensor(x_tile(b, s, r), ps[s][:, 0, 0:D], x_tile(b, s, r), ALU.add)
                ins.then_inc(st.x_new.sem, 1)
                dve.wait_ge(st.x_new.sem, st.x_new.at(0, b, 2 * r + u + 1))

            def res1(s, r):
                residual(s, r, 0)

            def res2(s, r):
                residual(s, r, 1)

            def gate_up(s, r):
                st = streams[s]
                dve.wait_ge(st.f.sem, st.f.at(0, b, r + 1))
                nc.vector.tensor_tensor(hid[s][:, 1, :], ps[s][:, 1, :], hid[s][:, 0, :], ALU.mult).then_inc(st.fm.sem, 1)

            dve.wait_ge(consts, 5)
            nc.vector.tensor_copy(identb[:], ident[:])

            def prep(b):
                dve.wait_ge(v_ps, b + 1)
                dve.nop(nofuse=True)
                for c in range(C0):
                    for r in range(2):
                        at = c * 3 * P + (2 * c + r) * J - window(c)
                        last = nc.vector.tensor_scalar(vT0[D0 * r:D0 * r + D0, at:at + J],
                                                       ps[1][D0 * r:D0 * r + D0, c // 4, c % 4 * J:c % 4 * J + J],
                                                       relv_0[D0 * r:D0 * r + D0, :], None, ALU.add)
                last.then_inc(vT_ready, 1)

            with dve.Fori(0, B) as b:
                link.enter(b, DVE_LINKS1)
                prep(b)
                for f, s, r in order(STEPS1, dict(engine=DV, stats1=ln1a, apply1=ln1b, half0=soft0, half1=soft1, norm=normalise,
                                                  out1=res1, stats2=ln2a, apply2=ln2b, gate_up=gate_up, out2=res2)):
                    f(s, r)
                for s in range(STREAMS):
                    dve.wait_ge(streams[s].xn_stored, 16 * (b * ROUNDS + ROUNDS))
            link.leave(B)

            def routing(logits, n_exp, block, n_blocks, n_streams, step, top2):
                tmp = [x[:, 0:NT * n_exp] for x in probs] + [x[:].rearrange("p c n -> p (c n)")[:, 0:NT * n_exp] for x in probsT]
                tmp = [x.rearrange("p (n e) -> p n e", e=n_exp) for x in tmp]
                revs = rev[:, E0 - n_exp:E0].unsqueeze(1).to_broadcast([P, NT, n_exp])
                tt, tr = nc.vector.tensor_tensor, nc.vector.tensor_reduce

                def top(scores, best, hot):
                    link(tr(out=best, in_=scores, axis=X, op=ALU.max))
                    link(tt(tmp[7], scores, rep(best, n_exp), ALU.is_equal))
                    link(tt(tmp[7], tmp[7], revs, ALU.mult))
                    link(tr(out=route[:, 7, :], in_=tmp[7], axis=X, op=ALU.max))
                    link(tt(hot, tmp[7], rep(route[:, 7, :], n_exp), ALU.is_equal))

                hots = [tmp[0], tmp[1]][:2 if top2 else 1]
                m1, m2, w1, w2s = (route[:, n, :] for n in range(4))
                top(logits, route[:, 0, :], hots[0])
                if not top2:
                    nc.vector.tensor_copy(one_hot[:].rearrange("p (n e) -> p n e", e=n_exp), hots[0])\
                        .then_inc(one_hot_ready, 1)
                    nc.vector.tensor_copy(route[:, 5, :], route[:, 0, :]).then_inc(top_ready, 1)
                    dve.wait_ge(score_exp, 1)
                    link(nc.vector.tensor_scalar_add(route[:, 1, :], route[:, 1, :], 1.0))
                    link(nc.vector.reciprocal(route[:, 1, :], route[:, 1, :]))
                else:
                    link(nc.vector.scalar_tensor_tensor(out=tmp[4], in0=hots[0], scalar=NEVER, in1=logits,
                                                        op0=ALU.mult, op1=ALU.add))
                    top(tmp[4], route[:, 1, :], hots[1])
                    oh = one_hot[:, 0:NT * n_exp].rearrange("p (n e) -> p n e", e=n_exp)
                    tt(oh, hots[0], hots[1], ALU.add).then_inc(one_hot_ready, 1)
                    for n, best in ((2, m1), (3, m2)):
                        link(nc.vector.scalar_tensor_tensor(out=tmp[5 + n - 2], in0=logits, scalar=-1.0, in1=logits,
                                                            op0=ALU.mult, op1=ALU.max))
                        link(tt(tmp[5 + n - 2], tmp[5 + n - 2], rep(best, n_exp), ALU.max))
                        link(tt(tmp[7], rep(best, n_exp), logits, ALU.subtract))
                        if n == 2:
                            nc.vector.tensor_copy(tmp[2], tmp[7])
                        link(nc.vector.scalar_tensor_tensor(out=tmp[5 + n - 2], in0=tmp[5 + n - 2], scalar=2 * JITTER,
                                                            in1=tmp[7], op0=ALU.mult, op1=ALU.is_ge))
                    tt(tmp[3], tmp[4], rep(m2, n_exp), ALU.subtract).then_inc(top_ready, 1)
                    dve.wait_ge(score_exp, 2)
                    for n in range(2):
                        link(tt(tmp[2 + n], tmp[2 + n], tmp[5 + n], ALU.mult))
                        link(tr(out=route[:, 2 + n, :], in_=tmp[2 + n], axis=X, op=ALU.add))
                        link(nc.vector.reciprocal(route[:, 2 + n, :], route[:, 2 + n, :]))
                dve.wait_ge(rank_ready, 2 if top2 else 1)
                nblk, end, start = (blocks_of[:, n, 0:n_exp] for n in range(3))
                n_step = B * T // block
                big = probsT[0][:].rearrange("p c n -> p (c n)")
                cmp = big[:, 0:n_exp * n_step].rearrange("p (e k) -> p e k", k=n_step)
                link(tt(cmp, rep(ps[1][:, 0, 0:n_exp], n_step),
                        kstep[:, step, 0:n_step].unsqueeze(1).to_broadcast([P, n_exp, n_step]), ALU.is_gt))
                link(tr(out=nblk, in_=cmp, axis=X, op=ALU.add))
                tri = big[:, 0:n_exp * n_exp].rearrange("p (e f) -> p e f", f=n_exp)
                link(tt(tri, nblk.unsqueeze(1).to_broadcast([P, n_exp, n_exp]), low_tri[:, 0:n_exp, 0:n_exp], ALU.mult))
                link(tr(out=end, in_=tri, axis=X, op=ALU.add))
                link(tt(start, end, nblk, ALU.subtract))
                half = n_blocks // 2
                for n in range(2):
                    out3 = big[:, 0:half * n_exp].rearrange("p (k e) -> p k e", e=n_exp)
                    link(tt(out3, end.unsqueeze(1).to_broadcast([P, half, n_exp]),
                            rep(blks[:, n * half:(n + 1) * half], n_exp), ALU.is_le))
                    link(tr(out=expert[:, n * half:(n + 1) * half], in_=out3, axis=X, op=ALU.add))
                e, ld = expert[:, 0:n_blocks], load_f[:, 0:n_blocks]
                link(tt(ld[:, 1:], e[:, 1:], e[:, 0:n_blocks - 1], ALU.is_equal))
                link(nc.vector.scalar_tensor_tensor(out=ld[:, 1:], in0=ld[:, 1:], scalar=float(n_exp), in1=e[:, 1:],
                                                    op0=ALU.mult, op1=ALU.add))
                first = ld.rearrange("p (s i) -> p s i", i=n_blocks // n_streams)[:, :, 0]
                link(nc.vector.tensor_scalar(first, e.rearrange("p (s i) -> p s i", i=n_blocks // n_streams)[:, :, 0],
                                             float(n_exp - 1), None, ALU.min))
                link(nc.vector.tensor_scalar(ld, ld, float(P), row[:], ALU.mult, ALU.add))
                nc.vector.tensor_copy(load[:, 0:n_blocks], ld)
                link(nc.vector.scalar_tensor_tensor(
                    out=tmp[7], in0=start.unsqueeze(1).to_broadcast([P, NT, n_exp]), scalar=float(block),
                    in1=ps[0][:, 0, 0:NT * n_exp].rearrange("p (n e) -> p n e", e=n_exp), op0=ALU.mult, op1=ALU.add))
                for n, hot in enumerate(hots):
                    link(tt(tmp[5 + n], tmp[7], hot, ALU.mult))
                    link(tr(out=route[:, 5 + n, :], in_=tmp[5 + n], axis=X, op=ALU.add))
                    last = nc.vector.tensor_copy(slot[:, n, :], route[:, 5 + n, :])
                last.then_inc(routed, 1)

            dve.wait_ge(loaded["shape"], 16 * 5)
            routing(logits0[:], E0, BLK0, NB0, STREAMS, 0, False)
            dve.wait_ge(loaded["xn"], 16)
            for tl in range(NT):
                last = nc.vector.tensor_scalar(rows0[:, tl, :], rows0[:, tl, :], route[:, 1, tl:tl + 1], None, ALU.mult)
            last.then_inc(scaled, 1)

            def expert_mul(s, phase, i, k):
                st = streams[s]
                dve.wait_ge(st.f.sem, st.f.at(phase, i, k))
                nc.vector.tensor_tensor(hid[s][:, 1, :], ps[s][:, 1, :], hid[s][:, 0, :], ALU.mult).then_inc(st.fm.sem, 1)

            def expert_pass(i, first):
                for s in range(STREAMS):
                    expert_mul(s, 1, i, 1)
                for s in range(STREAMS):
                    st = streams[s]
                    dve.wait_ge(st.y_ps.sem, st.y_ps.at(1, i, 1))
                    if not first:
                        dve.wait_ge(st.y_out, 16 * i)
                    nc.vector.tensor_copy(y_sb[s], ps[s][:, 0, 0:D]).then_inc(st.x_new.sem, 1)

            expert_pass(0, True)
            with dve.Fori(1, PASSES[1]) as i:
                expert_pass(i, False)
            dve.wait_ge(gathered, 16 * NT)
            for tl in range(NT):
                last = nc.vector.tensor_tensor(x_all[:, tl, :], rows0[:, tl, :], x_all[:, tl, :], ALU.add)
            link(last)

            dve.wait_ge(loaded["p2"], 16 * (12 + 8 + 8))
            dve.wait_ge(loaded["mask"], 16)
            nc.vector.tensor_scalar(unmasked[:].rearrange("p n j -> p (n j)"), mask_in[:].bitcast(U8), 0.0, None, ALU.is_equal)
            for l in LAYERS:
                nc.vector.tensor_copy(v_bd[l][:].rearrange("p k (s d) -> p k s d", d=VW)[:, :, :, ATT], slot_mask[:])

            def quantise(out_q, src, scales, tmp2):
                s_, r_ = scales
                link(nc.vector.tensor_reduce(out=s_, in_=src, axis=X, op=ALU.max, apply_absolute_value=True))
                link(nc.vector.tensor_scalar(s_, s_, 1e-12, 1.0 / QMAX, ALU.max, ALU.mult))
                link(nc.vector.reciprocal(r_, s_))
                link(nc.vector.tensor_scalar(tmp2, src, r_, QMAX, ALU.mult, ALU.min))
                link(nc.vector.tensor_scalar(tmp2, tmp2, -QMAX, MAGIC, ALU.max, ALU.add))
                return nc.vector.tensor_scalar(out_q, tmp2, MAGIC, None, ALU.subtract)

            for c in range(KC):
                link(quantise(rhs_q[:, c, :], rhs_T[:, c, :], (rhs_scale[:, c:c + 1], rhs_scale[:, 2 + c:3 + c]),
                              rhs_T[:, c, :]))
                last = nc.vector.tensor_scalar(diag[:, c, :], ident[:], rhs_scale[:, c:c + 1], None, ALU.mult)
            last.then_inc(rhs_ready, 1)

            def prep2(b):
                for l in LAYERS:
                    dve.wait_ge(prep_ps.sem, prep_ps.at(2, b, l))
                    for c in range(KC):
                        src = ps[l - 1][:, 0, c * J:c * J + J].unsqueeze(1).to_broadcast([P, 4, J])
                        dst = k_bd[l][:, c, :].rearrange("p (q j) -> p q j", j=J)
                        if l < 3:
                            nc.vector.scalar_tensor_tensor(out=dst, in0=src, scalar=bk2[l][:, c:c + 1],
                                                           in1=rep(head_mask[:], J), op0=ALU.add, op1=ALU.mult)
                        else:
                            nc.vector.tensor_tensor(dst, src, rep(head_mask[:], J), ALU.mult)
                    nc.vector.tensor_tensor(
                        v_bd[l][:].rearrange("p k (s d) -> p (k s) d", d=VW)[:, :, 0:ATT],
                        ps[l - 1][:, 1, 0:NCH * SLOTS * ATT].rearrange("p (n d) -> p n d", d=ATT),
                        rep(slot_mask[:].rearrange("p k s -> p (k s)"), ATT), ALU.mult).then_inc(prep_sb.sem, 1)

            def stats2(s, r):
                ln_stats(s, r)

            def apply2(k):
                def step(s, r):
                    if k == 1 and r:
                        dve.wait_ge(streams[s].xn_stored, 16 * (b * ROUNDS + (ROUNDS * B + r)))
                    ln_apply(s, r, 2, 6 * r + k)
                return step

            def half2(l, half):
                def step(s, r):
                    st = streams[s]
                    dve.wait_ge(st.s_ps.sem, st.s_ps.at(2, b, 6 * r + 2 * l - 1 + half))
                    src, dst = psum_scores(s), sbuf_scores(s, half)
                    if l == 3 or (s == 0 and r == 0):
                        k = r + 1 if s else (3 + r if l == 3 else l)
                        dve.wait_ge(st.filled.sem, st.filled.at(2, b, k))
                        dve.nop(nofuse=True)
                        m = (filled_mask[s] if l == 3 else causal)[:]
                        for a in range(2):
                            last = nc.vector.copy_predicated(dst[:, a], m.unsqueeze(1).to_broadcast([P, 4, J]), src[:, a])
                        link(last)
                        src = dst
                    m = mx[s][:, 8 * half:8 * half + 8].rearrange("p (r q) -> p r q", r=2)
                    link(nc.vector.tensor_reduce(out=m, in_=src, axis=X, op=ALU.max))
                    nc.vector.tensor_tensor(dst, src, rep(m, J), ALU.subtract).then_inc(st.p_sub.sem, 1)
                return step

            def attended(l):
                def step(s, r):
                    st = streams[s]
                    dve.wait_ge(st.o_ps.sem, st.o_ps.at(2, b, 3 * r + l))
                    av = ps[s][:, 0, 0:H * VW].rearrange("p (h d) -> p h d", d=VW)
                    link(nc.vector.reciprocal(mx[s][:], av[:, :, ATT]))
                    nc.vector.tensor_tensor(xn[s][:].rearrange("p (h d) -> p h d", d=ATT), av[:, :, 0:ATT],
                                            rep(mx[s][:], ATT), ALU.mult).then_inc(st.o.sem, 1)
                return step

            def residual2(k):
                def step(s, r):
                    st = streams[s]
                    dve.wait_ge(st.y_ps.sem, st.y_ps.at(2, b, 6 * r + k))
                    if k == 6:
                        nc.vector.tensor_copy(logits3[:, bass.ds(tile(b, s, r), 1), :].rearrange("p a d -> p (a d)"),
                                              ps[s][:, 0, 0:E3]).then_inc(st.x_new.sem, 1)
                        return
                    y = ps[s][:, 0, 0:D]
                    if k == 4:
                        link(nc.vector.scalar_tensor_tensor(out=xn[s][:], in0=y, scalar=scale[s][:, 0:1],
                                                            in1=rhs_scale_row[:], op0=ALU.mult, op1=ALU.mult))
                        y = xn[s][:]
                    nc.vector.tensor_tensor(x_tile(b, s, r), y, x_tile(b, s, r), ALU.add).then_inc(st.x_new.sem, 1)
                    dve.wait_ge(st.x_new.sem, st.x_new.at(2, b, 6 * r + k))
                return step

            def quant(s, r):
                st = streams[s]
                dve.wait_ge(st.xn.sem, st.xn.at(2, b, 6 * r + 4))
                quantise(x_q[s][:], xn[s][:], (scale[s][:, 0:1], scale[s][:, 1:2]), xn[s][:]).then_inc(st.fm.sem, 1)

            own = {"engine": DV}
            for l in LAYERS:
                own |= {f"stats{l}": stats2, f"fstats{l}": stats2, f"apply{l}": apply2(2 * l - 1), f"fapply{l}": apply2(2 * l)}
                own |= {f"half0_{l}": half2(l, 0), f"half1_{l}": half2(l, 1), f"av{l}": attended(l),
                        f"out{l}": residual2(2 * l - 1)}
            own |= dict(fout1=residual2(2), fout2=residual2(4), gate3=residual2(6), quant2=quant)
            with dve.Fori(0, B) as b:
                link.enter(b, DVE_LINKS2)
                prep2(b)
                for f, s, r in order(STEPS2, own):
                    f(s, r)
                for s in range(STREAMS):
                    dve.wait_ge(streams[s].xn_stored, 16 * (b * ROUNDS + ROUNDS * (B + 1)))
            link.leave(B)

            for s in range(STREAMS):
                dve.wait_ge(streams[s].x_new.sem, streams[s].x_new.at(2, B - 1, 12))
            routing(logits3[:], E3, BLK3, NB3, MS3, 1, True)
            with dve.Fori(0, PASSES[3]) as i:
                for n in range(F3 // P // 2):
                    for s in range(MS3):
                        st = streams[s]
                        dve.wait_ge(st.f.sem, st.f.at(3, i, n + 1))
                        nc.vector.tensor_tensor(
                            hid3[s][:, 2 * n:2 * n + 2, :].rearrange("p a n -> p (a n)"), ps[2 * s + (n + 1) % 2][:, 1, :],
                            act3[s][:], ALU.mult).then_inc(st.fm.sem, 1)
                for s in range(MS3):
                    st = streams[s]
                    dve.wait_ge(st.y_ps.sem, st.y_ps.at(3, i, 1))
                    dve.wait_ge(st.y_out, 16 * i + 16 * PASSES[1])
                    nc.vector.tensor_copy(y3[s][:].rearrange("p a d -> p (a d)"), ps[2 * s + 1][:, 0, :])\
                        .then_inc(st.x_new.sem, 1)
            for n in range(2):
                dve.wait_ge(gathered3[n], 16 * NT)
                for tl in range(NT):
                    last = nc.vector.scalar_tensor_tensor(out=x_all[:, tl, :], in0=rows3[n][:, tl, :],
                                                          scalar=route[:, 2 + n, tl:tl + 1], in1=x_all[:, tl, :],
                                                          op0=ALU.mult, op1=ALU.add)
                if n == 0:
                    link(last)
            last.then_inc(combined, 1)

        @block.tensor
        def _(pe):
            mm = nc.tensor.matmul
            pe.sem_inc(prep_ps.sem, 1)
            def prep(b):
                pe.wait_ge(ctx_ready, b + 1)
                for s in range(STREAMS):
                    pe.wait_ge(streams[s].x_new.sem, streams[s].x_new.at(0, b, 0))
                for n, (w, arrived) in enumerate(((wk0, "k"), (wv0, "v"))):
                    pe.wait_ge(loaded[arrived], 32)
                    for c in range(C0):
                        for kc in range(KC):
                            last = mm(ps[n][:, c // 4, c % 4 * J:c % 4 * J + J], w[:, kc, c * P:c * P + P],
                                      ctx_b[:, kc, :], start=kc == 0, stop=kc == KC - 1)
                    last.then_inc((prep_ps.sem, v_ps)[n], 1)
                pe.wait_ge(loaded["qT"], 16)
                for n, (kc, half) in enumerate(((0, 0), (0, 1), (1, 0), (1, 1))):
                    pe.wait_ge(prep_sb.sem, prep_sb.at(0, b, 1))
                    if n == 3:
                        pe.wait_ge(vT_ready, b + 1)
                    pair = (2 + n) % 4
                    for par in range(2):
                        for c in range(4):
                            last = mm(ps[pair][:, par, c * J:c * J + J],
                                      wqT0[D0 * par:D0 * par + D0, 4 * half + c, kc * P:kc * P + P],
                                      kT0[D0 * par:D0 * par + D0, 4 * half + c, :], start=True, stop=True)
                    last.then_inc(prep_ps.sem, 1)
                pe.wait_ge(loaded["o"], 16)
                for n in range(3):
                    pe.wait_ge(prep_sb.sem, prep_sb.at(0, b, 2 + n))
                    pair = (2 + n) % 4
                    for k in range(4 * n, min(4 * n + 4, NCH)):
                        m = P if k < NCH - 1 else LAST_CH
                        cs = [c for c in range(C0) if c * 2 * J < k * P + P and (c + 1) * 2 * J > k * P]
                        for i, c in enumerate(cs):
                            at = c * 3 * P + k * P - window(c)
                            last = mm(ps[pair][0:m, k % 4 // 2, k % 2 * D:k % 2 * D + D], vT0[:, at:at + m],
                                      wo0[:, c, :], start=i == 0, stop=i == len(cs) - 1)
                    last.then_inc(prep_ps.sem, 1)
                pe.wait_ge(prep_sb.sem, prep_sb.at(0, b, 5))
                pe.wait_ge(rel_const, 1)
                for g in range(4):
                    for par in range(2):
                        last = mm(ps[1][:, g // 2, g % 2 * D:g % 2 * D + D], relv_m[:, par, :], wo0[:, 2 * g + par, :],
                                  start=par == 0, stop=par == 1)
                last.then_inc(prep_ps.sem, 1)
                pe.wait_ge(prep_sb.sem, prep_sb.at(0, b, 9))

            def xn_T(s, st_sem, value):
                st = streams[s]
                pe.wait_ge(st_sem, value)
                for c in range(KC):
                    last = nc.tensor.transpose(ps[s][:, 0, c * P:c * P + P], xn[s][:, c * P:c * P + P], ident[:])
                last.then_inc(st.xnT_ps.sem, 1)

            def xnT1(s, r):
                xn_T(s, streams[s].xn.sem, streams[s].xn.at(0, b, 2 * r + 1))

            def xnT2(s, r):
                xn_T(s, streams[s].xn.sem, streams[s].xn.at(0, b, 2 * r + 2))

            def rel_scores(s, r):
                if s or r:
                    return
                st = streams[0]
                pe.wait_ge(loaded["q"], 16)
                pe.wait_ge(st.xnT.sem, st.xnT.at(0, b, 1))
                for c in range(C0):
                    for kc in range(KC):
                        last = mm(ps[0][:, c // 4, c % 4 * P:c % 4 * P + P], wq0[:, kc, c * P:c * P + P],
                                  xnT[0][:, kc, :], start=kc == 0, stop=kc == KC - 1)
                last.then_inc(st.q_ps.sem, 1)
                for g in range(4):
                    pe.wait_ge(st.q.sem, st.q.at(0, b, 1 + g))
                    for par in range(2):
                        for c in range(2):
                            last = mm(ps[0][:, par, c * EXT:c * EXT + EXT],
                                      qT0[D0 * par:D0 * par + D0, 2 * g + c, :],
                                      relk_ext[D0 * par:D0 * par + D0, :], start=True, stop=True)
                    last.then_inc(st.q_ps.sem, 1)
                pe.wait_ge(st.q.sem, st.q.at(0, b, 5))

            def scores(s, r, half):
                st = streams[s]
                if half == 0:
                    pe.wait_ge(st.xnT.sem, st.xnT.at(0, b, 2 * r + 1))
                else:
                    pe.wait_ge(st.p_sub.sem, st.p_sub.at(0, b, 2 * r + 1))
                for a in range(2):
                    at = half * HALF + a * QUART
                    for kc in range(KC):
                        last = mm(ps[s][:, a, 0:QUART], xnT[s][:, kc, :], qk0[:, kc, at:at + QUART],
                                  start=kc == 0, stop=kc == KC - 1)
                last.then_inc(st.s_ps.sem, 1)

            def scores0(s, r):
                scores(s, r, 0)

            def scores1(s, r):
                scores(s, r, 1)

            def probs_T(s, phase, k, part):
                st = streams[s]
                if part == 1:
                    pe.wait_ge(st.pT.sem, st.pT.at(phase, b, k - 1))
                elif phase == 0:
                    pe.wait_ge(st.o.sem, st.o.at(0, b, k // 2 + 1))
                else:
                    pe.wait_ge(st.p_exp.sem, st.p_exp.at(2, b, k + 1))
                for i in range(5):
                    n = 5 * part + i
                    m = P if n < NCH - 1 else LAST_CH
                    last = nc.tensor.transpose(ps[s][0:m, i // 4, i % 4 * P:i % 4 * P + P],
                                               probs[s][:, n * P:n * P + m], ident[:])
                last.then_inc(st.pT_ps.sem, 1)

            def pT0(s, r):
                probs_T(s, 0, 2 * r + 1, 0)

            def pT1(s, r):
                probs_T(s, 0, 2 * r + 2, 1)

            def band_T(s, r):
                if s or r:
                    return
                st = streams[0]
                pe.wait_ge(st.pT.sem, st.pT.at(0, b, 2))
                pe.wait_ge(band_in, 16 * b + 16)
                pe.wait_ge(band_tail, b + 1)
                for g in range(4):
                    last = nc.tensor.transpose(ps[0][:, 0, g * P:g * P + P],
                                               band[:, 4 * g:4 * g + 4, :].rearrange("p h e -> p (h e)"), ident[:])
                last.then_inc(st.q_ps.sem, 1)

            def attn_out(s, r):
                st = streams[s]
                first = s == 0 and r == 0
                pe.wait_ge(st.pT.sem, st.pT.at(0, b, 2 * r + 2))
                if first:
                    pe.wait_ge(st.q.sem, st.q.at(0, b, 6))
                    pe.wait_ge(loaded["rest"], 16 * 5)
                y = ps[s][:, 0, 0:D]
                mm(y, ones[:], bo0[:], start=True, stop=False)
                if first:
                    for g in range(4):
                        mm(y, bandT[:, g, :], relvo[:, g, :], start=False, stop=False)
                for k in range(NCH):
                    m = P if k < NCH - 1 else LAST_CH
                    last = mm(y, probsT[s][0:m, k, :], vo0[0:m, k, :], start=False, stop=k == NCH - 1)
                last.then_inc(st.y_ps.sem, 1)

            def gate_up(s, phase, i, k_in, k, wg, wu):
                st = streams[s]
                pe.wait_ge(st.xnT.sem, st.xnT.at(phase, i, k_in))
                for a, w in enumerate((wg, wu)):
                    for f in range(FC0):
                        for kc in range(KC):
                            last = mm(ps[s][:, a, f * P:f * P + P], w[:, kc, f * P:f * P + P], xnT[s][:, kc, :],
                                      start=kc == 0, stop=kc == KC - 1)
                last.then_inc(st.f_ps.sem, 1)

            def ffn_down(s, phase, i, k, wd):
                st = streams[s]
                pe.wait_ge(st.fm.sem, st.fm.at(phase, i, k))
                for f in range(FC0):
                    last = mm(ps[s][:, 0, 0:D], hid[s][:, 1, f * P:f * P + P], wd[:, f, :], start=f == 0, stop=f == FC0 - 1)
                return last

            def shared_out(s, r):
                ffn_down(s, 0, b, r + 1, sdw)
                for kc in range(KC):
                    last = mm(ps[s][:, 1, 0:E0], xnT[s][:, kc, :], gate0[:, kc, :], start=kc == 0, stop=kc == KC - 1)
                last.then_inc(streams[s].y_ps.sem, 1)

            pe.wait_ge(consts, 5)
            with pe.Fori(0, B) as b:
                prep(b)
                for f, s, r in order(STEPS1, dict(engine=PE, apply1=xnT1, rel=rel_scores, half0=scores0, half1=scores1, pT0=pT0,
                                                  pT1=pT1, band=band_T, out1=attn_out, apply2=xnT2,
                                                  gate_up=lambda s, r: gate_up(s, 0, b, 2 * r + 2, r + 1, sgw, suw),
                                                  out2=shared_out)):
                    f(s, r)

            def ranks(n_exp, ready):
                pe.wait_ge(one_hot_ready, ready)
                hot = one_hot[:, 0:NT * n_exp].rearrange("p (n e) -> p n e", e=n_exp)
                rank = ps[0][:, 0, 0:NT * n_exp].rearrange("p (n e) -> p n e", e=n_exp)
                mm(rank, squareb[:], hot, start=True, stop=True, skip_group_check=True)
                for n in range(NT - 1):
                    mm(rank[:, n + 1:NT, :], onesb[:], hot[:, n:n + 1, :].to_broadcast([P, NT - 1 - n, n_exp]),
                       start=False, stop=True, skip_group_check=True)
                for n in range(NT):
                    last = mm(ps[1][:, 0, 0:n_exp], onesb[:], hot[:, n, :], start=n == 0, stop=n == NT - 1)
                last.then_inc(rank_ready, 1)

            ranks(E0, 1)
            pe.wait_ge(routed, 1)
            with pe.Fori(0, PASSES[1]) as i:
                for s in range(STREAMS):
                    st = streams[s]
                    pe.wait_ge(st.x_new.sem, st.x_new.at(1, i, 0))
                    xn_T(s, st.rows_loaded, 16 * i + 16)
                for s in range(STREAMS):
                    st = streams[s]
                    pe.wait_ge(st.in_loaded, 16 * i + 16)
                    gate_up(s, 1, i, 1, 1, w_in0[s][:, 0], w_in0[s][:, 1])
                for s in range(STREAMS):
                    pe.wait_ge(streams[s].out_loaded, 16 * i + 16)
                    ffn_down(s, 1, i, 1, w_out0[s]).then_inc(streams[s].y_ps.sem, 1)

            pe.wait_ge(rhs_ready, 1)
            for s in range(STREAMS):
                pe.wait_ge(streams[s].x_new.sem, streams[s].x_new.at(2, 0, 0))
            qps = ps[0][:, 0, 0:D].bitcast(BF16).rearrange("p (c n) -> p c n", c=KC)
            for kc in range(KC):
                for c in range(KC):
                    nc.tensor.transpose(qps[:, kc, c * P:c * P + P], rhs_q[:, c, kc * P:kc * P + P], identb[:])
            for c in range(KC):
                last = mm(ps[0][:, 1, c * P:c * P + P], onesq[:], diag[:, c, :], start=True, stop=True)
            last.then_inc(rhs_ps, 1)
            pe.wait_ge(rhs_sb, 1)

            def prep2(b):
                for s in range(STREAMS):
                    pe.wait_ge(streams[s].x_new.sem, streams[s].x_new.at(2, b, 0))
                pe.wait_ge(rep_ready, b + 1)
                for l in LAYERS:
                    for c in range(KC):
                        for kc in range(KC):
                            mm(ps[l - 1][:, 0, c * J:c * J + J], w2["wk", l][:, kc, c * P:c * P + P], ctx_b[:, kc, :],
                               start=kc == 0, stop=kc == KC - 1)
                    for k in range(NCH):
                        v = ps[l - 1][:, 1, k * SLOTS * ATT:(k + 1) * SLOTS * ATT]
                        at = FIRST[k] * ATT
                        if l < 3:
                            mm(v, ones[:], bv2[l][:, at:at + SLOTS * ATT], start=True, stop=False)
                        for kc in range(KC):
                            last = mm(v, ctx_rep[:, kc, k * P:k * P + P], w2["wv", l][:, kc, at:at + SLOTS * ATT],
                                      start=kc == 0 and l == 3, stop=kc == KC - 1)
                    last.then_inc(prep_ps.sem, 1)
                pe.wait_ge(prep_sb.sem, prep_sb.at(2, b, 3))

            def apply_T(k):
                def step(s, r):
                    xn_T(s, streams[s].xn.sem, streams[s].xn.at(2, b, 6 * r + k))
                return step

            def q_proj(l):
                def step(s, r):
                    st = streams[s]
                    pe.wait_ge(st.xnT.sem, st.xnT.at(2, b, 5 * r + {1: 1, 2: 3, 3: 4}[l]))
                    for c in range(KC):
                        for kc in range(KC):
                            last = mm(ps[s][:, 0, c * P:c * P + P], w2["wq", l][:, kc, c * P:c * P + P],
                                      xnT[s][:, kc, :], start=kc == 0, stop=kc == KC - 1)
                    last.then_inc(st.q_ps.sem, 1)
                return step

            def half_scores(l, half):
                def step(s, r):
                    st = streams[s]
                    if half == 0:
                        pe.wait_ge(st.q.sem, st.q.at(2, b, 3 * r + l))
                    else:
                        pe.wait_ge(st.p_sub.sem, st.p_sub.at(2, b, 6 * r + 2 * l - 1))
                    for a in range(2):
                        last = mm(ps[s][:, a, 0:QUART], qT[s][D0 * a:D0 * a + D0, half, :],
                                  k_bd[l][D0 * a:D0 * a + D0, half, :], start=True, stop=True)
                    last.then_inc(st.s_ps.sem, 1)
                return step

            def values(l):
                def step(s, r):
                    st = streams[s]
                    pe.wait_ge(st.pT.sem, st.pT.at(2, b, 6 * r + 2 * l))
                    for k in range(NCH):
                        m = P if k < NCH - 1 else LAST_CH
                        last = mm(ps[s][:, 0, FIRST[k] * VW:(FIRST[k] + SLOTS) * VW], probsT[s][0:m, k, :],
                                  v_bd[l][0:m, k, :], start=k == 0, stop=True, skip_group_check=True)
                    last.then_inc(st.o_ps.sem, 1)
                return step

            def out_T(l):
                def step(s, r):
                    st = streams[s]
                    pe.wait_ge(st.o.sem, st.o.at(2, b, 3 * r + l))
                    for c in range(KC):
                        last = nc.tensor.transpose(ps[s][:, 1, c * P:c * P + P], xn[s][:, c * P:c * P + P], ident[:])
                    last.then_inc(st.oT_ps.sem, 1)
                return step

            def out_proj(l):
                def step(s, r):
                    st = streams[s]
                    pe.wait_ge(st.oT.sem, st.oT.at(2, b, 3 * r + l))
                    if l < 3:
                        mm(ps[s][:, 0, 0:D], ones[:], bo2[l][:], start=True, stop=False)
                    for c in range(KC):
                        last = mm(ps[s][:, 0, 0:D], xnT[s][:, c, :], w2["wo", l][:, c, :],
                                  start=c == 0 and l == 3, stop=c == KC - 1)
                    last.then_inc(st.y_ps.sem, 1)
                return step

            def low(s, r):
                st = streams[s]
                pe.wait_ge(st.xnT.sem, st.xnT.at(2, b, 5 * r + 2))
                for kc in range(KC):
                    last = mm(ps[s][0:LOW, 0, 0:P], u1[:, kc, :], xnT[s][:, kc, :], start=kc == 0, stop=kc == KC - 1)
                last.then_inc(st.f_ps.sem, 1)

            def up(s, r):
                st = streams[s]
                pe.wait_ge(st.f.sem, st.f.at(2, b, 4 * r + 1))
                for f in range(F1 // P):
                    last = mm(ps[s][:, f // 4, f % 4 * P:f % 4 * P + P], v1[:, f * P:f * P + P], low_T[s][0:LOW + 1, :],
                              start=True, stop=True)
                last.then_inc(st.f_ps.sem, 1)

            def low2(s, r):
                st = streams[s]
                pe.wait_ge(st.f.sem, st.f.at(2, b, 4 * r + 2))
                for f in range(F1 // P):
                    last = mm(ps[s][0:LOW, 0, 0:P], u2[:, f, :], probs[s][:, f * P:f * P + P],
                              start=f == 0, stop=f == F1 // P - 1)
                last.then_inc(st.f_ps.sem, 1)

            def low_out(s, r):
                st = streams[s]
                pe.wait_ge(st.f.sem, st.f.at(2, b, 4 * r + 3))
                mm(ps[s][:, 0, 0:D], low_T[s][0:LOW + 1, :], v2[:], start=True, stop=True).then_inc(st.y_ps.sem, 1)

            def quant_T(s, r):
                st = streams[s]
                pe.wait_ge(st.fm.sem, st.fm.at(2, b, r + 1))
                for c in range(KC):
                    last = nc.tensor.transpose(ps[s][:, 0, 0:P].bitcast(BF16)[:, c * P:c * P + P],
                                               x_q[s][:, c * P:c * P + P], identb[:])
                last.then_inc(st.f_ps.sem, 1)

            def quant_out(s, r):
                st = streams[s]
                pe.wait_ge(st.f.sem, st.f.at(2, b, 4 * r + 4))
                for kc in range(KC):
                    last = mm(ps[s][:, 0, 0:D], x_qT[s][:, kc * P:kc * P + P], rhs_qT[:, kc, :],
                              start=kc == 0, stop=kc == KC - 1)
                last.then_inc(st.y_ps.sem, 1)

            def gate(s, r):
                st = streams[s]
                pe.wait_ge(st.xnT.sem, st.xnT.at(2, b, 5 * r + 5))
                for kc in range(KC):
                    last = mm(ps[s][:, 0, 0:E3], xnT[s][:, kc, :], gate3[:, kc, :], start=kc == 0, stop=kc == KC - 1)
                last.then_inc(st.y_ps.sem, 1)

            own = {"engine": PE}
            for l in LAYERS:
                own |= {f"apply{l}": apply_T(2 * l - 1), f"q{l}": q_proj(l), f"av{l}": values(l), f"oT{l}": out_T(l),
                        f"out{l}": out_proj(l)}
                own |= {f"half{h}_{l}": half_scores(l, h) for h in range(2)}
                own |= {f"pT{h}_{l}": (lambda s, r, l=l, h=h: probs_T(s, 2, 6 * r + 2 * l - 1 + h, h)) for h in range(2)}
            own |= dict(fapply1=apply_T(2), fapply3=apply_T(6), low1=low, gelu1=up, low21=low2, fout1=low_out,
                        quant2=quant_T, fout2=quant_out, gate3=gate)
            with pe.Fori(0, B) as b:
                prep2(b)
                for f, s, r in order(STEPS2, own):
                    f(s, r)

            ranks(E3, 2)
            pe.wait_ge(routed, 2)
            with pe.Fori(0, PASSES[3]) as i:
                for s in range(MS3):
                    st = streams[s]
                    pe.wait_ge(st.x_new.sem, st.x_new.at(3, i, 0))
                    pe.wait_ge(st.rows_loaded, 16 * i + 16 * (PASSES[1] + 1))
                    for a in range(2):
                        for c in range(KC):
                            last = nc.tensor.transpose(ps[2 * s][:, 0, (2 * c + a) * P:(2 * c + a + 1) * P],
                                                       x_in[s][:, a, c * P:c * P + P], ident[:])
                    last.then_inc(st.xnT_ps.sem, 1)
                for n in range(F3 // P // 2):
                    for s in range(MS3):
                        st = streams[s]
                        if n == 0:
                            pe.wait_ge(st.in_loaded, 16 * i + 16 * (PASSES[1] + 1))
                            pe.wait_ge(st.xnT.sem, st.xnT.at(3, i, 1))
                        elif n >= 2:
                            pe.wait_ge(st.fm.sem, st.fm.at(3, i, n - 1))
                        for a in range(2):
                            for f in range(2):
                                for kc in range(KC):
                                    at = (2 * n + f) * P
                                    last = mm(ps[2 * s + (n + 1) % 2][:, a, f * BLK3:(f + 1) * BLK3], w_in3[s][:, a, kc, at:at + P],
                                              x_inT[s][:, kc, :], start=kc == 0, stop=kc == KC - 1)
                        last.then_inc(st.f_ps.sem, 1)
                for s in range(MS3):
                    st = streams[s]
                    pe.wait_ge(st.fm.sem, st.fm.at(3, i, 4))
                    pe.wait_ge(st.out_loaded, 16 * i + 16 * (PASSES[1] + 1))
                    for a in range(2):
                        for f in range(F3 // P):
                            last = mm(ps[2 * s + 1][:, 0, a * D:a * D + D], hid3[s][:, f, a * P:a * P + P],
                                      w_out3[s][:, f, :], start=f == 0, stop=f == F3 // P - 1)
                    last.then_inc(st.y_ps.sem, 1)


def kernel(**inputs):
    import concourse.bacc as bacc
    from concourse.bass_utils import run_bass_kernel_spmd

    a = {k: np.asarray(v) for k, v in inputs.items()}

    def rows_of(*ws):
        e, cp, n = ws[0].shape
        return np.stack(ws, 1).reshape(e, len(ws), cp // P, P, n).transpose(0, 3, 1, 2, 4).reshape(e * P, -1)

    relk, relv = a["L0_xattn_rel_k"], a["L0_xattn_rel_v"]
    dist = np.clip(np.arange(EXT) - (P - 1), -MAXREL, MAXREL) + MAXREL
    arrays = {
        "x": a["x"],
        "ctxT": a["ctx_1024"].transpose(2, 0, 1),
        "Wq0": a["L0_xattn_Wq"], "WqT0": a["L0_xattn_Wq"].T, "Wk0": a["L0_xattn_Wk"], "Wv0": a["L0_xattn_Wv"],
        "Wo0": a["L0_xattn_Wo"], "bo0": a["L0_xattn_bo"][None],
        "relk_ext": np.concatenate([relk[dist].T] * 2), "relk_0": np.concatenate([relk[0]] * 2)[:, None],
        "relv_T": np.concatenate([relv[1:].T] * 2), "relv_0": np.concatenate([relv[0]] * 2)[:, None],
        "sgw": a["L0_ffn_shared_gate_w"], "suw": a["L0_ffn_shared_up_w"], "sdw": a["L0_ffn_shared_down_w"],
        "gate0": a["L0_ffn_gate_w"],
        "w_in0": rows_of(a["L0_ffn_routed_gate_w"], a["L0_ffn_routed_up_w"]), "w_out0": rows_of(a["L0_ffn_routed_down_w"]),
        "w_in3": rows_of(a["L3_ffn_w1"].transpose(0, 2, 1), a["L3_ffn_w3"].transpose(0, 2, 1)),
        "w_out3": rows_of(a["L3_ffn_w2"].transpose(0, 2, 1)), "gate3": a["L3_ffn_gate_w"].T,
        "u1": a["L1_ffn_U1"], "u2": a["L1_ffn_U2"],
        "v1": np.concatenate([a["L1_ffn_V1"], a["L1_ffn_b1"][None]]),
        "v2": np.concatenate([a["L1_ffn_V2"], a["L1_ffn_b2"][None]]),
        "rhsT": a["L2_ffn_rhs"].T,
        "mask": np.ascontiguousarray(a["mask_BxSxS2_bk0"].reshape(NT, P, J).transpose(1, 0, 2)).reshape(P, NT * J)
        .view(np.int32),
    }
    for l in (1, 2):
        arrays |= {f"w{n.lower()}{l}": a[f"L{l}_xattn_W{n}"].T for n in "qkvo"}
        arrays |= {f"b{n}{l}": a[f"L{l}_xattn_b{n}"].reshape(KC, P).T for n in "qk"}
        arrays |= {f"b{n}{l}": a[f"L{l}_xattn_b{n}"][None] for n in "vo"}
    arrays |= {f"w{n}3": a[f"L3_xattn_w_{n}"].T for n in "qkvo"}
    p = np.arange(P)
    arrays["head_mask"] = (p[:, None] % D0 // ATT == np.arange(4)).astype(np.float32)
    arrays["slot_mask"] = ((P * np.arange(NCH)[:, None] + p[:, None, None]) // J
                           == np.array(FIRST)[:, None] + np.arange(SLOTS)).astype(np.float32)
    arrays["rev"] = np.broadcast_to(np.arange(E0, 0, -1, dtype=np.float32), (P, E0))
    arrays["kstep"] = np.broadcast_to(np.outer((BLK0, BLK3), np.arange(16)).astype(np.float32), (P, 2, 16))
    arrays["blks"] = np.broadcast_to(np.arange(NB0, dtype=np.float32), (P, NB0))
    arrays["row"] = p[:, None].astype(np.float32)
    arrays["low_tri"] = np.broadcast_to(np.tri(E0, dtype=np.float32), (P, E0, E0))
    arrays = {k: np.ascontiguousarray(v) for k, v in arrays.items()}
    nc = bacc.Bacc("TRN2", target_bir_lowering=False, num_devices=1)
    tensors = {k: nc.dram_tensor(k, v.shape, mybir.dt.from_np(v.dtype), kind="ExternalInput").ap()
               for k, v in arrays.items()}
    out = nc.dram_tensor("out", (B, T, D), F32, kind="ExternalOutput")
    build(nc, tensors, out.ap())
    r = run_bass_kernel_spmd(nc, [arrays], core_ids=[0])
    return r.results[0]["out"]
```

```python
import numpy as np
import concourse.bass as bass
from concourse import mybir
from contextlib import ExitStack

P = 128
B, T, D = 2, 1024, 256
J = 77
H = 16
KC = D // P
D0 = 64
INNER = H * D0
C0 = INNER // P
MAXREL = 16
TILES = T // P
STREAMS = 4
ROUNDS = TILES // STREAMS
HJ = H * J
HALF = HJ // 2
QUART = HALF // 2
NCH = -(-HJ // P)
LAST_CH = HJ - P * (NCH - 1)
EXT = P + J - 1
BAND = 2 * MAXREL - 1
PADW = (MAXREL - 1) + J + (P + MAXREL - 1 - J)
NREL = BAND + 1
F0 = 512
FC0 = F0 // P
E0 = 32
EPS = 1e-5
F32 = mybir.dt.float32
BF16 = mybir.dt.bfloat16
I32 = mybir.dt.int32
U32 = mybir.dt.uint32
U8 = mybir.dt.uint8
ALU = mybir.AluOpType
ACT = mybir.ActivationFunctionType
X = mybir.AxisListType.X
STEPS1 = ("stats1", "apply1", "rel", "half0", "half1", "norm", "pT0", "pT1", "band", "out1",
          "stats2", "apply2", "gate_up", "out2")
LAYERS = (1, 2, 3)
STEPS2 = tuple(f"{step}{l}" for l in LAYERS for step in
               ("stats", "apply", "q", "half0_", "half1_", "pT0_", "pT1_", "av", "oT", "out", "fstats", "fapply")
               + (("low", "gelu", "low2", "fout"), ("quant", "fout"), ("gate",))[l - 1])

PE, AC, DV, PO = "pe", "act", "dve", "pool"
STAGES = dict(
    stats=((DV, 0.65), (PO, 0.35)), apply=((DV, 0.35), (PE, 0.25), (AC, 0.3)),
    apply2=((DV, 0.35), (PO, 0, 0.1), (PE, 0.25), (AC, 0.3)), fapply3=((DV, 0.35), (PO, 0, 0.1), (PE, 0.25), (AC, 0.3)),
    q=((PE, 0.9), (PO, 0, 0.1), (AC, 0.4)), q3=((PE, 0.9), (PO, 0, 1.5), (AC, 0.3)),
    half0=((PE, 0.6, 1.1), (DV, 0.9, 1.8)), half1=((PE, 0.6, 1.1), (AC, 0, 0.65, "half0"), (DV, 1.8), (AC, 0.65)),
    pT0=((PE, 0.45, 0.9), (AC, 0.5, 1.0)), pT1=((PE, 0.2), (AC, 0.35)), av=((PE, 2.2), (DV, 0.65)),
    oT=((PE, 0.25), (AC, 0.3)), out=((PE, 1.3), (DV, 0.35)), low=((PE, 0.9), (AC, 0.2)),
    gelu=((PE, 1.8), (AC, 0.95)), down=((PE, 1.8), (AC, 0.2)), fout=((PE, 0.5), (DV, 0.35)),
    quant=((DV, 1.9), (PE, 0.15), (AC, 0.3)), gate=((PE, 0.4), (DV, 0.2)),
    wide_half0=((PE, 1.1, 2.2), (DV, 0.9, 1.8)), norm=((DV, 2.9),),
    wide_half1=((PE, 1.1, 2.2), (AC, 0, 0.65, "half0"), (DV, 1.8), (AC, 0.65)),
    out1=((PE, 4.9), (DV, 0.35)), gate_up=((PE, 3.5), (AC, 0.5), (DV, 1.3)), out2=((PE, 2.2), (DV, 0.5)),
    rel=((PE, 0, 6.0), (AC, 6.0)), band=((PE, 1.0), (AC, 0.6)))
TABLE = dict(half0="exp", half1="exp", gelu="gelu")
TABLE_LOAD = 0.0
KIND1 = dict(stats1="stats", apply1="apply", half0="wide_half0", half1="wide_half1", stats2="stats")
KIND2 = dict(fstats="stats", fapply="apply", half0_="half0", half1_="half1", pT0_="pT0", pT1_="pT1", low2="down")
HOP, WEIGHT = 0.3, 0.0


def plan(steps):
    chains = []
    for s in range(STREAMS):
        chain = []
        for r in range(ROUNDS):
            for step in steps:
                if step in ("rel", "band") and (s or r):
                    continue
                kind = KIND1.get(step, step) if steps is STEPS1 else (
                    step if step in STAGES else KIND2.get(step[:-1], step[:-1]))
                for stage in STAGES[kind]:
                    engine, time, held, of = (*stage, stage[1], None)[:4] if len(stage) == 2 else (*stage, None)[:4]
                    chain.append((engine, step.replace("half1", of) if of else step, s, r, time, held))
        chains.append(chain)
    free, ready, at = dict.fromkeys((PE, AC, DV, PO), 0.0), [0.0] * STREAMS, [0] * STREAMS
    found, table = [], "exp"
    while any(a < len(c) for a, c in zip(at, chains)):
        options = []
        for s in range(STREAMS):
            if at[s] < len(chains[s]):
                engine, step = chains[s][at[s]][:2]
                needs = TABLE.get(step.rstrip("123").rstrip("_"), table) if engine == AC else table
                options.append((max(free[engine], ready[s]) + TABLE_LOAD * (needs != table) + WEIGHT * at[s] / len(chains[s]), ready[s], s, needs))
        _, _, s, table = min(options)
        engine, step, _, r, time, held = chains[s][at[s]]
        start = max(free[engine], ready[s])
        free[engine] = start + held
        ready[s] = start + time + (HOP if time else 0)
        at[s] += 1
        found.append((engine, step, s, r))
    return found


POOL_LINKS1, POOL_LINKS2 = 16, 48
DVE_LINKS1, DVE_LINKS2 = 78, 256

ATT = 16
SLOTS = 3
VW = ATT + 1
FIRST = [min(P * k // J, H - SLOTS) for k in range(NCH)]
REPS = -(-P * NCH // J)
LOW, F1 = 64, 1024
F3 = 1024
E3 = 8
JITTER = 0.01
NEVER, MASKED = -3.0e38, -1.0e9
MAGIC = 1.5 * 2.0 ** 23
QMAX = 127.0
BLK = P
NB0 = B * T // BLK + E0
NB3 = 2 * B * T // BLK + E3
MS3 = 2
GROUPS = 4
PASSES = (B, NB0 // STREAMS, B, NB3 // MS3)
ROWS = max(NB0, NB3) * BLK
NT = B * TILES
PLAN = {steps: plan(steps) for steps in (STEPS1, STEPS2)}


def window(c):
    return 2 * J * c // P * P


class Count:

    def __init__(self, sem, per_pass, start=0):
        self.sem, self.per_pass = sem, per_pass
        self.base = [start + sum(m * n for m, n in zip(PASSES[:i], per_pass)) for i in range(len(per_pass))]

    def at(self, phase, i, k):
        return i * self.per_pass[phase] + (self.base[phase] + k)


class Links:

    def __init__(self, eng, sem):
        self.eng, self.sem, self.done, self.n, self.i, self.per_pass = eng, sem, 0, 0, 0, 0

    def enter(self, i, per_pass):
        self.done, self.n, self.i, self.per_pass = self.done + self.n, 0, i, per_pass

    def leave(self, passes):
        assert self.n == self.per_pass, ("links in a pass:", self.n)
        self.done, self.n, self.i, self.per_pass = self.done + passes * self.n, 0, 0, 0

    def __call__(self, ins):
        self.n += 1
        ins.then_inc(self.sem, 1)
        self.eng.wait_ge(self.sem, self.i * self.per_pass + (self.done + self.n))


def build(nc, t, out):
    ctx = ExitStack()
    with ctx:
        offset = [nc.sbuf_base + 31 & ~31]

        def sb(name, shape, dt=F32, at=None):
            size = int(np.prod(shape[1:])) * mybir.dt.size(dt)
            size = size + 31 & ~31
            if at is None:
                at = offset[0]
                offset[0] += size
                assert offset[0] <= nc.sbuf_usable_end, (name, offset[0])
            return nc.alloc_sbuf_tensor_at(name, shape, dt, offset=at), at + size

        def keep(name, shape, dt=F32):
            return sb(name, shape, dt)[0]

        def sem(name):
            return ctx.enter_context(nc.semaphore(name))

        x_all = keep("x_all", [P, B * TILES, D])
        ident = keep("ident", [P, P])
        ones = keep("ones", [1, P])
        minus_half = keep("minus_half", [P, 1])
        ctx_all = keep("ctx_all", [P, KC, B, J])
        ctx_b = keep("ctx_b", [P, KC, J])
        logits0 = keep("logits0", [P, B * TILES, E0])
        stats = [keep(f"stats{s}", [P, 6]) for s in range(STREAMS)]
        mean_var = [keep(f"mean_var{s}", [P, 2]) for s in range(STREAMS)]
        rstd = [keep(f"rstd{s}", [P, 2]) for s in range(STREAMS)]
        xn = [keep(f"xn{s}", [P, D]) for s in range(STREAMS)]
        xnT = [keep(f"xnT{s}", [P, KC, P]) for s in range(STREAMS)]
        probs = [keep(f"probs{s}", [P, HJ]) for s in range(STREAMS)]
        probsT = [keep(f"probsT{s}", [P, NCH, P]) for s in range(STREAMS)]
        mx = [keep(f"mx{s}", [P, H]) for s in range(STREAMS)]
        qT = [keep(f"qT{s}", [P, KC, P]) for s in range(STREAMS)]
        low_T = [keep(f"low_T{s}", [P, P]) for s in range(STREAMS)]
        filled_mask = [keep(f"filled_mask{s}", [P, J], U8) for s in range(STREAMS)]
        scale = [keep(f"scale{s}", [P, 2]) for s in range(STREAMS)]
        identb, squareb, onesb = (keep(n, [P, P], BF16) for n in ("identb", "squareb", "onesb"))
        onesq = keep("onesq", [P, P])
        causal_f, causal = keep("causal_f", [P, J]), keep("causal", [P, J], U8)
        logits3 = keep("logits3", [P, NT, E3])
        rev, kstep = keep("rev", [P, E0]), keep("kstep", [P, B * T // BLK])
        blks, row = keep("blks", [P, NB0]), keep("row", [P, 1])
        low_tri = keep("low_tri", [P, E0, E0])
        one_hot = keep("one_hot", [P, NT * E0], BF16)
        route = keep("route", [P, 8, NT])
        blocks_of = keep("blocks_of", [P, 4, E0])
        slot = keep("slot", [P, 2, NT], I32)
        zeros = keep("zeros", [P, D])
        expert = keep("expert", [P, NB0])
        load_f, load = keep("load_f", [P, NB0]), keep("load", [P, NB0], U32)
        load_now = keep("load_now", [P, 2, STREAMS], U32)
        phase_start = offset[0]

        wq0 = keep("wq0", [P, KC, INNER])
        wqT0 = keep("wqT0", [P, C0, D])
        wk0 = keep("wk0", [P, KC, INNER])
        wv0 = keep("wv0", [P, KC, INNER])
        wo0 = keep("wo0", [P, C0, D])
        bo0 = keep("bo0", [1, D])
        kT0 = keep("kT0", [P, C0, J])
        qk0 = keep("qk0", [P, KC, HJ])
        vT0 = keep("vT0", [P, C0 * 3 * P + 104])
        vo0 = keep("vo0", [P, NCH, D])
        diag_f = keep("diag_f", [P, P])
        relk_ext = keep("relk_ext", [P, EXT])
        relk_0 = keep("relk_0", [P, 1])
        relv_0 = keep("relv_0", [P, 1])
        relv_T = keep("relv_T", [P, NREL])
        relv_m = keep("relv_m", [P, 2, P])
        relvo = keep("relvo", [P, H // 4, D])
        tail_mask = keep("tail_mask", [P, J])
        rel_q = keep("rel_q", [P, H, EXT])
        band_src = rel_q[:].rearrange("p h e -> p (h e)")[:, 0:H * PADW].rearrange("p (h e) -> p h e", h=H)
        rel_s = keep("rel_s", [P, HJ])
        band = keep("band", [P, H, NREL])
        bandT = keep("bandT", [P, 4, P])
        qT0 = probsT[0][:, 0:C0, :]
        sgw = keep("sgw", [P, KC, F0])
        suw = keep("suw", [P, KC, F0])
        sdw = keep("sdw", [P, FC0, D])
        gate0 = keep("gate0", [P, KC, E0])
        hid = [probs[s][:, 0:2 * F0].rearrange("p (a f) -> p a f", a=2) for s in range(STREAMS)]

        offset[0] = phase_start
        ctx_rep = keep("ctx_rep", [P, KC, B, REPS * J])
        k_all = keep("k_all", [P, B, KC, len(LAYERS), J])
        w2 = {(n, l): keep(f"{n}_{l}", [P, KC, D]) for l in LAYERS for n in ("wq", "wk", "wo")}
        wv2 = keep("wv2", [P, KC, len(LAYERS), D])
        bq2 = {l: keep(f"bq_{l}", [P, KC]) for l in (1, 2)}
        bk2 = {l: keep(f"bk_{l}", [P, KC]) for l in (1, 2)}
        bv2 = keep("bv2", [1, 2, D])
        bo2 = {l: keep(f"bo_{l}", [1, D]) for l in (1, 2)}
        head_mask, slot_mask = keep("head_mask", [P, 4]), keep("slot_mask", [P, NCH, len(LAYERS), SLOTS])
        u1, v1 = keep("u1", [P, KC, LOW]), keep("v1", [LOW + 1, F1])
        u2, v2 = keep("u2", [P, F1 // P, LOW]), keep("v2", [LOW + 1, D])
        rhs_T, rhs_q = keep("rhs_T", [P, KC, D]), keep("rhs_q", [P, KC, D], BF16)
        rhs_qT = keep("rhs_qT", [P, KC, D], BF16)
        rhs_scale, rhs_scale_row = keep("rhs_scale", [P, 2 * KC]), keep("rhs_scale_row", [P, D])
        diag = keep("diag", [P, KC, P])
        x_q = [keep(f"x_q{s}", [P, D], BF16) for s in range(STREAMS)]
        x_qT = [keep(f"x_qT{s}", [P, D], BF16) for s in range(STREAMS)]
        mask_in, unmasked = keep("mask_in", [P, NT * J // 4], I32), keep("unmasked", [P, NT, J], U8)
        gate3 = keep("gate3", [P, KC, E3])
        moe_start = offset[0]
        k_bd = keep("k_bd", [P, len(LAYERS), KC, 4 * J])
        v_bd = keep("v_bd", [P, B, NCH, len(LAYERS), SLOTS * VW])
        offset[0] = moe_start
        w_in0 = [keep(f"w_in0{s}", [P, 2, KC, F0]) for s in range(STREAMS)]
        w_out0 = [keep(f"w_out0{s}", [P, FC0, D]) for s in range(STREAMS)]
        y_sb = [qT[s][:].rearrange("p c n -> p (c n)") for s in range(STREAMS)]
        rows0 = [probsT[n // 4][:].rearrange("p c n -> p (c n)")[:, n % 4 * D:(n % 4 + 1) * D] for n in range(NT)]
        offset[0] = moe_start
        w_in3 = [keep(f"w_in3{s}", [P, 2, KC, F3]) for s in range(MS3)]
        w_out3 = [keep(f"w_out3{s}", [P, F3 // P, D]) for s in range(MS3)]
        offset[0] = phase_start
        rows3 = [keep(f"rows3{n}", [P, NT, D]) for n in range(2)]
        x_in = [keep(f"x_in{s}", [P, D]) for s in range(MS3)]
        x_inT = [keep(f"x_inT{s}", [P, KC, BLK]) for s in range(MS3)]
        act3 = [keep(f"act3{s}", [P, 4 * BLK]) for s in range(MS3)]
        hid3 = [keep(f"hid3{s}", [P, F3 // P, BLK]) for s in range(MS3)]
        y3 = [keep(f"y3{s}", [P, D]) for s in range(MS3)]
        assert offset[0] <= moe_start, (offset[0], moe_start)

        sorted_dram = nc.dram_tensor("sorted_dram", [ROWS, D], F32)
        y_dram = nc.dram_tensor("y_dram", [ROWS, D], F32)
        xn3_dram = nc.dram_tensor("xn3_dram", [B * T, D], F32)
        rel_dram = nc.dram_tensor("rel_dram", [P * H * EXT + P], F32)
        band_dram = nc.dram_tensor("band_dram", [P * H * PADW + P], F32)
        xn0_dram = nc.dram_tensor("xn0_dram", [B * T, D], F32)

        ps = [ctx.enter_context(nc.psum_tensor(f"ps{s}", [P, 2, 512], F32)) for s in range(STREAMS)]

        class Stream:
            def __init__(self, s):
                def count(name, *per_pass, start=0):
                    return Count(sem(f"{name}{s}"), per_pass, start)

                first = s == 0
                self.aggr, self.rstd = count("aggr", 4, 0, 12, 0), count("rstd", 4, 0, 12, 0)
                self.xn, self.xn_stored = count("xn", 4, 0, 12, 0), sem(f"xn_stored{s}")
                self.xnT_ps, self.xnT = count("xnT_ps", 4, 1, 10, 1), count("xnT", 4, 1, 10, 1)
                self.q_ps = count("q_ps", 6 * first, 0, 6, 0)
                self.q = count("q", 6 * first, 0, 6, 0)
                self.s_ps, self.filled = count("s_ps", 8, 0, 24, 0), count("filled", 0, 0, 2 + 2 * first, 0)
                self.p_sub, self.p_exp = count("p_sub", 8, 0, 24, 0), count("p_exp", 4, 0, 12, 0)
                self.pT_ps, self.pT = count("pT_ps", 6, 0, 18, 0), count("pT", 6, 0, 18, 0)
                self.o_ps, self.o = count("o_ps", 0, 0, 6, 0), count("o", 2, 0, 6, 0)
                self.oT_ps, self.oT = count("oT_ps", 0, 0, 6, 0), count("oT", 0, 0, 6, 0)
                self.f_ps, self.f, self.fm = count("f_ps", 2, 1, 8, 2), count("f", 2, 1, 8, 2), count("fm", 2, 1, 2, 2)
                self.y_ps, self.x_new = count("y_ps", 4, 1, 12, 1), count("x_new", 4, 1, 12, 1, start=1)
                self.in_loaded, self.out_loaded, self.rows_loaded, self.y_out = (
                    sem(f"{name}{s}") for name in ("in_loaded", "out_loaded", "rows_loaded", "y_out"))

        streams = [Stream(s) for s in range(STREAMS)]
        loaded = {n: sem(f"loaded_{n}") for n in ("x0", "x1", "ctx", "k", "v", "qT", "o", "rel", "rest",
                                                 "shape", "p2", "xn")}
        rhs_ps, rhs_sb = sem("rhs_ps"), sem("rhs_sb")
        top_ready, score_exp = sem("top_ready"), sem("score_exp")
        one_hot_ready, rank_ready, routed, scaled = sem("one_hot_ready"), sem("rank_ready"), sem("routed"), sem("scaled")
        zero_out, combined = sem("zero_out"), sem("combined")
        loads_ready = sem("loads_ready")
        kv_ps, kv_sb, k_built = sem("kv_ps"), sem("kv_sb"), sem("k_built")
        scattered, gathered, rep_ready = sem("scattered"), sem("gathered"), sem("rep_ready")
        gathered3 = [sem(f"gathered3_{n}") for n in range(GROUPS)]
        consts, CONSTS = sem("consts"), 9 + STREAMS
        ctx_ready = sem("ctx_ready")
        prep_ps = Count(sem("prep_ps"), (9, 0, 0, 0), start=1)
        prep_sb = Count(sem("prep_sb"), (9, 0, 0, 0))
        v_ps, vT_ready = sem("v_ps"), sem("vT_ready")
        rel_const = sem("rel_const")
        rel_out, rel_in = sem("rel_out"), sem("rel_in")
        band_ready, band_out, band_in = sem("band_ready"), sem("band_out"), sem("band_in")
        band_tail = sem("band_tail")
        dve_link, pool_link = sem("dve_link"), sem("pool_link")
        stored = sem("stored")
        block = ctx.enter_context(nc.Block())

        def order(steps, own):
            for engine, step, s, r in PLAN[steps]:
                if engine == own["engine"] and step in own:
                    yield own[step], s, r

        def kv_bank(n):
            return ps[n // 2][:, n % 2, :]

        def tile(b, s, r):
            return b * TILES + (r * STREAMS + s)

        def x_tile(b, s, r):
            return x_all[:, bass.ds(tile(b, s, r), 1), :].rearrange("p a d -> p (a d)")

        def rep(ap, n):
            return ap.unsqueeze(len(ap.shape)).to_broadcast([*ap.shape, n])

        def heads4(ap):
            return ap.rearrange("p r (q j) -> p r q j", j=J)

        def psum_scores(s):
            return heads4(ps[s][:, :, 0:QUART])

        def sbuf_scores(s, half):
            return heads4(probs[s][:, half * HALF:(half + 1) * HALF].rearrange("p (r n) -> p r n", r=2))

        @block.sync
        def _(sp):
            sp.dma_start(ctx_all[:], t["ctxT"].rearrange("(c p) b j -> p c b j", p=P)).then_inc(loaded["ctx"], 16)
            sp.dma_start(wk0[:], t["Wk0"].rearrange("(c p) n -> p c n", p=P)).then_inc(loaded["k"], 16)
            sp.dma_start(relk_0[:], t["relk_0"]).then_inc(loaded["k"], 16)
            sp.dma_start(wv0[:], t["Wv0"].rearrange("(c p) n -> p c n", p=P)).then_inc(loaded["v"], 16)
            sp.dma_start(relv_0[:], t["relv_0"]).then_inc(loaded["v"], 16)
            sp.dma_start(wqT0[:], t["WqT0"].rearrange("(c p) n -> p c n", p=P)).then_inc(loaded["qT"], 16)
            sp.dma_start(wo0[:], t["Wo0"].rearrange("(c p) n -> p c n", p=P)).then_inc(loaded["o"], 16)
            sp.dma_start(relk_ext[:], t["relk_ext"]).then_inc(loaded["rel"], 16)
            sp.dma_start(relv_T[:], t["relv_T"]).then_inc(loaded["rel"], 16)
            sp.dma_start(x_all[:, 0:TILES, :], t["x"][0].rearrange("(n p) d -> p n d", p=P)).then_inc(loaded["x0"], 16)
            sp.dma_start(wq0[:], t["Wq0"].rearrange("(c p) n -> p c n", p=P)).then_inc(loaded["rel"], 16)
            sp.dma_start(bo0[:], t["bo0"]).then_inc(loaded["rest"], 16)
            for dst, src in ((sgw, "sgw"), (suw, "suw"), (sdw, "sdw"), (gate0, "gate0")):
                sp.dma_start(dst[:], t[src].rearrange("(c p) n -> p c n", p=P)).then_inc(loaded["rest"], 16)
            sp.dma_start(x_all[:, TILES:, :], t["x"][1].rearrange("(n p) d -> p n d", p=P)).then_inc(loaded["x1"], 16)
            for dst, src in ((rev, "rev"), (kstep, "kstep"), (blks, "blks"), (row, "row"), (low_tri, "low_tri")):
                sp.dma_start(dst[:], t[src]).then_inc(loaded["shape"], 16)
            sp.wait_ge(consts, CONSTS)
            for n in range(ROWS // (8 * P)):
                sp.dma_start(sorted_dram[n * 8 * P:(n + 1) * 8 * P, :].rearrange("(p a) d -> p a d", a=8),
                             zeros[:].unsqueeze(1).to_broadcast([P, 8, D])).then_inc(zero_out, 16)
            with sp.Fori(0, B) as b:
                s0 = streams[0]
                sp.wait_ge(s0.q.sem, s0.q.at(0, b, 5))
                sp.dma_start(rel_dram[0:P * H * EXT].rearrange("(p n) -> p n", p=P),
                             rel_q[:].rearrange("p h e -> p (h e)")).then_inc(rel_out, 16)
                sp.wait_ge(rel_out, 16 * b + 16)
                sp.dma_start(rel_s[:].rearrange("p (h j) -> p h j", h=H),
                             bass.AP(rel_dram, P - 1, [[H * EXT - 1, P], [EXT, H], [1, J]])).then_inc(rel_in, 16)
                sp.wait_ge(band_ready, b + 1)
                sp.dma_start(band_dram[0:P * H * PADW].rearrange("(p n) -> p n", p=P),
                             band_src.rearrange("p h e -> p (h e)")).then_inc(band_out, 16)
                sp.wait_ge(band_out, 16 * b + 16)
                sp.dma_start(band[:, :, 0:BAND],
                             bass.AP(band_dram, 0, [[H * PADW + 1, P], [PADW, H], [1, BAND]])).then_inc(band_in, 16)
            for s in range(STREAMS):
                sp.wait_ge(streams[s].x_new.sem, streams[s].x_new.at(0, B - 1, 4))
            for s in range(STREAMS):
                sp.wait_ge(streams[s].xn_stored, 16 * ROUNDS * B)
            for n in range(4):
                sp.dma_start(probsT[n][:].rearrange("p c n -> p (c n)")[:, 0:4 * D].rearrange("p (n d) -> p n d", d=D),
                             xn0_dram[n * 4 * P:(n + 1) * 4 * P, :].rearrange("(n p) d -> p n d", p=P))\
                    .then_inc(loaded["xn"], 16)
            for l in LAYERS:
                for n in ("wq", "wk", "wo"):
                    sp.dma_start(w2[n, l][:], t[f"{n}{l}"].rearrange("(c p) n -> p c n", p=P)).then_inc(loaded["p2"], 16)
                sp.dma_start(wv2[:, :, l - 1, :], t[f"wv{l}"].rearrange("(c p) n -> p c n", p=P)).then_inc(loaded["p2"], 16)
                if l < 3:
                    sp.dma_start(bv2[:, l - 1, :], t[f"bv{l}"]).then_inc(loaded["p2"], 16)
                    for n, d in (("bq", bq2), ("bk", bk2), ("bo", bo2)):
                        sp.dma_start(d[l][:], t[f"{n}{l}"]).then_inc(loaded["p2"], 16)
            for dst, src in ((head_mask, "head_mask"), (slot_mask, "slot_mask"), (v1, "v1"), (v2, "v2")):
                sp.dma_start(dst[:], t[src]).then_inc(loaded["p2"], 16)
            for dst, src in ((u1, "u1"), (u2, "u2"), (rhs_T, "rhsT"), (gate3, "gate3")):
                sp.dma_start(dst[:], t[src].rearrange("(c p) n -> p c n", p=P)).then_inc(loaded["p2"], 16)
            sp.dma_start(mask_in[:], t["mask"]).then_inc(loaded["p2"], 16)

            def rows_in(phase, s, i, value):
                st = streams[s]
                sp.wait_ge(st.xnT_ps.sem, value)
                sp.dma_start((xn if phase == 1 else x_in)[s][:], sorted_dram[bass.ds((i + s * PASSES[phase]) * BLK, BLK), :])\
                    .then_inc(st.rows_loaded, 16)

            def results_out(phase, s, i):
                st = streams[s]
                sp.wait_ge(st.x_new.sem, st.x_new.at(phase, i, 1))
                sp.dma_start(y_dram[bass.ds((i + s * PASSES[phase]) * BLK, BLK), :], y_sb[s] if phase == 1 else y3[s][:])\
                    .then_inc(st.y_out, 16)

            def blocks(phase, n_streams):
                for s in range(n_streams):
                    rows_in(phase, s, 0, streams[s].xnT_ps.at(phase, 0, 0))
                with sp.Fori(0, PASSES[phase] - 1) as i:
                    for s in range(n_streams):
                        rows_in(phase, s, i + 1, streams[s].xnT_ps.at(phase, i, 1))
                    for s in range(n_streams):
                        results_out(phase, s, i)
                for s in range(n_streams):
                    results_out(phase, s, PASSES[phase] - 1)

            sp.wait_ge(scattered, 16 * NT)
            blocks(1, STREAMS)
            for s in range(STREAMS):
                sp.wait_ge(streams[s].x_new.sem, streams[s].x_new.at(2, B - 1, 12))
            for s in range(STREAMS):
                sp.wait_ge(streams[s].xn_stored, 16 * 2 * ROUNDS * B)
            sp.wait_ge(gathered, 16 * NT)
            sp.dma_start(rows3[0][:], xn3_dram[:].rearrange("(n p) d -> p n d", p=P)).then_inc(loaded["xn"], 16)
            sp.wait_ge(scattered, 16 * 3 * NT)
            blocks(3, MS3)
            per = NT // GROUPS
            for g in range(GROUPS):
                sp.wait_ge(combined, g + 1)
                sp.dma_start(out.rearrange("b (n p) d -> p (b n) d", p=P)[:, g * per:(g + 1) * per, :],
                             x_all[:, g * per:(g + 1) * per, :]).then_inc(stored, 16)
            sp.wait_ge(stored, 16 * GROUPS)

        @block.gpsimd
        def _(pool):
            link = Links(pool, pool_link)
            nc.gpsimd.memset(zeros[:], 0.0).then_inc(consts, 1)
            link(nc.gpsimd.memset(ident[:], 0.0))
            nc.gpsimd.affine_select(out=ident[:], in_=ident[:], compare_op=ALU.not_equal, fill=1.0, base=0,
                                    pattern=[[-1, P]], channel_multiplier=1).then_inc(consts, 1)
            nc.gpsimd.memset(ones[:], 1.0).then_inc(consts, 1)
            nc.gpsimd.memset(minus_half[:], -0.5).then_inc(consts, 1)
            nc.gpsimd.memset(vT0[:], 0.0).then_inc(consts, 1)
            link(nc.gpsimd.memset(tail_mask[:], 1.0))
            nc.gpsimd.affine_select(out=tail_mask[:], in_=tail_mask[:], compare_op=ALU.is_ge, fill=0.0,
                                    base=-MAXREL, pattern=[[1, J]], channel_multiplier=-1).then_inc(consts, 1)

            for m, op, base in ((causal_f, ALU.is_ge, 0),):
                link(nc.gpsimd.memset(m[:], 1.0))
                nc.gpsimd.affine_select(out=m[:], in_=m[:], compare_op=op, fill=0.0, base=base,
                                        pattern=[[-1, J]], channel_multiplier=1).then_inc(consts, 1)
            link(nc.gpsimd.memset(diag_f[:], 1.0))
            nc.gpsimd.affine_select(out=diag_f[:], in_=diag_f[:], compare_op=ALU.is_gt, fill=0.0, base=0,
                                    pattern=[[1, P]], channel_multiplier=-1).then_inc(consts, 1)
            nc.gpsimd.memset(onesq[:], 1.0).then_inc(consts, 1)
            for s in range(STREAMS):
                nc.gpsimd.memset(low_T[s][:], 1.0).then_inc(consts, 1)

            def ln_rstd(s, phase, k):
                st = streams[s]
                pool.wait_ge(st.aggr.sem, st.aggr.at(phase, b, k))
                pool.nop(nofuse=True)
                link(nc.gpsimd.tensor_scalar(rstd[s][:, 1:2], mean_var[s][:, 1:2], EPS, None, ALU.add))
                nc.gpsimd.tensor_tensor(rstd[s][:, 0:1], rstd[s][:, 1:2], minus_half[:], ALU.pow)\
                    .then_inc(st.rstd.sem, 1)

            def ln1(s, r):
                ln_rstd(s, 0, 2 * r + 1)

            def ln2(s, r):
                ln_rstd(s, 0, 2 * r + 2)

            def xn_store(s, r):
                st = streams[s]
                pool.wait_ge(st.xn.sem, st.xn.at(0, b, 2 * r + 2))
                pool.dma_start(xn0_dram[bass.ds(tile(b, s, r) * P, P), :], xn[s][:]).then_inc(st.xn_stored, 16)

            pool.wait_ge(loaded["ctx"], 16)
            with pool.Fori(0, B) as b:
                link.enter(b, POOL_LINKS1)
                pool.wait_ge(prep_ps.sem, prep_ps.at(0, b, 0))
                pool.nop(nofuse=True)
                nc.gpsimd.tensor_copy(ctx_b[:].rearrange("p c j -> p c j"),
                                      ctx_all[:, :, bass.ds(b, 1), :].rearrange("p c a j -> p c (a j)"))\
                    .then_inc(ctx_ready, 1)
                for f, s, r in order(STEPS1, dict(engine=PO, stats1=ln1, stats2=ln2, apply2=xn_store)):
                    f(s, r)
            link.leave(B)

            def scatter(row, n, tl):
                pool.indirect_dma_start(out=sorted_dram[:], out_offset=bass.IndirectOffsetOnAxis(
                    ap=slot[:, n, tl:tl + 1], axis=0), in_=row, in_offset=None).then_inc(scattered, 16)

            def gather(row, n, tl, done):
                pool.indirect_dma_start(out=row, out_offset=None, in_=y_dram[:],
                                        in_offset=bass.IndirectOffsetOnAxis(ap=slot[:, n, tl:tl + 1], axis=0))\
                    .then_inc(done, 16)

            def load_weights(i, phase, n_streams, w_in, w_out, src_in, src_out, n_exp):
                for n, (w, src) in enumerate(((w_in, src_in), (w_out, src_out))):
                    for s in range(n_streams):
                        st = streams[s]
                        last = (st.f_ps, st.y_ps)[n]
                        pool.wait_ge(last.sem, last.at(phase, i, 0))
                        pool.nop(nofuse=True)
                        link(nc.gpsimd.tensor_copy(load_now[:, n, s:s + 1], load[:, bass.ds(i + s * PASSES[phase], 1)]))
                        pool.nop(nofuse=True)
                        pool.indirect_dma_start(
                            out=w[s][:].rearrange("p a c n -> p (a c n)" if n == 0 else "p c n -> p (c n)"),
                            out_offset=None, in_=t[src],
                            in_offset=bass.IndirectOffsetOnAxis(ap=load_now[:, n, s:s + 1], axis=0),
                            bounds_check=n_exp * P - 1, oob_is_err=False).then_inc((st.in_loaded, st.out_loaded)[n], 16)

            def experts(phase, n_streams, slots, rows, *weights):
                pool.wait_ge(routed, 1 if phase == 1 else 2)
                for n in range(slots):
                    for tl in range(NT):
                        if phase == 1:
                            pool.wait_ge(scaled, tl + 1)
                        scatter(rows(tl), n, tl)
                pool.wait_ge(loads_ready, 1 if phase == 1 else 2)
                load_weights(0, phase, n_streams, *weights)
                with pool.Fori(1, PASSES[phase]) as i:
                    link.enter(i - 1, 2 * n_streams)
                    load_weights(i, phase, n_streams, *weights)
                link.leave(PASSES[phase] - 1)

            pool.wait_ge(zero_out, 16 * (ROWS // (8 * P)))
            experts(1, STREAMS, 1, lambda tl: rows0[tl], w_in0, w_out0, "w_in0", "w_out0", E0)
            for s in range(STREAMS):
                pool.wait_ge(streams[s].y_out, 16 * PASSES[1])
            for tl in range(NT):
                gather(rows0[tl], 0, tl, gathered)

            def rstd2(k):
                return lambda s, r: ln_rstd(s, 2, 6 * r + k)

            def fill(l):
                def step(s, r):
                    st = streams[s]
                    if l < 3 and (s or r):
                        return
                    pool.wait_ge(st.q_ps.sem, st.q_ps.at(2, b, 3 * r + l))
                    pool.nop(nofuse=True)
                    ins = nc.gpsimd.memset(probs[s][:], NEVER if l < 3 else MASKED * 4)
                    if l == 3:
                        ins = nc.gpsimd.tensor_copy(
                            filled_mask[s][:], unmasked[:, bass.ds(tile(b, s, r), 1), :].rearrange("p a j -> p (a j)"))
                    ins.then_inc(st.filled.sem, 1)
                return step

            def xn_store2(s, r):
                st = streams[s]
                pool.wait_ge(st.xn.sem, st.xn.at(2, b, 6 * r + 6))
                pool.dma_start(xn3_dram[bass.ds(tile(b, s, r) * P, P), :], xn[s][:]).then_inc(st.xn_stored, 16)

            own = {f"stats{l}": rstd2(2 * l - 1) for l in LAYERS}
            own |= {f"fstats{l}": rstd2(2 * l) for l in LAYERS} | {f"q{l}": fill(l) for l in LAYERS}
            with pool.Fori(0, B) as b:
                link.enter(b, POOL_LINKS2)
                for f, s, r in order(STEPS2, own | dict(engine=PO, fapply3=xn_store2)):
                    f(s, r)
            link.leave(B)

            pool.wait_ge(loaded["xn"], 16 * 5)
            experts(3, MS3, 2, lambda tl: rows3[0][:, tl, :], w_in3, w_out3, "w_in3", "w_out3", E3)
            for s in range(MS3):
                pool.wait_ge(streams[s].y_out, 16 * (PASSES[1] + PASSES[3]))
            for tl in range(NT):
                for n in range(2):
                    gather(rows3[n][:, tl, :], n, tl, gathered3[tl * GROUPS // NT])

        def act_copy(dst, src):
            return nc.scalar.activation(dst, src, ACT.Copy)

        @block.scalar
        def _(act):
            def prep(b):
                act.wait_ge(prep_ps.sem, prep_ps.at(0, b, 1))
                for a in range(2):
                    last = nc.scalar.activation(kT0[:, 4 * a:4 * a + 4, :],
                                                ps[0][:, a, 0:4 * J].rearrange("p (c j) -> p c j", j=J),
                                                ACT.Identity, bias=relk_0[:])
                last.then_inc(prep_sb.sem, 1)
                for n, (kc, half) in enumerate(((0, 0), (0, 1), (1, 0), (1, 1))):
                    act.wait_ge(prep_ps.sem, prep_ps.at(0, b, 2 + n))
                    pair = (2 + n) % 4
                    for par in range(2):
                        last = act_copy(
                            qk0[:, kc, half * HALF:(half + 1) * HALF].rearrange("p (c r j) -> p r c j", r=2, j=J)[:, par],
                            ps[pair][:, par, 0:QUART].rearrange("p (c j) -> p c j", j=J))
                    last.then_inc(prep_sb.sem, 1)
                for n in range(3):
                    act.wait_ge(prep_ps.sem, prep_ps.at(0, b, 6 + n))
                    pair = (2 + n) % 4
                    if n < 2:
                        last = act_copy(vo0[:, 4 * n:4 * n + 4, :].rearrange("p (a g) n -> p a (g n)", a=2), ps[pair][:])
                    else:
                        act_copy(vo0[:, 8, :], ps[pair][:, 0, 0:D])
                        last = act_copy(vo0[0:LAST_CH, 9, :], ps[pair][0:LAST_CH, 0, D:2 * D])
                    last.then_inc(prep_sb.sem, 1)
                act.wait_ge(prep_ps.sem, prep_ps.at(0, b, 9))
                act_copy(relvo[:].rearrange("p g n -> p (g n)"), ps[1][:].rearrange("p a n -> p (a n)"))\
                    .then_inc(prep_sb.sem, 1)

            def xn_T(s, phase, i, k):
                st = streams[s]
                act.wait_ge(st.xnT_ps.sem, st.xnT_ps.at(phase, i, k))
                act_copy(xnT[s][:].rearrange("p c n -> p (c n)"), ps[s][:, 0, 0:D]).then_inc(st.xnT.sem, 1)

            def xnT1(s, r):
                xn_T(s, 0, b, 2 * r + 1)

            def xnT2(s, r):
                xn_T(s, 0, b, 2 * r + 2)

            def rel_scores(s, r):
                if s or r:
                    return
                st = streams[0]
                act.wait_ge(st.q_ps.sem, st.q_ps.at(0, b, 1))
                act_copy(qT0.rearrange("p (a c) n -> p a (c n)", a=2), ps[0][:]).then_inc(st.q.sem, 1)
                for g in range(4):
                    act.wait_ge(st.q_ps.sem, st.q_ps.at(0, b, 2 + g))
                    for par in range(2):
                        last = act_copy(rel_q[:, 4 * g:4 * g + 4, :].rearrange("p (c r) e -> p r c e", r=2)[:, par],
                                        ps[0][:, par, 0:2 * EXT].rearrange("p (c e) -> p c e", e=EXT))
                    last.then_inc(st.q.sem, 1)

            def exp(s, phase, k, half):
                st = streams[s]
                act.wait_ge(st.p_sub.sem, st.p_sub.at(phase, b, 2 * k))
                part = probs[s][:, half * HALF:(half + 1) * HALF]
                nc.scalar.activation(part, part, ACT.Exp, scale=(D0 if phase == 0 else ATT) ** -0.5)\
                    .then_inc(st.p_exp.sem, 1)

            def exp0(s, r):
                exp(s, 0, 2 * r + 1, 0)

            def exp1(s, r):
                exp(s, 0, 2 * r + 2, 1)

            def probs_T(s, phase, n, step):
                st = streams[s]
                flat = probsT[s][:].rearrange("p c n -> p (c n)")
                for part in ((0, 1), (2,))[step]:
                    act.wait_ge(st.pT_ps.sem, st.pT_ps.at(phase, b, 3 * n + part + 1))
                    if part < 2:
                        last = act_copy(flat[:, part * 512:(part + 1) * 512], ps[s][:, part, :])
                    else:
                        act_copy(flat[:, 1024:1152], ps[s][:, 0, 0:P])
                        last = act_copy(flat[0:LAST_CH, 1152:1280], ps[s][0:LAST_CH, 0, P:2 * P])
                    last.then_inc(st.pT.sem, 1)

            def pT0(s, r):
                probs_T(s, 0, r, 0)

            def pT1(s, r):
                probs_T(s, 0, r, 1)

            def band_T(s, r):
                if s or r:
                    return
                st = streams[0]
                act.wait_ge(st.q_ps.sem, st.q_ps.at(0, b, 6))
                act_copy(bandT[:].rearrange("p c n -> p (c n)"), ps[0][:, 0, :]).then_inc(st.q.sem, 1)

            def gate_tanh(s, r):
                st = streams[s]
                act.wait_ge(st.f_ps.sem, st.f_ps.at(0, b, r + 1))
                nc.scalar.activation(hid[s][:, 0, :], ps[s][:, 0, :], ACT.Tanh, scale=0.5).then_inc(st.f.sem, 1)

            def gate_act(s, phase, i, k):
                st = streams[s]
                act.wait_ge(st.f_ps.sem, st.f_ps.at(phase, i, k))
                nc.scalar.activation(hid[s][:, 0, :], ps[s][:, 0, :], ACT.Silu).then_inc(st.f.sem, 1)

            act.wait_ge(consts, CONSTS)
            act.wait_ge(loaded["k"], 32)
            with act.Fori(0, B) as b:
                prep(b)
                for f, s, r in order(STEPS1, dict(engine=AC, apply1=xnT1, rel=rel_scores, half0=exp0, half1=exp1, pT0=pT0, pT1=pT1,
                                                  band=band_T, apply2=xnT2, gate_up=gate_tanh)):
                    f(s, r)

            for s in range(STREAMS):
                act.wait_ge(streams[s].x_new.sem, streams[s].x_new.at(0, B - 1, 4))
            for kc in range(KC):
                for b in range(B):
                    last = act_copy(ctx_rep[:, kc, b, :].rearrange("p (n j) -> p n j", j=J),
                                    ctx_all[:, kc, b:b + 1, :].to_broadcast([P, REPS, J]))
            last.then_inc(rep_ready, 1)
            act.wait_ge(top_ready, 1)
            nc.scalar.activation(route[:, 1, :], route[:, 0, :], ACT.Exp, scale=-1.0).then_inc(score_exp, 1)
            with act.Fori(0, PASSES[1]) as i:
                for s in range(STREAMS):
                    xn_T(s, 1, i, 1)
                for s in range(STREAMS):
                    gate_act(s, 1, i, 1)

            act.wait_ge(rhs_ps, 1)
            act_copy(rhs_qT[:].rearrange("p c n -> p (c n)"), ps[2][:, 0, 0:D].bitcast(BF16))
            act_copy(rhs_scale_row[:], ps[2][:, 1, 0:D]).then_inc(rhs_sb, 1)

            def xnT_of(n):
                return lambda s, r: xn_T(s, 2, b, 5 * r + n)

            def q_T(l):
                def step(s, r):
                    st = streams[s]
                    act.wait_ge(st.q_ps.sem, st.q_ps.at(2, b, 3 * r + l))
                    if l == 3:
                        last = act_copy(qT[s][:].rearrange("p c n -> p (c n)"), ps[s][:, 0, 0:D])
                    else:
                        for c in range(KC):
                            last = nc.scalar.activation(qT[s][:, c, :], ps[s][:, 0, c * P:c * P + P], ACT.Identity,
                                                        bias=bq2[l][:, c:c + 1])
                    last.then_inc(st.q.sem, 1)
                return step

            def out_T(l):
                def step(s, r):
                    st = streams[s]
                    act.wait_ge(st.oT_ps.sem, st.oT_ps.at(2, b, 3 * r + l))
                    act_copy(xnT[s][:].rearrange("p c n -> p (c n)"), ps[s][:, 1, 0:D]).then_inc(st.oT.sem, 1)
                return step

            def low_copy(n):
                def step(s, r):
                    st = streams[s]
                    act.wait_ge(st.f_ps.sem, st.f_ps.at(2, b, 4 * r + n))
                    act_copy(low_T[s][0:LOW, :], ps[s][0:LOW, 0, 0:P]).then_inc(st.f.sem, 1)
                return step

            def gelu(s, r):
                st = streams[s]
                act.wait_ge(st.f_ps.sem, st.f_ps.at(2, b, 4 * r + 2))
                nc.scalar.activation(probs[s][:, 0:F1], ps[s][:].rearrange("p a n -> p (a n)"), ACT.Gelu_apprx_tanh)\
                    .then_inc(st.f.sem, 1)

            def quant_T(s, r):
                st = streams[s]
                act.wait_ge(st.f_ps.sem, st.f_ps.at(2, b, 4 * r + 4))
                act_copy(x_qT[s][:], ps[s][:, 0, 0:P].bitcast(BF16)).then_inc(st.f.sem, 1)

            own = {"engine": AC}
            for l in LAYERS:
                own |= {f"apply{l}": xnT_of({1: 1, 2: 3, 3: 4}[l]), f"q{l}": q_T(l), f"oT{l}": out_T(l)}
                own |= {f"half{h}_{l}": (lambda s, r, l=l, h=h: exp(s, 2, 6 * r + 2 * l - 1 + h, h)) for h in range(2)}
                own |= {f"pT{h}_{l}": (lambda s, r, l=l, h=h: probs_T(s, 2, 3 * r + l - 1, h)) for h in range(2)}
            own |= dict(fapply1=xnT_of(2), fapply3=xnT_of(5), low1=low_copy(1), gelu1=gelu, low21=low_copy(3), quant2=quant_T)
            with act.Fori(0, B) as b:
                for f, s, r in order(STEPS2, own):
                    f(s, r)

            act.wait_ge(top_ready, 2)
            e1, e2 = (probs[0][:, n * NT * E3:(n + 1) * NT * E3] for n in (2, 3))
            nc.scalar.activation(e1, e1, ACT.Exp, scale=-1.0)
            nc.scalar.activation(e2, e2, ACT.Exp).then_inc(score_exp, 1)
            with act.Fori(0, PASSES[3]) as i:
                for s in range(MS3):
                    st = streams[s]
                    act.wait_ge(st.xnT_ps.sem, st.xnT_ps.at(3, i, 1))
                    act_copy(x_inT[s][:].rearrange("p c n -> p (c n)"), ps[2 * s][:, 0, 0:D]).then_inc(st.xnT.sem, 1)
                for n in range(2):
                    for s in range(MS3):
                        st = streams[s]
                        act.wait_ge(st.f_ps.sem, st.f_ps.at(3, i, n + 1))
                        if n:
                            act.wait_ge(st.fm.sem, st.fm.at(3, i, n))
                        nc.scalar.activation(act3[s][:], ps[2 * s + (n + 1) % 2][:, 0, :], ACT.Silu).then_inc(st.f.sem, 1)

        @block.vector
        def _(dve):
            link = Links(dve, dve_link)
            for s in range(STREAMS):
                dve.sem_inc(streams[s].x_new.sem, 1)
            dve.wait_ge(loaded["k"], 32)
            dve.wait_ge(loaded["v"], 32)
            dve.wait_ge(loaded["rel"], 48)
            nc.vector.tensor_scalar(relk_ext[:], relk_ext[:], relk_0[:], None, ALU.subtract)
            link(nc.vector.memset(relv_m[:], 0.0))
            for par in range(2):
                for r in range(2):
                    at = (2 * par + r) * NREL
                    last = nc.vector.tensor_scalar(relv_m[D0 * r:D0 * r + D0, par, at:at + NREL],
                                                   relv_T[D0 * r:D0 * r + D0, :], relv_0[D0 * r:D0 * r + D0, :],
                                                   None, ALU.subtract)
            last.then_inc(rel_const, 1)
            dve.wait_ge(consts, CONSTS)
            nc.vector.tensor_copy(causal[:], causal_f[:])
            nc.vector.tensor_copy(squareb[:], diag_f[:])
            nc.vector.tensor_copy(onesb[:], onesq[:])

            def ln_stats(s, r):
                if s == 0:
                    dve.wait_ge(loaded["x1" if r else "x0"], 16)
                dve.nop(nofuse=True)
                link(nc.vector.bn_stats(stats[s][:], x_tile(b, s, r)))
                dve.nop(nofuse=True)
                nc.vector.bn_aggr(mean_var[s][:], stats[s][:]).then_inc(streams[s].aggr.sem, 1)

            def ln_apply(s, r, phase, k):
                st = streams[s]
                dve.wait_ge(st.rstd.sem, st.rstd.at(phase, b, k))
                nc.vector.tensor_scalar(xn[s][:], x_tile(b, s, r), mean_var[s][:, 0:1], rstd[s][:, 0:1],
                                        ALU.subtract, ALU.mult).then_inc(st.xn.sem, 1)

            def ln1a(s, r):
                ln_stats(s, r)

            def ln1b(s, r):
                if r:
                    dve.wait_ge(streams[s].xn_stored, 16 * (b * ROUNDS + r))
                ln_apply(s, r, 0, 2 * r + 1)

            def ln2a(s, r):
                ln_stats(s, r)

            def ln2b(s, r):
                ln_apply(s, r, 0, 2 * r + 2)

            def softmax_half(s, r, half):
                st = streams[s]
                for a in range(2):
                    dve.wait_ge(st.s_ps.sem, st.s_ps.at(0, b, 4 * r + 2 * half + a + 1))
                    src, dst = psum_scores(s)[:, a], sbuf_scores(s, half)[:, a]
                    if s == 0 and r == 0:
                        if half == 0:
                            dve.wait_ge(rel_in, 16 * b + 16)
                        rel = heads4(rel_s[:, half * HALF:(half + 1) * HALF].rearrange("p (r n) -> p r n", r=2))[:, a]
                        link(nc.vector.tensor_tensor(dst, src, rel, ALU.add))
                        src = dst
                    m = mx[s][:, 8 * half + 4 * a:8 * half + 4 * a + 4]
                    link(nc.vector.tensor_reduce(out=m, in_=src, axis=X, op=ALU.max))
                    nc.vector.tensor_tensor(dst, src, rep(m, J), ALU.subtract).then_inc(st.p_sub.sem, 1)

            def soft0(s, r):
                softmax_half(s, r, 0)

            def soft1(s, r):
                softmax_half(s, r, 1)

            def normalise(s, r):
                st = streams[s]
                dve.wait_ge(st.p_exp.sem, st.p_exp.at(0, b, 2 * r + 2))
                p3 = probs[s][:].rearrange("p (h j) -> p h j", j=J)
                link(nc.vector.tensor_reduce(out=mx[s][:], in_=p3, axis=X, op=ALU.add))
                link(nc.vector.reciprocal(mx[s][:], mx[s][:]))
                ins = nc.vector.tensor_tensor(p3, p3, rep(mx[s][:], J), ALU.mult)
                ins.then_inc(st.o.sem, 1)
                if s == 0 and r == 0:
                    dve.wait_ge(st.o.sem, st.o.at(0, b, 1))
                    link(nc.vector.memset(band_src, 0.0))
                    nc.vector.tensor_copy(band_src[:, :, MAXREL - 1:MAXREL - 1 + J], p3).then_inc(band_ready, 1)
                    tail = rel_s[:].rearrange("p (h j) -> p h j", j=J)
                    link(nc.vector.tensor_tensor(tail, p3, tail_mask[:].unsqueeze(1).to_broadcast([P, H, J]), ALU.mult))
                    nc.vector.tensor_reduce(out=band[:, :, BAND], in_=tail, axis=X, op=ALU.add).then_inc(band_tail, 1)

            def residual(s, r, u):
                st = streams[s]
                dve.wait_ge(st.y_ps.sem, st.y_ps.at(0, b, 2 * r + u + 1))
                if u:
                    nc.vector.tensor_copy(logits0[:, bass.ds(tile(b, s, r), 1), :].rearrange("p a d -> p (a d)"),
                                          ps[s][:, 1, 0:E0])
                ins = nc.vector.tensor_tensor(x_tile(b, s, r), ps[s][:, 0, 0:D], x_tile(b, s, r), ALU.add)
                ins.then_inc(st.x_new.sem, 1)
                dve.wait_ge(st.x_new.sem, st.x_new.at(0, b, 2 * r + u + 1))

            def res1(s, r):
                residual(s, r, 0)

            def res2(s, r):
                residual(s, r, 1)

            def gate_up(s, r):
                st = streams[s]
                dve.wait_ge(st.f.sem, st.f.at(0, b, r + 1))
                link(nc.vector.scalar_tensor_tensor(out=hid[s][:, 0, :], in0=hid[s][:, 0, :], scalar=1.0, in1=ps[s][:, 0, :],
                                                    op0=ALU.add, op1=ALU.mult))
                nc.vector.scalar_tensor_tensor(out=hid[s][:, 1, :], in0=hid[s][:, 0, :], scalar=0.5, in1=ps[s][:, 1, :],
                                               op0=ALU.mult, op1=ALU.mult).then_inc(st.fm.sem, 1)

            dve.wait_ge(consts, CONSTS)
            nc.vector.tensor_copy(identb[:], ident[:])

            def prep(b):
                dve.wait_ge(v_ps, b + 1)
                dve.nop(nofuse=True)
                for c in range(C0):
                    for r in range(2):
                        at = c * 3 * P + (2 * c + r) * J - window(c)
                        last = nc.vector.tensor_scalar(vT0[D0 * r:D0 * r + D0, at:at + J],
                                                       ps[1][D0 * r:D0 * r + D0, c // 4, c % 4 * J:c % 4 * J + J],
                                                       relv_0[D0 * r:D0 * r + D0, :], None, ALU.add)
                last.then_inc(vT_ready, 1)

            with dve.Fori(0, B) as b:
                link.enter(b, DVE_LINKS1)
                prep(b)
                for f, s, r in order(STEPS1, dict(engine=DV, stats1=ln1a, apply1=ln1b, half0=soft0, half1=soft1, norm=normalise,
                                                  out1=res1, stats2=ln2a, apply2=ln2b, gate_up=gate_up, out2=res2)):
                    f(s, r)
                for s in range(STREAMS):
                    dve.wait_ge(streams[s].xn_stored, 16 * (b * ROUNDS + ROUNDS))
            link.leave(B)

            def routing(logits, n_exp, top2):
                size = NT * n_exp
                tmp = {0: probs[0][:, 0:size], 7: probs[2][:, 0:size]}
                if top2:
                    tmp |= {n: probs[0][:, n * size:(n + 1) * size] for n in range(8)}
                tmp = {n: x.rearrange("p (n e) -> p n e", e=n_exp) for n, x in tmp.items()}
                tmp.setdefault(5, tmp[7])
                revs = rev[:, E0 - n_exp:E0].unsqueeze(1).to_broadcast([P, NT, n_exp])
                tt, tr = nc.vector.tensor_tensor, nc.vector.tensor_reduce

                def top(scores, best, hot):
                    link(tr(out=best, in_=scores, axis=X, op=ALU.max))
                    link(tt(tmp[7], scores, rep(best, n_exp), ALU.is_equal))
                    link(tt(tmp[7], tmp[7], revs, ALU.mult))
                    link(tr(out=route[:, 7, :], in_=tmp[7], axis=X, op=ALU.max))
                    link(tt(hot, tmp[7], rep(route[:, 7, :], n_exp), ALU.is_equal))

                hots = [tmp[0], tmp[1]] if top2 else [tmp[0]]
                m1, m2, w1, w2s = (route[:, n, :] for n in range(4))
                top(logits, route[:, 0, :], hots[0])
                if not top2:
                    nc.vector.tensor_copy(one_hot[:].rearrange("p (n e) -> p n e", e=n_exp), hots[0])\
                        .then_inc(one_hot_ready, 1)
                    nc.vector.tensor_copy(route[:, 5, :], route[:, 0, :]).then_inc(top_ready, 1)
                    dve.wait_ge(score_exp, 1)
                    link(nc.vector.tensor_scalar_add(route[:, 1, :], route[:, 1, :], 1.0))
                    link(nc.vector.reciprocal(route[:, 1, :], route[:, 1, :]))
                else:
                    link(nc.vector.scalar_tensor_tensor(out=tmp[4], in0=hots[0], scalar=NEVER, in1=logits,
                                                        op0=ALU.mult, op1=ALU.add))
                    top(tmp[4], route[:, 1, :], hots[1])
                    oh = one_hot[:, 0:NT * n_exp].rearrange("p (n e) -> p n e", e=n_exp)
                    tt(oh, hots[0], hots[1], ALU.add).then_inc(one_hot_ready, 1)
                    for n, best in ((2, m1), (3, m2)):
                        link(nc.vector.scalar_tensor_tensor(out=tmp[5 + n - 2], in0=logits, scalar=-1.0, in1=logits,
                                                            op0=ALU.mult, op1=ALU.max))
                        link(tt(tmp[5 + n - 2], tmp[5 + n - 2], rep(best, n_exp), ALU.max))
                        link(tt(tmp[7], rep(best, n_exp), logits, ALU.subtract))
                        if n == 2:
                            nc.vector.tensor_copy(tmp[2], tmp[7])
                        link(nc.vector.scalar_tensor_tensor(out=tmp[5 + n - 2], in0=tmp[5 + n - 2], scalar=2 * JITTER,
                                                            in1=tmp[7], op0=ALU.mult, op1=ALU.is_ge))
                    tt(tmp[3], tmp[4], rep(m2, n_exp), ALU.subtract).then_inc(top_ready, 1)
                    dve.wait_ge(score_exp, 2)
                    for n in range(2):
                        link(tt(tmp[2 + n], tmp[2 + n], tmp[5 + n], ALU.mult))
                        link(tr(out=route[:, 2 + n, :], in_=tmp[2 + n], axis=X, op=ALU.add))
                        link(nc.vector.reciprocal(route[:, 2 + n, :], route[:, 2 + n, :]))
                dve.wait_ge(rank_ready, 2 if top2 else 1)
                nblk, end, start = (blocks_of[:, n, 0:n_exp] for n in range(3))
                n_step = B * T // BLK
                big = probs[1][:]
                cmp = big[:, 0:n_exp * n_step].rearrange("p (e k) -> p e k", k=n_step)
                link(tt(cmp, rep(ps[1][:, 0, 0:n_exp], n_step),
                        kstep[:].unsqueeze(1).to_broadcast([P, n_exp, n_step]), ALU.is_gt))
                link(tr(out=nblk, in_=cmp, axis=X, op=ALU.add))
                tri = big[:, 0:n_exp * n_exp].rearrange("p (e f) -> p e f", f=n_exp)
                link(tt(tri, nblk.unsqueeze(1).to_broadcast([P, n_exp, n_exp]), low_tri[:, 0:n_exp, 0:n_exp], ALU.mult))
                link(tr(out=end, in_=tri, axis=X, op=ALU.add))
                link(tt(start, end, nblk, ALU.subtract))
                link(nc.vector.scalar_tensor_tensor(
                    out=tmp[7], in0=start.unsqueeze(1).to_broadcast([P, NT, n_exp]), scalar=float(BLK),
                    in1=ps[0][:, 0, 0:NT * n_exp].rearrange("p (n e) -> p n e", e=n_exp), op0=ALU.mult, op1=ALU.add))
                for n, hot in enumerate(hots):
                    link(tt(tmp[5 + n], tmp[7], hot, ALU.mult))
                    link(tr(out=route[:, 5 + n, :], in_=tmp[5 + n], axis=X, op=ALU.add))
                    last = nc.vector.tensor_copy(slot[:, n, :], route[:, 5 + n, :])
                last.then_inc(routed, 1)

            def loads(n_exp, n_blocks, n_streams):
                tt, tr, end = nc.vector.tensor_tensor, nc.vector.tensor_reduce, blocks_of[:, 1, 0:n_exp]
                big = probs[1][:]
                half = n_blocks // 2
                for n in range(2):
                    out3 = big[:, 0:half * n_exp].rearrange("p (k e) -> p k e", e=n_exp)
                    link(tt(out3, end.unsqueeze(1).to_broadcast([P, half, n_exp]),
                            rep(blks[:, n * half:(n + 1) * half], n_exp), ALU.is_le))
                    link(tr(out=expert[:, n * half:(n + 1) * half], in_=out3, axis=X, op=ALU.add))
                e, ld = expert[:, 0:n_blocks], load_f[:, 0:n_blocks]
                link(tt(ld[:, 1:], e[:, 1:], e[:, 0:n_blocks - 1], ALU.is_equal))
                link(nc.vector.scalar_tensor_tensor(out=ld[:, 1:], in0=ld[:, 1:], scalar=float(n_exp), in1=e[:, 1:],
                                                    op0=ALU.mult, op1=ALU.add))
                first = ld.rearrange("p (s i) -> p s i", i=n_blocks // n_streams)[:, :, 0]
                link(nc.vector.tensor_scalar(first, e.rearrange("p (s i) -> p s i", i=n_blocks // n_streams)[:, :, 0],
                                             float(n_exp - 1), None, ALU.min))
                link(nc.vector.tensor_scalar(ld, ld, float(P), row[:], ALU.mult, ALU.add))
                nc.vector.tensor_copy(load[:, 0:n_blocks], ld).then_inc(loads_ready, 1)

            dve.wait_ge(loaded["shape"], 16 * 5)
            routing(logits0[:], E0, False)
            dve.wait_ge(loaded["xn"], 16 * 4)
            for tl in range(NT):
                nc.vector.tensor_scalar(rows0[tl], rows0[tl], route[:, 1, tl:tl + 1], None, ALU.mult).then_inc(scaled, 1)
            loads(E0, NB0, STREAMS)

            def expert_mul(s, phase, i, k):
                st = streams[s]
                dve.wait_ge(st.f.sem, st.f.at(phase, i, k))
                nc.vector.tensor_tensor(hid[s][:, 1, :], ps[s][:, 1, :], hid[s][:, 0, :], ALU.mult).then_inc(st.fm.sem, 1)

            def expert_pass(i, first):
                for s in range(STREAMS):
                    expert_mul(s, 1, i, 1)
                for s in range(STREAMS):
                    st = streams[s]
                    dve.wait_ge(st.y_ps.sem, st.y_ps.at(1, i, 1))
                    if not first:
                        dve.wait_ge(st.y_out, 16 * i)
                    nc.vector.tensor_copy(y_sb[s], ps[s][:, 0, 0:D]).then_inc(st.x_new.sem, 1)

            expert_pass(0, True)
            with dve.Fori(1, PASSES[1]) as i:
                expert_pass(i, False)
            dve.wait_ge(loaded["p2"], 16 * (12 + 8 + 9))
            nc.vector.tensor_scalar(unmasked[:].rearrange("p n j -> p (n j)"), mask_in[:].bitcast(U8), 0.0, None, ALU.is_equal)
            nc.vector.tensor_copy(v_bd[:, 0].rearrange("p k l (s d) -> p (k l) s d", d=VW)[:, :, :, ATT],
                                  slot_mask[:].rearrange("p k l s -> p (k l) s"))
            nc.vector.tensor_copy(v_bd[:, 1].rearrange("p k l (s d) -> p (k l) s d", d=VW)[:, :, :, ATT],
                                  slot_mask[:].rearrange("p k l s -> p (k l) s"))
            dve.wait_ge(kv_ps, 1)
            for l in LAYERS:
                for c in range(KC):
                    src = kv_bank(l - 1)[:, c * B * J:(c + 1) * B * J].rearrange("p (b j) -> p b j", b=B)
                    dst = k_all[:, :, c, l - 1, :]
                    if l < 3:
                        last = nc.vector.tensor_scalar(dst, src, bk2[l][:, c:c + 1], None, ALU.add)
                    else:
                        last = nc.vector.tensor_copy(dst, src)
            last.then_inc(kv_sb, 1)

            def quantise(out_q, src, scales, tmp2):
                s_, r_ = scales
                link(nc.vector.tensor_reduce(out=s_, in_=src, axis=X, op=ALU.max, apply_absolute_value=True))
                link(nc.vector.tensor_scalar(s_, s_, 1e-12, 1.0 / QMAX, ALU.max, ALU.mult))
                link(nc.vector.reciprocal(r_, s_))
                link(nc.vector.tensor_scalar(tmp2, src, r_, QMAX, ALU.mult, ALU.min))
                link(nc.vector.tensor_scalar(tmp2, tmp2, -QMAX, MAGIC, ALU.max, ALU.add))
                return nc.vector.tensor_scalar(out_q, tmp2, MAGIC, None, ALU.subtract)

            for c in range(KC):
                link(quantise(rhs_q[:, c, :], rhs_T[:, c, :], (rhs_scale[:, c:c + 1], rhs_scale[:, 2 + c:3 + c]),
                              rhs_T[:, c, :]))
                last = nc.vector.tensor_scalar(diag[:, c, :], ident[:], rhs_scale[:, c:c + 1], None, ALU.mult)
            last.then_inc(kv_sb, 1)

            for b in range(B):
                dve.wait_ge(kv_ps, 2 + b)
                for n in range(4):
                    ks = range(3 * n, min(3 * n + 3, NCH))
                    m = len(ks) * len(LAYERS)
                    last = nc.vector.tensor_tensor(
                        v_bd[:, b, ks[0]:ks[-1] + 1].rearrange("p k l (s d) -> p (k l) s d", d=VW)[:, :, :, 0:ATT],
                        kv_bank(4 * (1 - b) + n)[:, 0:m * SLOTS * ATT].rearrange("p (m s d) -> p m s d", s=SLOTS, d=ATT),
                        rep(slot_mask[:, ks[0]:ks[-1] + 1].rearrange("p k l s -> p (k l) s"), ATT), ALU.mult)
                last.then_inc(kv_sb, 1)
            dve.wait_ge(gathered, 16 * NT)
            for tl in range(NT):
                last = nc.vector.tensor_tensor(x_all[:, tl, :], rows0[tl], x_all[:, tl, :], ALU.add)
            link(last)

            def prep2(b):
                dve.nop(nofuse=True)
                for l in LAYERS:
                    for c in range(KC):
                        src = k_all[:, bass.ds(b, 1), c, l - 1, :].to_broadcast([P, 4, J])
                        last = nc.vector.tensor_tensor(k_bd[:, l - 1, c, :].rearrange("p (q j) -> p q j", j=J), src,
                                                       rep(head_mask[:], J), ALU.mult)
                last.then_inc(k_built, 1)

            def stats2(s, r):
                ln_stats(s, r)

            def apply2(k):
                def step(s, r):
                    if k == 1 and r:
                        dve.wait_ge(streams[s].xn_stored, 16 * (b * ROUNDS + (ROUNDS * B + r)))
                    ln_apply(s, r, 2, 6 * r + k)
                return step

            def half2(l, half):
                def step(s, r):
                    st = streams[s]
                    masked = l == 3 or (s == 0 and r == 0)
                    if masked:
                        k = r + 1 if s else (3 + r if l == 3 else l)
                        dve.wait_ge(st.filled.sem, st.filled.at(2, b, k))
                        dve.nop(nofuse=True)
                    for a in range(2):
                        src, dst = psum_scores(s)[:, a], sbuf_scores(s, half)[:, a]
                        dve.wait_ge(st.s_ps.sem, st.s_ps.at(2, b, 12 * r + 4 * l - 4 + 2 * half + a + 1))
                        if masked:
                            dve.nop(nofuse=True)
                            m = (filled_mask[s] if l == 3 else causal)[:]
                            link(nc.vector.copy_predicated(dst, m.unsqueeze(1).to_broadcast([P, 4, J]), src))
                            src = dst
                        m = mx[s][:, 8 * half + 4 * a:8 * half + 4 * a + 4]
                        link(nc.vector.tensor_reduce(out=m, in_=src, axis=X, op=ALU.max))
                        nc.vector.tensor_tensor(dst, src, rep(m, J), ALU.subtract).then_inc(st.p_sub.sem, 1)
                return step

            def attended(l):
                def step(s, r):
                    st = streams[s]
                    dve.wait_ge(st.o_ps.sem, st.o_ps.at(2, b, 3 * r + l))
                    av = ps[s][:, 0, 0:H * VW].rearrange("p (h d) -> p h d", d=VW)
                    link(nc.vector.reciprocal(mx[s][:], av[:, :, ATT]))
                    nc.vector.tensor_tensor(xn[s][:].rearrange("p (h d) -> p h d", d=ATT), av[:, :, 0:ATT],
                                            rep(mx[s][:], ATT), ALU.mult).then_inc(st.o.sem, 1)
                return step

            def residual2(k):
                def step(s, r):
                    st = streams[s]
                    dve.wait_ge(st.y_ps.sem, st.y_ps.at(2, b, 6 * r + k))
                    if k == 6:
                        nc.vector.tensor_copy(logits3[:, bass.ds(tile(b, s, r), 1), :].rearrange("p a d -> p (a d)"),
                                              ps[s][:, 0, 0:E3]).then_inc(st.x_new.sem, 1)
                        return
                    y = ps[s][:, 0, 0:D]
                    if k == 4:
                        link(nc.vector.scalar_tensor_tensor(out=xn[s][:], in0=y, scalar=scale[s][:, 0:1],
                                                            in1=rhs_scale_row[:], op0=ALU.mult, op1=ALU.mult))
                        y = xn[s][:]
                    nc.vector.tensor_tensor(x_tile(b, s, r), y, x_tile(b, s, r), ALU.add).then_inc(st.x_new.sem, 1)
                    dve.wait_ge(st.x_new.sem, st.x_new.at(2, b, 6 * r + k))
                return step

            def quant(s, r):
                st = streams[s]
                dve.wait_ge(st.xn.sem, st.xn.at(2, b, 6 * r + 4))
                quantise(x_q[s][:], xn[s][:], (scale[s][:, 0:1], scale[s][:, 1:2]), xn[s][:]).then_inc(st.fm.sem, 1)

            own = {"engine": DV}
            for l in LAYERS:
                own |= {f"stats{l}": stats2, f"fstats{l}": stats2, f"apply{l}": apply2(2 * l - 1), f"fapply{l}": apply2(2 * l)}
                own |= {f"half0_{l}": half2(l, 0), f"half1_{l}": half2(l, 1), f"av{l}": attended(l),
                        f"out{l}": residual2(2 * l - 1)}
            own |= dict(fout1=residual2(2), fout2=residual2(4), gate3=residual2(6), quant2=quant)
            with dve.Fori(0, B) as b:
                link.enter(b, DVE_LINKS2)
                prep2(b)
                for f, s, r in order(STEPS2, own):
                    f(s, r)
                for s in range(STREAMS):
                    dve.wait_ge(streams[s].xn_stored, 16 * (b * ROUNDS + ROUNDS * (B + 1)))
            link.leave(B)

            for s in range(STREAMS):
                dve.wait_ge(streams[s].x_new.sem, streams[s].x_new.at(2, B - 1, 12))
            routing(logits3[:], E3, True)
            loads(E3, NB3, MS3)
            with dve.Fori(0, PASSES[3]) as i:
                for n in range(2):
                    for s in range(MS3):
                        st = streams[s]
                        dve.wait_ge(st.f.sem, st.f.at(3, i, n + 1))
                        nc.vector.tensor_tensor(
                            hid3[s][:, 4 * n:4 * n + 4, :].rearrange("p a n -> p (a n)"), ps[2 * s + (n + 1) % 2][:, 1, :],
                            act3[s][:], ALU.mult).then_inc(st.fm.sem, 1)
                for s in range(MS3):
                    st = streams[s]
                    dve.wait_ge(st.y_ps.sem, st.y_ps.at(3, i, 1))
                    dve.wait_ge(st.y_out, 16 * i + 16 * PASSES[1])
                    nc.vector.tensor_copy(y3[s][:], ps[2 * s + 1][:, 0, 0:D])\
                        .then_inc(st.x_new.sem, 1)
            per = NT // GROUPS
            for g in range(GROUPS):
                dve.wait_ge(gathered3[g], 16 * 2 * per)
                for n in range(2):
                    for tl in range(g * per, (g + 1) * per):
                        last = nc.vector.scalar_tensor_tensor(out=x_all[:, tl, :], in0=rows3[n][:, tl, :],
                                                              scalar=route[:, 2 + n, tl:tl + 1], in1=x_all[:, tl, :],
                                                              op0=ALU.mult, op1=ALU.add)
                    if n == 0:
                        link(last)
                last.then_inc(combined, 1)

        @block.tensor
        def _(pe):
            mm = nc.tensor.matmul
            pe.sem_inc(prep_ps.sem, 1)
            def prep(b):
                pe.wait_ge(ctx_ready, b + 1)
                for s in range(STREAMS):
                    pe.wait_ge(streams[s].x_new.sem, streams[s].x_new.at(0, b, 0))
                for n, (w, arrived) in enumerate(((wk0, "k"), (wv0, "v"))):
                    pe.wait_ge(loaded[arrived], 32)
                    for c in range(C0):
                        for kc in range(KC):
                            last = mm(ps[n][:, c // 4, c % 4 * J:c % 4 * J + J], w[:, kc, c * P:c * P + P],
                                      ctx_b[:, kc, :], start=kc == 0, stop=kc == KC - 1)
                    last.then_inc((prep_ps.sem, v_ps)[n], 1)
                pe.wait_ge(loaded["qT"], 16)
                for n, (kc, half) in enumerate(((0, 0), (0, 1), (1, 0), (1, 1))):
                    pe.wait_ge(prep_sb.sem, prep_sb.at(0, b, 1))
                    if n == 3:
                        pe.wait_ge(vT_ready, b + 1)
                    pair = (2 + n) % 4
                    for par in range(2):
                        for c in range(4):
                            last = mm(ps[pair][:, par, c * J:c * J + J],
                                      wqT0[D0 * par:D0 * par + D0, 4 * half + c, kc * P:kc * P + P],
                                      kT0[D0 * par:D0 * par + D0, 4 * half + c, :], start=True, stop=True)
                    last.then_inc(prep_ps.sem, 1)
                pe.wait_ge(loaded["o"], 16)
                for n in range(3):
                    pe.wait_ge(prep_sb.sem, prep_sb.at(0, b, 2 + n))
                    pair = (2 + n) % 4
                    for k in range(4 * n, min(4 * n + 4, NCH)):
                        m = P if k < NCH - 1 else LAST_CH
                        cs = [c for c in range(C0) if c * 2 * J < k * P + P and (c + 1) * 2 * J > k * P]
                        for i, c in enumerate(cs):
                            at = c * 3 * P + k * P - window(c)
                            last = mm(ps[pair][0:m, k % 4 // 2, k % 2 * D:k % 2 * D + D], vT0[:, at:at + m],
                                      wo0[:, c, :], start=i == 0, stop=i == len(cs) - 1)
                    last.then_inc(prep_ps.sem, 1)
                pe.wait_ge(prep_sb.sem, prep_sb.at(0, b, 5))
                pe.wait_ge(rel_const, 1)
                for g in range(4):
                    for par in range(2):
                        last = mm(ps[1][:, g // 2, g % 2 * D:g % 2 * D + D], relv_m[:, par, :], wo0[:, 2 * g + par, :],
                                  start=par == 0, stop=par == 1)
                last.then_inc(prep_ps.sem, 1)
                pe.wait_ge(prep_sb.sem, prep_sb.at(0, b, 9))

            def xn_T(s, st_sem, value):
                st = streams[s]
                pe.wait_ge(st_sem, value)
                for c in range(KC):
                    last = nc.tensor.transpose(ps[s][:, 0, c * P:c * P + P], xn[s][:, c * P:c * P + P], ident[:])
                last.then_inc(st.xnT_ps.sem, 1)

            def xnT1(s, r):
                xn_T(s, streams[s].xn.sem, streams[s].xn.at(0, b, 2 * r + 1))

            def xnT2(s, r):
                xn_T(s, streams[s].xn.sem, streams[s].xn.at(0, b, 2 * r + 2))

            def rel_scores(s, r):
                if s or r:
                    return
                st = streams[0]
                pe.wait_ge(loaded["rel"], 48)
                pe.wait_ge(st.xnT.sem, st.xnT.at(0, b, 1))
                for c in range(C0):
                    for kc in range(KC):
                        last = mm(ps[0][:, c // 4, c % 4 * P:c % 4 * P + P], wq0[:, kc, c * P:c * P + P],
                                  xnT[0][:, kc, :], start=kc == 0, stop=kc == KC - 1)
                last.then_inc(st.q_ps.sem, 1)
                for g in range(4):
                    pe.wait_ge(st.q.sem, st.q.at(0, b, 1 + g))
                    for par in range(2):
                        for c in range(2):
                            last = mm(ps[0][:, par, c * EXT:c * EXT + EXT],
                                      qT0[D0 * par:D0 * par + D0, 2 * g + c, :],
                                      relk_ext[D0 * par:D0 * par + D0, :], start=True, stop=True)
                    last.then_inc(st.q_ps.sem, 1)
                pe.wait_ge(st.q.sem, st.q.at(0, b, 5))

            def scores(s, r, half):
                st = streams[s]
                if half == 0:
                    pe.wait_ge(st.xnT.sem, st.xnT.at(0, b, 2 * r + 1))
                for a in range(2):
                    if half == 1:
                        pe.wait_ge(st.p_sub.sem, st.p_sub.at(0, b, 4 * r + a + 1))
                    at = half * HALF + a * QUART
                    for kc in range(KC):
                        last = mm(ps[s][:, a, 0:QUART], xnT[s][:, kc, :], qk0[:, kc, at:at + QUART],
                                  start=kc == 0, stop=kc == KC - 1)
                    last.then_inc(st.s_ps.sem, 1)

            def scores0(s, r):
                scores(s, r, 0)

            def scores1(s, r):
                scores(s, r, 1)

            def probs_T(s, phase, n, step):
                st = streams[s]
                if step == 1:
                    pe.wait_ge(st.pT.sem, st.pT.at(phase, b, 3 * n + 1))
                elif phase == 0:
                    pe.wait_ge(st.o.sem, st.o.at(0, b, n + 1))
                else:
                    pe.wait_ge(st.p_exp.sem, st.p_exp.at(2, b, 2 * n + 2))
                for part in ((0, 1), (2,))[step]:
                    for k in range(4 * part, min(4 * part + 4, NCH)):
                        m = P if k < NCH - 1 else LAST_CH
                        last = nc.tensor.transpose(ps[s][0:m, part % 2, k % 4 * P:k % 4 * P + P],
                                                   probs[s][:, k * P:k * P + m], ident[:])
                    last.then_inc(st.pT_ps.sem, 1)

            def pT0(s, r):
                probs_T(s, 0, r, 0)

            def pT1(s, r):
                probs_T(s, 0, r, 1)

            def band_T(s, r):
                if s or r:
                    return
                st = streams[0]
                pe.wait_ge(st.pT.sem, st.pT.at(0, b, 3))
                pe.wait_ge(band_in, 16 * b + 16)
                pe.wait_ge(band_tail, b + 1)
                for g in range(4):
                    last = nc.tensor.transpose(ps[0][:, 0, g * P:g * P + P],
                                               band[:, 4 * g:4 * g + 4, :].rearrange("p h e -> p (h e)"), ident[:])
                last.then_inc(st.q_ps.sem, 1)

            def attn_out(s, r):
                st = streams[s]
                first = s == 0 and r == 0
                pe.wait_ge(st.pT.sem, st.pT.at(0, b, 3 * r + 3))
                if first:
                    pe.wait_ge(st.q.sem, st.q.at(0, b, 6))
                    pe.wait_ge(loaded["rest"], 16 * 5)
                y = ps[s][:, 0, 0:D]
                mm(y, ones[:], bo0[:], start=True, stop=False)
                if first:
                    for g in range(4):
                        mm(y, bandT[:, g, :], relvo[:, g, :], start=False, stop=False)
                for k in range(NCH):
                    m = P if k < NCH - 1 else LAST_CH
                    last = mm(y, probsT[s][0:m, k, :], vo0[0:m, k, :], start=False, stop=k == NCH - 1)
                last.then_inc(st.y_ps.sem, 1)

            def gate_up(s, phase, i, k_in, k, wg, wu):
                st = streams[s]
                pe.wait_ge(st.xnT.sem, st.xnT.at(phase, i, k_in))
                for a, w in enumerate((wg, wu)):
                    for f in range(FC0):
                        for kc in range(KC):
                            last = mm(ps[s][:, a, f * P:f * P + P], w[:, kc, f * P:f * P + P], xnT[s][:, kc, :],
                                      start=kc == 0, stop=kc == KC - 1)
                last.then_inc(st.f_ps.sem, 1)

            def ffn_down(s, phase, i, k, wd):
                st = streams[s]
                pe.wait_ge(st.fm.sem, st.fm.at(phase, i, k))
                for f in range(FC0):
                    last = mm(ps[s][:, 0, 0:D], hid[s][:, 1, f * P:f * P + P], wd[:, f, :], start=f == 0, stop=f == FC0 - 1)
                return last

            def shared_out(s, r):
                ffn_down(s, 0, b, r + 1, sdw)
                for kc in range(KC):
                    last = mm(ps[s][:, 1, 0:E0], xnT[s][:, kc, :], gate0[:, kc, :], start=kc == 0, stop=kc == KC - 1)
                last.then_inc(streams[s].y_ps.sem, 1)

            pe.wait_ge(consts, CONSTS)
            with pe.Fori(0, B) as b:
                prep(b)
                for f, s, r in order(STEPS1, dict(engine=PE, apply1=xnT1, rel=rel_scores, half0=scores0, half1=scores1, pT0=pT0,
                                                  pT1=pT1, band=band_T, out1=attn_out, apply2=xnT2,
                                                  gate_up=lambda s, r: gate_up(s, 0, b, 2 * r + 2, r + 1, sgw, suw),
                                                  out2=shared_out)):
                    f(s, r)

            def ranks(n_exp, ready):
                pe.wait_ge(one_hot_ready, ready)
                hot = one_hot[:, 0:NT * n_exp].rearrange("p (n e) -> p n e", e=n_exp)
                rank = ps[0][:, 0, 0:NT * n_exp].rearrange("p (n e) -> p n e", e=n_exp)
                mm(rank, squareb[:], hot, start=True, stop=True, skip_group_check=True)
                for n in range(NT - 1):
                    mm(rank[:, n + 1:NT, :], onesb[:], hot[:, n:n + 1, :].to_broadcast([P, NT - 1 - n, n_exp]),
                       start=False, stop=True, skip_group_check=True)
                for n in range(NT):
                    last = mm(ps[1][:, 0, 0:n_exp], onesb[:], hot[:, n, :], start=n == 0, stop=n == NT - 1)
                last.then_inc(rank_ready, 1)

            ranks(E0, 1)
            pe.wait_ge(routed, 1)
            with pe.Fori(0, PASSES[1]) as i:
                for s in range(STREAMS):
                    st = streams[s]
                    pe.wait_ge(st.x_new.sem, st.x_new.at(1, i, 0))
                    xn_T(s, st.rows_loaded, 16 * i + 16)
                for s in range(STREAMS):
                    st = streams[s]
                    pe.wait_ge(st.in_loaded, 16 * i + 16)
                    gate_up(s, 1, i, 1, 1, w_in0[s][:, 0], w_in0[s][:, 1])
                for s in range(STREAMS):
                    pe.wait_ge(streams[s].out_loaded, 16 * i + 16)
                    ffn_down(s, 1, i, 1, w_out0[s]).then_inc(streams[s].y_ps.sem, 1)

            pe.wait_ge(loaded["p2"], 16 * (12 + 8 + 9))
            pe.wait_ge(rep_ready, 1)
            for s in range(STREAMS):
                pe.wait_ge(streams[s].x_new.sem, streams[s].x_new.at(2, 0, 0))
            for l in LAYERS:
                for c in range(KC):
                    for kc in range(KC):
                        last = mm(kv_bank(l - 1)[:, c * B * J:(c + 1) * B * J], w2["wk", l][:, kc, c * P:c * P + P],
                                  ctx_all[:, kc].rearrange("p b j -> p (b j)"), start=kc == 0, stop=kc == KC - 1)
            last.then_inc(kv_ps, 1)
            for b in range(B):
                if b:
                    pe.wait_ge(kv_sb, 1)
                for k in range(NCH):
                    at, cols = FIRST[k] * ATT, SLOTS * ATT
                    v = kv_bank(4 * (1 - b) + k // 3)[:, k % 3 * 3 * cols:(k % 3 + 1) * 3 * cols]
                    for kc in range(KC):
                        mm(v, ctx_rep[:, kc, b, k * P:k * P + P], wv2[:, kc, :, at:at + cols],
                           start=kc == 0, stop=True, skip_group_check=True)
                    last = mm(v[:, 0:2 * cols], ones[:], bv2[:, :, at:at + cols], start=False, stop=True,
                              skip_group_check=True)
                last.then_inc(kv_ps, 1)
            pe.wait_ge(kv_sb, 3)
            qps = ps[2][:, 0, 0:D].bitcast(BF16).rearrange("p (c n) -> p c n", c=KC)
            for kc in range(KC):
                for c in range(KC):
                    nc.tensor.transpose(qps[:, kc, c * P:c * P + P], rhs_q[:, c, kc * P:kc * P + P], identb[:])
            for c in range(KC):
                last = mm(ps[2][:, 1, c * P:c * P + P], onesq[:], diag[:, c, :], start=True, stop=True)
            last.then_inc(rhs_ps, 1)
            pe.wait_ge(rhs_sb, 1)
            pe.wait_ge(kv_sb, 4)

            def apply_T(k):
                def step(s, r):
                    xn_T(s, streams[s].xn.sem, streams[s].xn.at(2, b, 6 * r + k))
                return step

            def q_proj(l):
                def step(s, r):
                    st = streams[s]
                    pe.wait_ge(st.xnT.sem, st.xnT.at(2, b, 5 * r + {1: 1, 2: 3, 3: 4}[l]))
                    for c in range(KC):
                        for kc in range(KC):
                            last = mm(ps[s][:, 0, c * P:c * P + P], w2["wq", l][:, kc, c * P:c * P + P],
                                      xnT[s][:, kc, :], start=kc == 0, stop=kc == KC - 1)
                    last.then_inc(st.q_ps.sem, 1)
                return step

            def half_scores(l, half):
                def step(s, r):
                    st = streams[s]
                    if half == 0:
                        pe.wait_ge(st.q.sem, st.q.at(2, b, 3 * r + l))
                        if l == 1 and r == 0:
                            pe.wait_ge(k_built, b + 1)
                    for a in range(2):
                        if half == 1:
                            pe.wait_ge(st.p_sub.sem, st.p_sub.at(2, b, 12 * r + 4 * l - 4 + a + 1))
                        mm(ps[s][:, a, 0:QUART], qT[s][D0 * a:D0 * a + D0, half, :],
                           k_bd[D0 * a:D0 * a + D0, l - 1, half, :], start=True, stop=True).then_inc(st.s_ps.sem, 1)
                return step

            def values(l):
                def step(s, r):
                    st = streams[s]
                    pe.wait_ge(st.pT.sem, st.pT.at(2, b, 9 * r + 3 * l))
                    for k in range(NCH):
                        m = P if k < NCH - 1 else LAST_CH
                        last = mm(ps[s][:, 0, FIRST[k] * VW:(FIRST[k] + SLOTS) * VW], probsT[s][0:m, k, :],
                                  v_bd[0:m, bass.ds(b, 1), k, l - 1, :].rearrange("p a n -> p (a n)"), start=k == 0, stop=True, skip_group_check=True)
                    last.then_inc(st.o_ps.sem, 1)
                return step

            def out_T(l):
                def step(s, r):
                    st = streams[s]
                    pe.wait_ge(st.o.sem, st.o.at(2, b, 3 * r + l))
                    for c in range(KC):
                        last = nc.tensor.transpose(ps[s][:, 1, c * P:c * P + P], xn[s][:, c * P:c * P + P], ident[:])
                    last.then_inc(st.oT_ps.sem, 1)
                return step

            def out_proj(l):
                def step(s, r):
                    st = streams[s]
                    pe.wait_ge(st.oT.sem, st.oT.at(2, b, 3 * r + l))
                    if l < 3:
                        mm(ps[s][:, 0, 0:D], ones[:], bo2[l][:], start=True, stop=False)
                    for c in range(KC):
                        last = mm(ps[s][:, 0, 0:D], xnT[s][:, c, :], w2["wo", l][:, c, :],
                                  start=c == 0 and l == 3, stop=c == KC - 1)
                    last.then_inc(st.y_ps.sem, 1)
                return step

            def low(s, r):
                st = streams[s]
                pe.wait_ge(st.xnT.sem, st.xnT.at(2, b, 5 * r + 2))
                for kc in range(KC):
                    last = mm(ps[s][0:LOW, 0, 0:P], u1[:, kc, :], xnT[s][:, kc, :], start=kc == 0, stop=kc == KC - 1)
                last.then_inc(st.f_ps.sem, 1)

            def up(s, r):
                st = streams[s]
                pe.wait_ge(st.f.sem, st.f.at(2, b, 4 * r + 1))
                for f in range(F1 // P):
                    last = mm(ps[s][:, f // 4, f % 4 * P:f % 4 * P + P], v1[:, f * P:f * P + P], low_T[s][0:LOW + 1, :],
                              start=True, stop=True)
                last.then_inc(st.f_ps.sem, 1)

            def low2(s, r):
                st = streams[s]
                pe.wait_ge(st.f.sem, st.f.at(2, b, 4 * r + 2))
                for f in range(F1 // P):
                    last = mm(ps[s][0:LOW, 0, 0:P], u2[:, f, :], probs[s][:, f * P:f * P + P],
                              start=f == 0, stop=f == F1 // P - 1)
                last.then_inc(st.f_ps.sem, 1)

            def low_out(s, r):
                st = streams[s]
                pe.wait_ge(st.f.sem, st.f.at(2, b, 4 * r + 3))
                mm(ps[s][:, 0, 0:D], low_T[s][0:LOW + 1, :], v2[:], start=True, stop=True).then_inc(st.y_ps.sem, 1)

            def quant_T(s, r):
                st = streams[s]
                pe.wait_ge(st.fm.sem, st.fm.at(2, b, r + 1))
                for c in range(KC):
                    last = nc.tensor.transpose(ps[s][:, 0, 0:P].bitcast(BF16)[:, c * P:c * P + P],
                                               x_q[s][:, c * P:c * P + P], identb[:])
                last.then_inc(st.f_ps.sem, 1)

            def quant_out(s, r):
                st = streams[s]
                pe.wait_ge(st.f.sem, st.f.at(2, b, 4 * r + 4))
                for kc in range(KC):
                    last = mm(ps[s][:, 0, 0:D], x_qT[s][:, kc * P:kc * P + P], rhs_qT[:, kc, :],
                              start=kc == 0, stop=kc == KC - 1)
                last.then_inc(st.y_ps.sem, 1)

            def gate(s, r):
                st = streams[s]
                pe.wait_ge(st.xnT.sem, st.xnT.at(2, b, 5 * r + 5))
                for kc in range(KC):
                    last = mm(ps[s][:, 0, 0:E3], xnT[s][:, kc, :], gate3[:, kc, :], start=kc == 0, stop=kc == KC - 1)
                last.then_inc(st.y_ps.sem, 1)

            own = {"engine": PE}
            for l in LAYERS:
                own |= {f"apply{l}": apply_T(2 * l - 1), f"q{l}": q_proj(l), f"av{l}": values(l), f"oT{l}": out_T(l),
                        f"out{l}": out_proj(l)}
                own |= {f"half{h}_{l}": half_scores(l, h) for h in range(2)}
                own |= {f"pT{h}_{l}": (lambda s, r, l=l, h=h: probs_T(s, 2, 3 * r + l - 1, h)) for h in range(2)}
            own |= dict(fapply1=apply_T(2), fapply3=apply_T(6), low1=low, gelu1=up, low21=low2, fout1=low_out,
                        quant2=quant_T, fout2=quant_out, gate3=gate)
            with pe.Fori(0, B) as b:
                for f, s, r in order(STEPS2, own):
                    f(s, r)

            ranks(E3, 2)
            pe.wait_ge(routed, 2)
            with pe.Fori(0, PASSES[3]) as i:
                for s in range(MS3):
                    st = streams[s]
                    pe.wait_ge(st.x_new.sem, st.x_new.at(3, i, 0))
                    pe.wait_ge(st.rows_loaded, 16 * i + 16 * (PASSES[1] + 1))
                    for c in range(KC):
                        last = nc.tensor.transpose(ps[2 * s][:, 0, c * P:c * P + P], x_in[s][:, c * P:c * P + P], ident[:])
                    last.then_inc(st.xnT_ps.sem, 1)
                for n in range(2):
                    for s in range(MS3):
                        st = streams[s]
                        if n == 0:
                            pe.wait_ge(st.in_loaded, 16 * i + 16 * (PASSES[1] + 1))
                            pe.wait_ge(st.xnT.sem, st.xnT.at(3, i, 1))
                        for a in range(2):
                            for f in range(4):
                                for kc in range(KC):
                                    at = (4 * n + f) * P
                                    last = mm(ps[2 * s + 1 - n][:, a, f * BLK:(f + 1) * BLK],
                                              w_in3[s][:, a, kc, at:at + P], x_inT[s][:, kc, :],
                                              start=kc == 0, stop=kc == KC - 1)
                        last.then_inc(st.f_ps.sem, 1)
                for s in range(MS3):
                    st = streams[s]
                    pe.wait_ge(st.fm.sem, st.fm.at(3, i, 2))
                    pe.wait_ge(st.out_loaded, 16 * i + 16 * (PASSES[1] + 1))
                    for f in range(F3 // P):
                        last = mm(ps[2 * s + 1][:, 0, 0:D], hid3[s][:, f, :], w_out3[s][:, f, :],
                                  start=f == 0, stop=f == F3 // P - 1)
                    last.then_inc(st.y_ps.sem, 1)


def kernel(**inputs):
    import concourse.bacc as bacc
    from concourse.bass_utils import run_bass_kernel_spmd

    a = {k: np.asarray(v) for k, v in inputs.items()}

    def rows_of(*ws):
        e, cp, n = ws[0].shape
        return np.stack(ws, 1).reshape(e, len(ws), cp // P, P, n).transpose(0, 3, 1, 2, 4).reshape(e * P, -1)

    relk, relv = a["L0_xattn_rel_k"], a["L0_xattn_rel_v"]
    dist = np.clip(np.arange(EXT) - (P - 1), -MAXREL, MAXREL) + MAXREL
    arrays = {
        "x": a["x"],
        "ctxT": a["ctx_1024"].transpose(2, 0, 1),
        "Wq0": a["L0_xattn_Wq"], "WqT0": a["L0_xattn_Wq"].T, "Wk0": a["L0_xattn_Wk"], "Wv0": a["L0_xattn_Wv"],
        "Wo0": a["L0_xattn_Wo"], "bo0": a["L0_xattn_bo"][None],
        "relk_ext": np.concatenate([relk[dist].T] * 2), "relk_0": np.concatenate([relk[0]] * 2)[:, None],
        "relv_T": np.concatenate([relv[1:].T] * 2), "relv_0": np.concatenate([relv[0]] * 2)[:, None],
        "sgw": a["L0_ffn_shared_gate_w"], "suw": a["L0_ffn_shared_up_w"], "sdw": a["L0_ffn_shared_down_w"],
        "gate0": a["L0_ffn_gate_w"],
        "w_in0": rows_of(a["L0_ffn_routed_gate_w"], a["L0_ffn_routed_up_w"]), "w_out0": rows_of(a["L0_ffn_routed_down_w"]),
        "w_in3": rows_of(a["L3_ffn_w1"].transpose(0, 2, 1), a["L3_ffn_w3"].transpose(0, 2, 1)),
        "w_out3": rows_of(a["L3_ffn_w2"].transpose(0, 2, 1)), "gate3": a["L3_ffn_gate_w"].T,
        "u1": a["L1_ffn_U1"], "u2": a["L1_ffn_U2"],
        "v1": np.concatenate([a["L1_ffn_V1"], a["L1_ffn_b1"][None]]),
        "v2": np.concatenate([a["L1_ffn_V2"], a["L1_ffn_b2"][None]]),
        "rhsT": a["L2_ffn_rhs"].T,
        "mask": np.ascontiguousarray(a["mask_BxSxS2_bk0"].reshape(NT, P, J).transpose(1, 0, 2)).reshape(P, NT * J)
        .view(np.int32),
    }
    for l in (1, 2):
        arrays |= {f"w{n.lower()}{l}": a[f"L{l}_xattn_W{n}"].T for n in "qkvo"}
        arrays |= {f"b{n}{l}": a[f"L{l}_xattn_b{n}"].reshape(KC, P).T for n in "qk"}
        arrays |= {f"b{n}{l}": a[f"L{l}_xattn_b{n}"][None] for n in "vo"}
    arrays |= {f"w{n}3": a[f"L3_xattn_w_{n}"].T for n in "qkvo"}
    p = np.arange(P)
    arrays["head_mask"] = (p[:, None] % D0 // ATT == np.arange(4)).astype(np.float32)
    mask = (P * np.arange(NCH)[:, None] + p[:, None, None]) // J == np.array(FIRST)[:, None] + np.arange(SLOTS)
    arrays["slot_mask"] = np.repeat(mask[:, :, None].astype(np.float32), len(LAYERS), 2)
    arrays["rev"] = np.broadcast_to(np.arange(E0, 0, -1, dtype=np.float32), (P, E0))
    arrays["kstep"] = np.broadcast_to(BLK * np.arange(B * T // BLK, dtype=np.float32), (P, B * T // BLK))
    arrays["blks"] = np.broadcast_to(np.arange(NB0, dtype=np.float32), (P, NB0))
    arrays["row"] = p[:, None].astype(np.float32)
    arrays["low_tri"] = np.broadcast_to(np.tri(E0, dtype=np.float32), (P, E0, E0))
    arrays = {k: np.ascontiguousarray(v) for k, v in arrays.items()}
    nc = bacc.Bacc("TRN2", target_bir_lowering=False, num_devices=1)
    tensors = {k: nc.dram_tensor(k, v.shape, mybir.dt.from_np(v.dtype), kind="ExternalInput").ap()
               for k, v in arrays.items()}
    out = nc.dram_tensor("out", (B, T, D), F32, kind="ExternalOutput")
    build(nc, tensors, out.ap())
    r = run_bass_kernel_spmd(nc, [arrays], core_ids=[0])
    return r.results[0]["out"]
```

```python
import numpy as np
import concourse.bass as bass
from concourse import mybir
from contextlib import ExitStack

P = 128
B, T, D = 2, 1024, 256
J = 77
H = 16
KC = D // P
D0 = 64
INNER = H * D0
C0 = INNER // P
MAXREL = 16
TILES = T // P
STREAMS = 4
ROUNDS = TILES // STREAMS
HJ = H * J
HALF = HJ // 2
QUART = HALF // 2
NCH = -(-HJ // P)
LAST_CH = HJ - P * (NCH - 1)
EXT = P + J - 1
BAND = 2 * MAXREL - 1
PADW = (MAXREL - 1) + J + (P + MAXREL - 1 - J)
NREL = BAND + 1
F0 = 512
FC0 = F0 // P
E0 = 32
EPS = 1e-5
F32 = mybir.dt.float32
BF16 = mybir.dt.bfloat16
I32 = mybir.dt.int32
U32 = mybir.dt.uint32
U8 = mybir.dt.uint8
ALU = mybir.AluOpType
ACT = mybir.ActivationFunctionType
X = mybir.AxisListType.X
STEPS1 = ("stats1", "apply1", "rel", "half0", "half1", "norm", "pT0", "pT1", "band", "out1",
          "stats2", "apply2", "gate_up", "out2")
LAYERS = (1, 2, 3)
STEPS2 = tuple(f"{step}{l}" for l in LAYERS for step in
               ("stats", "apply", "q", "half0_", "half1_", "pT0_", "pT1_", "av", "oT", "out", "fstats", "fapply")
               + (("low", "gelu", "low2", "fout"), ("quant", "fout"), ("gate",))[l - 1])

PE, AC, DV, PO = "pe", "act", "dve", "pool"
STAGES = dict(
    stats=((DV, 0.65), (PO, 0.35)), apply=((DV, 0.35), (PE, 0.25), (AC, 0.3)),
    apply2=((DV, 0.35), (PO, 0, 0.1), (PE, 0.25), (AC, 0.3)), fapply3=((DV, 0.35), (PO, 0, 0.1), (PE, 0.25), (AC, 0.3)),
    q=((PE, 0.9), (PO, 0, 0.1), (AC, 0.4)), q3=((PE, 0.9), (PO, 0, 1.5), (AC, 0.3)),
    half0=((PE, 0.6, 1.1), (DV, 0.9, 1.8)), half1=((PE, 0.6, 1.1), (AC, 0, 0.65, "half0"), (DV, 1.8), (AC, 0.65)),
    pT0=((PE, 0.45, 0.9), (AC, 0.5, 1.0)), pT1=((PE, 0.2), (AC, 0.35)), av=((PE, 2.2), (DV, 0.65)),
    oT=((PE, 0.25), (AC, 0.3)), out=((PE, 1.3), (DV, 0.35)), low=((PE, 0.9), (AC, 0.2)),
    gelu=((PE, 1.8), (AC, 0.95)), down=((PE, 1.8), (AC, 0.2)), fout=((PE, 0.5), (DV, 0.35)),
    quant=((DV, 1.9), (PE, 0.15), (AC, 0.3)), gate=((PE, 0.4), (DV, 0.2)),
    wide_half0=((PE, 1.1, 2.2), (DV, 0.9, 1.8)), norm=((DV, 2.9),),
    wide_half1=((PE, 1.1, 2.2), (AC, 0, 0.65, "half0"), (DV, 1.8), (AC, 0.65)),
    out1=((PE, 4.4), (DV, 0.35)), gate_up=((PE, 3.5), (AC, 0.5), (DV, 1.3)), out2=((PE, 2.2), (DV, 0.5)),
    rel=((PE, 0, 6.0), (AC, 6.0)), band=((PE, 1.0), (AC, 0.6)))
KIND1 = dict(stats1="stats", apply1="apply", half0="wide_half0", half1="wide_half1", stats2="stats")
KIND2 = dict(fstats="stats", fapply="apply", half0_="half0", half1_="half1", pT0_="pT0", pT1_="pT1", low2="down")
HOP1, HOP2 = 0.2, 0.5


def plan(steps):
    chains = []
    for s in range(STREAMS):
        chain = []
        for r in range(ROUNDS):
            for step in steps:
                if step in ("rel", "band") and (s or r):
                    continue
                kind = KIND1.get(step, step) if steps is STEPS1 else (
                    step if step in STAGES else KIND2.get(step[:-1], step[:-1]))
                for stage in STAGES[kind]:
                    engine, time, held, of = (*stage, stage[1], None)[:4] if len(stage) == 2 else (*stage, None)[:4]
                    chain.append((engine, step.replace("half1", of) if of else step, s, r, time, held))
        chains.append(chain)
    free, ready, at = dict.fromkeys((PE, AC, DV, PO), 0.0), [0.0] * STREAMS, [0] * STREAMS
    found = []
    while any(a < len(c) for a, c in zip(at, chains)):
        _, _, s = min((max(free[chains[s][at[s]][0]], ready[s]), ready[s], s)
                      for s in range(STREAMS) if at[s] < len(chains[s]))
        engine, step, _, r, time, held = chains[s][at[s]]
        start = max(free[engine], ready[s])
        free[engine] = start + held
        ready[s] = start + time + ((HOP1 if steps is STEPS1 else HOP2) if time else 0)
        at[s] += 1
        found.append((engine, step, s, r))
    return found


POOL_LINKS1, POOL_LINKS2 = 16, 48
DVE_LINKS1, DVE_LINKS2 = 78, 256

ATT = 16
SLOTS = 3
VW = ATT + 1
FIRST = [min(P * k // J, H - SLOTS) for k in range(NCH)]
REPS = -(-P * NCH // J)
LOW, F1 = 64, 1024
F3 = 1024
E3 = 8
JITTER = 0.01
NEVER, MASKED = -3.0e38, -1.0e9
MAGIC = 1.5 * 2.0 ** 23
QMAX = 127.0
BLK = P
NB0 = B * T // BLK + E0
NB3 = 2 * B * T // BLK + E3
MS3 = 2
GROUPS = 4
PASSES = (B, NB0 // STREAMS, B, NB3 // MS3)
ROWS = NB0 * BLK
NT = B * TILES
PLAN = {steps: plan(steps) for steps in (STEPS1, STEPS2)}


def window(c):
    return 2 * J * c // P * P


class Count:

    def __init__(self, sem, per_pass, start=0):
        self.sem, self.per_pass = sem, per_pass
        self.base = [start + sum(m * n for m, n in zip(PASSES[:i], per_pass)) for i in range(len(per_pass))]

    def at(self, phase, i, k):
        return i * self.per_pass[phase] + (self.base[phase] + k)


class Links:

    def __init__(self, eng, sem):
        self.eng, self.sem, self.done, self.n, self.i, self.per_pass = eng, sem, 0, 0, 0, 0

    def enter(self, i, per_pass):
        self.done, self.n, self.i, self.per_pass = self.done + self.n, 0, i, per_pass

    def leave(self, passes):
        assert self.n == self.per_pass, ("links in a pass:", self.n)
        self.done, self.n, self.i, self.per_pass = self.done + passes * self.n, 0, 0, 0

    def __call__(self, ins):
        self.n += 1
        ins.then_inc(self.sem, 1)
        self.eng.wait_ge(self.sem, self.i * self.per_pass + (self.done + self.n))


def build(nc, t, out):
    ctx = ExitStack()
    with ctx:
        offset = [nc.sbuf_base + 31 & ~31]

        def sb(name, shape, dt=F32, at=None):
            size = int(np.prod(shape[1:])) * mybir.dt.size(dt)
            size = size + 31 & ~31
            if at is None:
                at = offset[0]
                offset[0] += size
                assert offset[0] <= nc.sbuf_usable_end, (name, offset[0])
            return nc.alloc_sbuf_tensor_at(name, shape, dt, offset=at), at + size

        def keep(name, shape, dt=F32):
            return sb(name, shape, dt)[0]

        def sem(name):
            return ctx.enter_context(nc.semaphore(name))

        x_all = keep("x_all", [P, B * TILES, D])
        ident = keep("ident", [P, P])
        ones = keep("ones", [1, P])
        minus_half = keep("minus_half", [P, 1])
        ctx_all = keep("ctx_all", [P, KC, B, J])
        logits0 = keep("logits0", [P, B * TILES, E0])
        stats = [keep(f"stats{s}", [P, 6]) for s in range(STREAMS)]
        mean_var = [keep(f"mean_var{s}", [P, 2]) for s in range(STREAMS)]
        rstd = [keep(f"rstd{s}", [P, 2]) for s in range(STREAMS)]
        xn = [keep(f"xn{s}", [P, D]) for s in range(STREAMS)]
        xnT = [keep(f"xnT{s}", [P, KC, P]) for s in range(STREAMS)]
        probs = [keep(f"probs{s}", [P, HJ]) for s in range(STREAMS)]
        probsT = [keep(f"probsT{s}", [P, NCH, P]) for s in range(STREAMS)]
        mx = [keep(f"mx{s}", [P, H]) for s in range(STREAMS)]
        qT = [keep(f"qT{s}", [P, KC, P]) for s in range(STREAMS)]
        low_T = [keep(f"low_T{s}", [P, P]) for s in range(STREAMS)]
        filled_mask = [keep(f"filled_mask{s}", [P, J], U8) for s in range(STREAMS)]
        scale = [keep(f"scale{s}", [P, 2]) for s in range(STREAMS)]
        identb, squareb, onesb = (keep(n, [P, P], BF16) for n in ("identb", "squareb", "onesb"))
        onesq = keep("onesq", [P, P])
        causal_f, causal = keep("causal_f", [P, J]), keep("causal", [P, J], U8)
        logits3 = keep("logits3", [P, NT, E3])
        rev, kstep = keep("rev", [P, E0]), keep("kstep", [P, B * T // BLK])
        blks, row = keep("blks", [P, NB0]), keep("row", [P, 1])
        cols, nums = keep("cols", [P, BLK]), keep("nums", [P, 2 * NT])
        low_tri = keep("low_tri", [P, E0, E0])
        one_hot = keep("one_hot", [P, NT * E0], BF16)
        route = keep("route", [P, 8, NT])
        blocks_of = keep("blocks_of", [P, 4, E0])
        slot = keep("slot", [P, 2, NT], I32)
        zeros = keep("zeros", [P, D])
        expert = keep("expert", [P, NB0])
        load_f, load = keep("load_f", [P, NB0]), keep("load", [P, NB0], U32)
        load_now = keep("load_now", [P, 2, STREAMS], U32)
        phase_start = offset[0]

        wq0 = keep("wq0", [P, KC, INNER])
        wqT0 = keep("wqT0", [P, C0, D])
        kv_weights = offset[0]
        wk0 = keep("wk0", [P, KC, INNER])
        wv0 = keep("wv0", [P, KC, INNER])
        kv_weights_end = offset[0]
        wo0 = keep("wo0", [P, C0, D])
        kT0 = keep("kT0", [P, C0, B, J])
        vT_raw = keep("vT_raw", [P, C0, B, J])
        qk0 = keep("qk0", [P, B, KC, HJ])
        vT0 = keep("vT0", [P, C0 * 3 * P + 104])
        vo0 = keep("vo0", [P, NCH, D])
        diag_f = keep("diag_f", [P, P])
        relk_ext = keep("relk_ext", [P, EXT])
        relk_0 = keep("relk_0", [P, 1])
        relv_0 = keep("relv_0", [P, 1])
        relv_T = keep("relv_T", [P, NREL])
        relv_m = keep("relv_m", [P, 2, P])
        relvo = keep("relvo", [P, H // 4, D])
        tail_mask = keep("tail_mask", [P, J])
        rel_q = keep("rel_q", [P, H, EXT])
        band_src = rel_q[:].rearrange("p h e -> p (h e)")[:, 0:H * PADW].rearrange("p (h e) -> p h e", h=H)
        rel_s = keep("rel_s", [P, HJ])
        band = keep("band", [P, H, NREL])
        bandT = keep("bandT", [P, 4, P])
        qT0 = probsT[0][:, 0:C0, :]
        behind = offset[0]
        offset[0] = kv_weights
        sgw = keep("sgw", [P, KC, F0])
        suw = keep("suw", [P, KC, F0])
        sdw = keep("sdw", [P, FC0, D])
        gate0 = keep("gate0", [P, KC, E0])
        assert offset[0] <= kv_weights_end
        offset[0] = behind
        hid = [probs[s][:, 0:2 * F0].rearrange("p (a f) -> p a f", a=2) for s in range(STREAMS)]

        offset[0] = phase_start
        ctx_rep = keep("ctx_rep", [P, KC, B, REPS * J])
        k_all = keep("k_all", [P, B, KC, len(LAYERS), J])
        w2 = {(n, l): keep(f"{n}_{l}", [P, KC, D]) for l in LAYERS for n in ("wq", "wk", "wo")}
        wv2 = keep("wv2", [P, KC, len(LAYERS), D])
        bq2 = {l: keep(f"bq_{l}", [P, KC]) for l in (1, 2)}
        bk2 = {l: keep(f"bk_{l}", [P, KC]) for l in (1, 2)}
        bv2 = keep("bv2", [1, 2, D])
        bo2 = {l: keep(f"bo_{l}", [1, D]) for l in (1, 2)}
        head_mask, slot_mask = keep("head_mask", [P, 4]), keep("slot_mask", [P, NCH, len(LAYERS), SLOTS])
        u1, v1 = keep("u1", [P, KC, LOW]), keep("v1", [LOW + 1, F1])
        u2, v2 = keep("u2", [P, F1 // P, LOW]), keep("v2", [LOW + 1, D])
        rhs_T, rhs_q = keep("rhs_T", [P, KC, D]), keep("rhs_q", [P, KC, D], BF16)
        rhs_qT = keep("rhs_qT", [P, KC, D], BF16)
        rhs_scale, rhs_scale_row = keep("rhs_scale", [P, 2 * KC]), keep("rhs_scale_row", [P, D])
        diag = keep("diag", [P, KC, P])
        x_q = [keep(f"x_q{s}", [P, D], BF16) for s in range(STREAMS)]
        x_qT = [keep(f"x_qT{s}", [P, D], BF16) for s in range(STREAMS)]
        mask_in, unmasked = keep("mask_in", [P, NT * J // 4], I32), keep("unmasked", [P, NT, J], U8)
        gate3 = keep("gate3", [P, KC, E3])
        moe_start = offset[0]
        k_bd = keep("k_bd", [P, len(LAYERS), KC, 4 * J])
        v_bd = keep("v_bd", [P, B, NCH, len(LAYERS), SLOTS * VW])
        offset[0] = moe_start
        w_in0 = [keep(f"w_in0{s}", [P, 2, KC, F0]) for s in range(STREAMS)]
        w_out0 = [keep(f"w_out0{s}", [P, FC0, D]) for s in range(STREAMS)]
        y_sb = [qT[s][:].rearrange("p c n -> p (c n)") for s in range(STREAMS)]
        rows0 = [probsT[n // 4][:].rearrange("p c n -> p (c n)")[:, n % 4 * D:(n % 4 + 1) * D] for n in range(NT)]
        offset[0] = moe_start
        w_in3 = [keep(f"w_in3{s}", [P, 2, KC, F3]) for s in range(MS3)]
        w_out3 = [keep(f"w_out3{s}", [P, F3 // P, D]) for s in range(MS3)]
        offset[0] = phase_start
        picks_start = offset[0]
        rows3 = [keep(f"rows3{n}", [P, NT, D]) for n in range(2)]
        x_in = [keep(f"x_in{s}", [P, D]) for s in range(MS3)]
        x_inT = [keep(f"x_inT{s}", [P, KC, BLK]) for s in range(MS3)]
        act3 = [keep(f"act3{s}", [P, 4 * BLK]) for s in range(MS3)]
        hid3 = [keep(f"hid3{s}", [P, F3 // P, BLK]) for s in range(MS3)]
        y3 = [keep(f"y3{s}", [P, D]) for s in range(MS3)]
        id_now = [keep(f"id_now{s}", [P, 2], U32) for s in range(MS3)]
        row_id, row_slot = keep("row_id", [P, NB3], U32), keep("row_slot", [P, NB3], U32)
        ids = keep("ids", [P, 4, NB3])
        assert offset[0] <= moe_start, (offset[0], moe_start)
        offset[0] = picks_start
        place_hot = keep("place_hot", [P, 2 * NT, BLK], BF16)
        block_hot = keep("block_hot", [P, 2 * NT, NB3])
        block_ids = keep("block_ids", [P, 2 * NT, 2 * NB3], BF16)
        place, blk_of = keep("place", [P, 2 * NT]), keep("blk_of", [P, 2 * NT])

        sorted_dram = nc.dram_tensor("sorted_dram", [ROWS, D], F32)
        y_dram = nc.dram_tensor("y_dram", [ROWS, D], F32)
        y3_dram = nc.dram_tensor("y3_dram", [2 * B * T, D], F32)
        xn3_dram = nc.dram_tensor("xn3_dram", [B * T, D], F32)
        rel_dram = nc.dram_tensor("rel_dram", [P * H * EXT + P], F32)
        band_dram = nc.dram_tensor("band_dram", [P * H * PADW + P], F32)
        xn0_dram = nc.dram_tensor("xn0_dram", [B * T, D], F32)

        ps = [ctx.enter_context(nc.psum_tensor(f"ps{s}", [P, 2, 512], F32)) for s in range(STREAMS)]

        class Stream:
            def __init__(self, s):
                def count(name, *per_pass, start=0):
                    return Count(sem(f"{name}{s}"), per_pass, start)

                first = s == 0
                self.aggr, self.rstd = count("aggr", 4, 0, 12, 0), count("rstd", 4, 0, 12, 0)
                self.xn, self.xn_stored = count("xn", 4, 0, 12, 0), sem(f"xn_stored{s}")
                self.xnT_ps, self.xnT = count("xnT_ps", 4, 1, 10, 1), count("xnT", 4, 1, 10, 1)
                self.q_ps = count("q_ps", 6 * first, 0, 6, 0)
                self.q = count("q", 6 * first, 0, 6, 0)
                self.s_ps, self.filled = count("s_ps", 8, 0, 24, 0), count("filled", 0, 0, 2 + 2 * first, 0)
                self.p_sub, self.p_exp = count("p_sub", 8, 0, 24, 0), count("p_exp", 4, 0, 12, 0)
                self.pT_ps, self.pT = count("pT_ps", 6, 0, 18, 0), count("pT", 6, 0, 18, 0)
                self.o_ps, self.o = count("o_ps", 0, 0, 6, 0), count("o", 2, 0, 6, 0)
                self.oT_ps, self.oT = count("oT_ps", 0, 0, 6, 0), count("oT", 0, 0, 6, 0)
                self.f_ps, self.f, self.fm = count("f_ps", 2, 1, 8, 2), count("f", 2, 1, 8, 2), count("fm", 2, 1, 2, 2)
                self.y_ps, self.x_new = count("y_ps", 4, 1, 12, 1), count("x_new", 4, 1, 12, 1, start=1)
                self.in_loaded, self.out_loaded, self.rows_loaded, self.y_out = (
                    sem(f"{name}{s}") for name in ("in_loaded", "out_loaded", "rows_loaded", "y_out"))

        streams = [Stream(s) for s in range(STREAMS)]
        loaded = {n: sem(f"loaded_{n}") for n in ("x0", "x1", "ctx", "k", "v", "qT", "o", "rel", "rest",
                                                 "shape", "p2", "xn")}
        rhs_ps, rhs_sb = sem("rhs_ps"), sem("rhs_sb")
        top_ready, score_exp = sem("top_ready"), sem("score_exp")
        one_hot_ready, rank_ready, routed, scaled = sem("one_hot_ready"), sem("rank_ready"), sem("routed"), sem("scaled")
        zero_out, combined = sem("zero_out"), sem("combined")
        loads_ready = sem("loads_ready")
        kv_ps, kv_sb, k_built = sem("kv_ps"), sem("kv_sb"), sem("k_built")
        scattered, gathered, rep_ready = sem("scattered"), sem("gathered"), sem("rep_ready")
        gathered3 = [sem(f"gathered3_{n}") for n in range(GROUPS)]
        rows3_loaded = [streams[MS3 + s].in_loaded for s in range(MS3)]
        results3 = [streams[MS3 + s].out_loaded for s in range(MS3)]
        consts, CONSTS = sem("consts"), 9 + 2 * STREAMS
        kq_ps, kq_sb = sem("kq_ps"), sem("kq_sb")
        prep_ps, prep_sb = Count(sem("prep_ps"), (3, 0, 0, 0)), Count(sem("prep_sb"), (3, 0, 0, 0))
        vT_ready = sem("vT_ready")
        rel_const = sem("rel_const")
        rel_out, rel_in = sem("rel_out"), sem("rel_in")
        band_ready, band_out, band_in = sem("band_ready"), sem("band_out"), sem("band_in")
        band_tail = sem("band_tail")
        dve_link, pool_link = sem("dve_link"), sem("pool_link")
        stored = sem("stored")
        block = ctx.enter_context(nc.Block())

        def order(steps, own):
            for engine, step, s, r in PLAN[steps]:
                if engine == own["engine"] and step in own:
                    yield own[step], s, r

        def kv_bank(n):
            return ps[n // 2][:, n % 2, :]

        def tile(b, s, r):
            return b * TILES + (r * STREAMS + s)

        def x_tile(b, s, r):
            return x_all[:, bass.ds(tile(b, s, r), 1), :].rearrange("p a d -> p (a d)")

        def rep(ap, n):
            return ap.unsqueeze(len(ap.shape)).to_broadcast([*ap.shape, n])

        def heads4(ap):
            return ap.rearrange("p r (q j) -> p r q j", j=J)

        def psum_scores(s):
            return heads4(ps[s][:, :, 0:QUART])

        def sbuf_scores(s, half):
            return heads4(probs[s][:, half * HALF:(half + 1) * HALF].rearrange("p (r n) -> p r n", r=2))

        @block.sync
        def _(sp):
            sp.dma_start(ctx_all[:], t["ctxT"].rearrange("(c p) b j -> p c b j", p=P)).then_inc(loaded["ctx"], 16)
            sp.dma_start(wk0[:], t["Wk0"].rearrange("(c p) n -> p c n", p=P)).then_inc(loaded["k"], 16)
            sp.dma_start(relk_0[:], t["relk_0"]).then_inc(loaded["k"], 16)
            sp.dma_start(wv0[:], t["Wv0"].rearrange("(c p) n -> p c n", p=P)).then_inc(loaded["v"], 16)
            sp.dma_start(relv_0[:], t["relv_0"]).then_inc(loaded["v"], 16)
            sp.dma_start(wqT0[:], t["WqT0"].rearrange("(c p) n -> p c n", p=P)).then_inc(loaded["qT"], 16)
            sp.dma_start(wo0[:], t["Wo0"].rearrange("(c p) n -> p c n", p=P)).then_inc(loaded["o"], 16)
            sp.dma_start(relk_ext[:], t["relk_ext"]).then_inc(loaded["rel"], 16)
            sp.dma_start(relv_T[:], t["relv_T"]).then_inc(loaded["rel"], 16)
            sp.dma_start(x_all[:, 0:TILES, :], t["x"][0].rearrange("(n p) d -> p n d", p=P)).then_inc(loaded["x0"], 16)
            sp.dma_start(wq0[:], t["Wq0"].rearrange("(c p) n -> p c n", p=P)).then_inc(loaded["rel"], 16)
            sp.dma_start(vo0[LAST_CH:LAST_CH + 1, NCH - 1, :], t["bo0"]).then_inc(loaded["rest"], 16)
            sp.wait_ge(kq_ps, 2)
            for dst, src in ((sgw, "sgw"), (suw, "suw"), (sdw, "sdw"), (gate0, "gate0")):
                sp.dma_start(dst[:], t[src].rearrange("(c p) n -> p c n", p=P)).then_inc(loaded["rest"], 16)
            sp.dma_start(x_all[:, TILES:, :], t["x"][1].rearrange("(n p) d -> p n d", p=P)).then_inc(loaded["x1"], 16)
            for dst, src in ((rev, "rev"), (kstep, "kstep"), (blks, "blks"), (row, "row"), (cols, "cols"),
                             (nums, "nums"), (low_tri, "low_tri")):
                sp.dma_start(dst[:], t[src]).then_inc(loaded["shape"], 16)
            sp.wait_ge(consts, CONSTS)
            for n in range(ROWS // (8 * P)):
                sp.dma_start(sorted_dram[n * 8 * P:(n + 1) * 8 * P, :].rearrange("(p a) d -> p a d", a=8),
                             zeros[:].unsqueeze(1).to_broadcast([P, 8, D])).then_inc(zero_out, 16)
            with sp.Fori(0, B) as b:
                s0 = streams[0]
                sp.wait_ge(s0.q.sem, s0.q.at(0, b, 5))
                sp.dma_start(rel_dram[0:P * H * EXT].rearrange("(p n) -> p n", p=P),
                             rel_q[:].rearrange("p h e -> p (h e)")).then_inc(rel_out, 16)
                sp.wait_ge(rel_out, 16 * b + 16)
                sp.dma_start(rel_s[:].rearrange("p (h j) -> p h j", h=H),
                             bass.AP(rel_dram, P - 1, [[H * EXT - 1, P], [EXT, H], [1, J]])).then_inc(rel_in, 16)
                sp.wait_ge(band_ready, b + 1)
                sp.dma_start(band_dram[0:P * H * PADW].rearrange("(p n) -> p n", p=P),
                             band_src.rearrange("p h e -> p (h e)")).then_inc(band_out, 16)
                sp.wait_ge(band_out, 16 * b + 16)
                sp.dma_start(band[:, :, 0:BAND],
                             bass.AP(band_dram, 0, [[H * PADW + 1, P], [PADW, H], [1, BAND]])).then_inc(band_in, 16)
            for s in range(STREAMS):
                sp.wait_ge(streams[s].x_new.sem, streams[s].x_new.at(0, B - 1, 4))
            for s in range(STREAMS):
                sp.wait_ge(streams[s].xn_stored, 16 * ROUNDS * B)
            for n in range(4):
                sp.dma_start(probsT[n][:].rearrange("p c n -> p (c n)")[:, 0:4 * D].rearrange("p (n d) -> p n d", d=D),
                             xn0_dram[n * 4 * P:(n + 1) * 4 * P, :].rearrange("(n p) d -> p n d", p=P))\
                    .then_inc(loaded["xn"], 16)
            for l in LAYERS:
                for n in ("wq", "wk", "wo"):
                    sp.dma_start(w2[n, l][:], t[f"{n}{l}"].rearrange("(c p) n -> p c n", p=P)).then_inc(loaded["p2"], 16)
                sp.dma_start(wv2[:, :, l - 1, :], t[f"wv{l}"].rearrange("(c p) n -> p c n", p=P)).then_inc(loaded["p2"], 16)
                if l < 3:
                    sp.dma_start(bv2[:, l - 1, :], t[f"bv{l}"]).then_inc(loaded["p2"], 16)
                    for n, d in (("bq", bq2), ("bk", bk2), ("bo", bo2)):
                        sp.dma_start(d[l][:], t[f"{n}{l}"]).then_inc(loaded["p2"], 16)
            for dst, src in ((head_mask, "head_mask"), (slot_mask, "slot_mask"), (v1, "v1"), (v2, "v2")):
                sp.dma_start(dst[:], t[src]).then_inc(loaded["p2"], 16)
            for dst, src in ((u1, "u1"), (u2, "u2"), (rhs_T, "rhsT"), (gate3, "gate3")):
                sp.dma_start(dst[:], t[src].rearrange("(c p) n -> p c n", p=P)).then_inc(loaded["p2"], 16)
            sp.dma_start(mask_in[:], t["mask"]).then_inc(loaded["p2"], 16)

            def rows_in(s, i, value):
                st = streams[s]
                sp.wait_ge(st.xnT_ps.sem, value)
                sp.dma_start(xn[s][:], sorted_dram[bass.ds((i + s * PASSES[1]) * BLK, BLK), :])\
                    .then_inc(st.rows_loaded, 16)

            def results_out(s, i):
                st = streams[s]
                sp.wait_ge(st.x_new.sem, st.x_new.at(1, i, 1))
                sp.dma_start(y_dram[bass.ds((i + s * PASSES[1]) * BLK, BLK), :], y_sb[s]).then_inc(st.y_out, 16)

            sp.wait_ge(scattered, 16 * NT)
            for s in range(STREAMS):
                rows_in(s, 0, streams[s].xnT_ps.at(1, 0, 0))
            with sp.Fori(0, PASSES[1] - 1) as i:
                for s in range(STREAMS):
                    rows_in(s, i + 1, streams[s].xnT_ps.at(1, i, 1))
                for s in range(STREAMS):
                    results_out(s, i)
            for s in range(STREAMS):
                results_out(s, PASSES[1] - 1)
            for s in range(MS3):
                sp.wait_ge(results3[s], 16 * (PASSES[1] + PASSES[3]))
            for g in range(GROUPS):
                for n in range(2):
                    at = (n * GROUPS + g) * (NT // GROUPS) * P
                    sp.dma_start(rows3[n][:, g * (NT // GROUPS):(g + 1) * (NT // GROUPS), :],
                                 y3_dram[at:at + NT // GROUPS * P, :].rearrange("(n p) d -> p n d", p=P))\
                        .then_inc(gathered3[g], 16)
            per = NT // GROUPS
            for g in range(GROUPS):
                sp.wait_ge(combined, g + 1)
                sp.dma_start(out.rearrange("b (n p) d -> p (b n) d", p=P)[:, g * per:(g + 1) * per, :],
                             x_all[:, g * per:(g + 1) * per, :]).then_inc(stored, 16)
            sp.wait_ge(stored, 16 * GROUPS)

        @block.gpsimd
        def _(pool):
            link = Links(pool, pool_link)
            nc.gpsimd.memset(zeros[:], 0.0).then_inc(consts, 1)
            link(nc.gpsimd.memset(ident[:], 0.0))
            nc.gpsimd.affine_select(out=ident[:], in_=ident[:], compare_op=ALU.not_equal, fill=1.0, base=0,
                                    pattern=[[-1, P]], channel_multiplier=1).then_inc(consts, 1)
            nc.gpsimd.memset(ones[:], 1.0).then_inc(consts, 1)
            nc.gpsimd.memset(minus_half[:], -0.5).then_inc(consts, 1)
            nc.gpsimd.memset(vT0[:], 0.0).then_inc(consts, 1)
            link(nc.gpsimd.memset(tail_mask[:], 1.0))
            nc.gpsimd.affine_select(out=tail_mask[:], in_=tail_mask[:], compare_op=ALU.is_ge, fill=0.0,
                                    base=-MAXREL, pattern=[[1, J]], channel_multiplier=-1).then_inc(consts, 1)

            link(nc.gpsimd.memset(causal_f[:], 1.0))
            nc.gpsimd.affine_select(out=causal_f[:], in_=causal_f[:], compare_op=ALU.is_ge, fill=0.0, base=0,
                                    pattern=[[-1, J]], channel_multiplier=1).then_inc(consts, 1)
            link(nc.gpsimd.memset(diag_f[:], 1.0))
            nc.gpsimd.affine_select(out=diag_f[:], in_=diag_f[:], compare_op=ALU.is_gt, fill=0.0, base=0,
                                    pattern=[[1, P]], channel_multiplier=-1).then_inc(consts, 1)
            nc.gpsimd.memset(onesq[:], 1.0).then_inc(consts, 1)
            for s in range(STREAMS):
                nc.gpsimd.memset(low_T[s][:], 1.0).then_inc(consts, 1)
                nc.gpsimd.memset(probsT[s][:, NCH - 1, :], 1.0).then_inc(consts, 1)

            def ln_rstd(s, phase, k):
                st = streams[s]
                pool.wait_ge(st.aggr.sem, st.aggr.at(phase, b, k))
                pool.nop(nofuse=True)
                link(nc.gpsimd.tensor_scalar(rstd[s][:, 1:2], mean_var[s][:, 1:2], EPS, None, ALU.add))
                nc.gpsimd.tensor_tensor(rstd[s][:, 0:1], rstd[s][:, 1:2], minus_half[:], ALU.pow)\
                    .then_inc(st.rstd.sem, 1)

            def ln1(s, r):
                ln_rstd(s, 0, 2 * r + 1)

            def ln2(s, r):
                ln_rstd(s, 0, 2 * r + 2)

            def xn_store(s, r):
                st = streams[s]
                pool.wait_ge(st.xn.sem, st.xn.at(0, b, 2 * r + 2))
                pool.dma_start(xn0_dram[bass.ds(tile(b, s, r) * P, P), :], xn[s][:]).then_inc(st.xn_stored, 16)

            with pool.Fori(0, B) as b:
                link.enter(b, POOL_LINKS1)
                for f, s, r in order(STEPS1, dict(engine=PO, stats1=ln1, stats2=ln2, apply2=xn_store)):
                    f(s, r)
            link.leave(B)

            def scatter(row, n, tl):
                pool.indirect_dma_start(out=sorted_dram[:], out_offset=bass.IndirectOffsetOnAxis(
                    ap=slot[:, n, tl:tl + 1], axis=0), in_=row, in_offset=None).then_inc(scattered, 16)

            def gather(row, n, tl, done):
                pool.indirect_dma_start(out=row, out_offset=None, in_=y_dram[:],
                                        in_offset=bass.IndirectOffsetOnAxis(ap=slot[:, n, tl:tl + 1], axis=0))\
                    .then_inc(done, 16)

            def load_weights(i, phase, n_streams, w_in, w_out, src_in, src_out, n_exp):
                for n, (w, src) in enumerate(((w_in, src_in), (w_out, src_out))):
                    for s in range(n_streams):
                        st = streams[s]
                        last = (st.f_ps, st.y_ps)[n]
                        pool.wait_ge(last.sem, last.at(phase, i, 0))
                        pool.nop(nofuse=True)
                        link(nc.gpsimd.tensor_copy(load_now[:, n, s:s + 1], load[:, bass.ds(i + s * PASSES[phase], 1)]))
                        pool.nop(nofuse=True)
                        pool.indirect_dma_start(
                            out=w[s][:].rearrange("p a c n -> p (a c n)" if n == 0 else "p c n -> p (c n)"),
                            out_offset=None, in_=t[src],
                            in_offset=bass.IndirectOffsetOnAxis(ap=load_now[:, n, s:s + 1], axis=0),
                            bounds_check=n_exp * P - 1, oob_is_err=False).then_inc((st.in_loaded, st.out_loaded)[n], 16)

            pool.wait_ge(zero_out, 16 * (ROWS // (8 * P)))
            pool.wait_ge(routed, 1)
            for tl in range(NT):
                pool.wait_ge(scaled, tl + 1)
                scatter(rows0[tl], 0, tl)
            weights0 = STREAMS, w_in0, w_out0, "w_in0", "w_out0", E0
            pool.wait_ge(loads_ready, 1)
            load_weights(0, 1, *weights0)
            with pool.Fori(1, PASSES[1]) as i:
                link.enter(i - 1, 2 * STREAMS)
                load_weights(i, 1, *weights0)
            link.leave(PASSES[1] - 1)
            for s in range(STREAMS):
                pool.wait_ge(streams[s].y_out, 16 * PASSES[1])
            for tl in range(NT):
                gather(rows0[tl], 0, tl, gathered)

            def rstd2(k):
                return lambda s, r: ln_rstd(s, 2, 6 * r + k)

            def fill(l):
                def step(s, r):
                    st = streams[s]
                    if l < 3 and (s or r):
                        return
                    pool.wait_ge(st.q_ps.sem, st.q_ps.at(2, b, 3 * r + l))
                    pool.nop(nofuse=True)
                    ins = nc.gpsimd.memset(probs[s][:], NEVER if l < 3 else MASKED * 4)
                    if l == 3:
                        ins = nc.gpsimd.tensor_copy(
                            filled_mask[s][:], unmasked[:, bass.ds(tile(b, s, r), 1), :].rearrange("p a j -> p (a j)"))
                    ins.then_inc(st.filled.sem, 1)
                return step

            def xn_store2(s, r):
                st = streams[s]
                pool.wait_ge(st.xn.sem, st.xn.at(2, b, 6 * r + 6))
                pool.dma_start(xn3_dram[bass.ds(tile(b, s, r) * P, P), :], xn[s][:]).then_inc(st.xn_stored, 16)

            own = {f"stats{l}": rstd2(2 * l - 1) for l in LAYERS}
            own |= {f"fstats{l}": rstd2(2 * l) for l in LAYERS} | {f"q{l}": fill(l) for l in LAYERS}
            with pool.Fori(0, B) as b:
                link.enter(b, POOL_LINKS2)
                for f, s, r in order(STEPS2, own | dict(engine=PO, fapply3=xn_store2)):
                    f(s, r)
            link.leave(B)

            def index(s, n, table, i):
                pool.nop(nofuse=True)
                link(nc.gpsimd.tensor_copy(id_now[s][:, n:n + 1], table[:, bass.ds(i + s * PASSES[3], 1)]))
                pool.nop(nofuse=True)
                return bass.IndirectOffsetOnAxis(ap=id_now[s][:, n:n + 1], axis=0)

            def rows_in(s, i, value):
                pool.wait_ge(streams[s].xnT_ps.sem, value)
                pool.indirect_dma_start(out=x_in[s][:], out_offset=None, in_=xn3_dram[:], in_offset=index(s, 0, row_id, i))\
                    .then_inc(rows3_loaded[s], 16)

            def results_out(s, i):
                pool.wait_ge(streams[s].x_new.sem, streams[s].x_new.at(3, i, 1))
                at = index(s, 1, row_slot, i)
                pool.indirect_dma_start(out=y3_dram[:], out_offset=at, in_=y3[s][:], in_offset=None,
                                        bounds_check=2 * B * T - 1, oob_is_err=False).then_inc(results3[s], 16)

            weights3 = MS3, w_in3, w_out3, "w_in3", "w_out3", E3
            pool.wait_ge(loads_ready, 2)
            load_weights(0, 3, *weights3)
            for s in range(STREAMS):
                pool.wait_ge(streams[s].xn_stored, 16 * 2 * ROUNDS * B)
            pool.wait_ge(loads_ready, 3)
            for s in range(MS3):
                rows_in(s, 0, streams[s].xnT_ps.at(3, 0, 0))
            with pool.Fori(0, PASSES[3] - 1) as i:
                link.enter(i, 4 * MS3)
                for s in range(MS3):
                    rows_in(s, i + 1, streams[s].xnT_ps.at(3, i, 1))
                load_weights(i + 1, 3, *weights3)
                for s in range(MS3):
                    results_out(s, i)
            link.leave(PASSES[3] - 1)
            for s in range(MS3):
                results_out(s, PASSES[3] - 1)

        def act_copy(dst, src):
            return nc.scalar.activation(dst, src, ACT.Copy)

        @block.scalar
        def _(act):
            act.wait_ge(consts, CONSTS)
            act.wait_ge(loaded["k"], 32)
            act.wait_ge(loaded["v"], 32)
            for n, (dst, bias) in enumerate(((kT0, relk_0), (vT_raw, relv_0))):
                act.wait_ge(kq_ps, 1 + n)
                for a in range(4):
                    last = nc.scalar.activation(
                        dst[:, 2 * a:2 * a + 2].rearrange("p c b j -> p (c b j)"),
                        ps[2 * n + a // 2][:, a % 2, 0:2 * B * J], ACT.Identity, bias=bias[:])
                last.then_inc(kq_sb, 1)
            for n in range(2 * C0 // 2):
                kc, two = n // 4, n % 4
                act.wait_ge(kq_ps, 3 + n)
                for par in range(2):
                    dst = qk0[:, :, kc, 4 * two * J:4 * (two + 1) * J].rearrange("p b (c r j) -> p r c b j", r=2, j=J)
                    last = act_copy(dst[:, par], ps[n % 4][:, par, 0:2 * B * J].rearrange("p (c b j) -> p c b j", c=2, b=B))
                last.then_inc(kq_sb, 1)
            act.wait_ge(kq_ps, 11)
            act_copy(relvo[:].rearrange("p g n -> p (g n)"), ps[0][:].rearrange("p a n -> p (a n)")).then_inc(kq_sb, 1)

            def prep(b):
                for n in range(3):
                    act.wait_ge(prep_ps.sem, prep_ps.at(0, b, 1 + n))
                    pair = 1 + n
                    if n < 2:
                        last = act_copy(vo0[:, 4 * n:4 * n + 4, :].rearrange("p (a g) n -> p a (g n)", a=2), ps[pair][:])
                    else:
                        act_copy(vo0[:, 8, :], ps[pair][:, 0, 0:D])
                        last = act_copy(vo0[0:LAST_CH, 9, :], ps[pair][0:LAST_CH, 0, D:2 * D])
                    last.then_inc(prep_sb.sem, 1)

            def xn_T(s, phase, i, k):
                st = streams[s]
                act.wait_ge(st.xnT_ps.sem, st.xnT_ps.at(phase, i, k))
                act_copy(xnT[s][:].rearrange("p c n -> p (c n)"), ps[s][:, 0, 0:D]).then_inc(st.xnT.sem, 1)

            def xnT1(s, r):
                xn_T(s, 0, b, 2 * r + 1)

            def xnT2(s, r):
                xn_T(s, 0, b, 2 * r + 2)

            def rel_scores(s, r):
                if s or r:
                    return
                st = streams[0]
                act.wait_ge(st.q_ps.sem, st.q_ps.at(0, b, 1))
                act_copy(qT0.rearrange("p (a c) n -> p a (c n)", a=2), ps[0][:]).then_inc(st.q.sem, 1)
                for g in range(4):
                    act.wait_ge(st.q_ps.sem, st.q_ps.at(0, b, 2 + g))
                    for par in range(2):
                        last = act_copy(rel_q[:, 4 * g:4 * g + 4, :].rearrange("p (c r) e -> p r c e", r=2)[:, par],
                                        ps[0][:, par, 0:2 * EXT].rearrange("p (c e) -> p c e", e=EXT))
                    last.then_inc(st.q.sem, 1)

            def exp(s, phase, k, half):
                st = streams[s]
                act.wait_ge(st.p_sub.sem, st.p_sub.at(phase, b, 2 * k))
                part = probs[s][:, half * HALF:(half + 1) * HALF]
                nc.scalar.activation(part, part, ACT.Exp, scale=(D0 if phase == 0 else ATT) ** -0.5)\
                    .then_inc(st.p_exp.sem, 1)

            def exp0(s, r):
                exp(s, 0, 2 * r + 1, 0)

            def exp1(s, r):
                exp(s, 0, 2 * r + 2, 1)

            def probs_T(s, phase, n, step):
                st = streams[s]
                flat = probsT[s][:].rearrange("p c n -> p (c n)")
                for part in ((0, 1), (2,))[step]:
                    act.wait_ge(st.pT_ps.sem, st.pT_ps.at(phase, b, 3 * n + part + 1))
                    if part < 2:
                        last = act_copy(flat[:, part * 512:(part + 1) * 512], ps[s][:, part, :])
                    else:
                        act_copy(flat[:, 1024:1152], ps[s][:, 0, 0:P])
                        last = act_copy(flat[0:LAST_CH, 1152:1280], ps[s][0:LAST_CH, 0, P:2 * P])
                    last.then_inc(st.pT.sem, 1)

            def pT0(s, r):
                probs_T(s, 0, r, 0)

            def pT1(s, r):
                probs_T(s, 0, r, 1)

            def band_T(s, r):
                if s or r:
                    return
                st = streams[0]
                act.wait_ge(st.q_ps.sem, st.q_ps.at(0, b, 6))
                act_copy(bandT[:].rearrange("p c n -> p (c n)"), ps[0][:, 0, :]).then_inc(st.q.sem, 1)

            def gate_tanh(s, r):
                st = streams[s]
                act.wait_ge(st.f_ps.sem, st.f_ps.at(0, b, r + 1))
                nc.scalar.activation(hid[s][:, 0, :], ps[s][:, 0, :], ACT.Tanh, scale=0.5).then_inc(st.f.sem, 1)

            def gate_act(s, phase, i, k):
                st = streams[s]
                act.wait_ge(st.f_ps.sem, st.f_ps.at(phase, i, k))
                nc.scalar.activation(hid[s][:, 0, :], ps[s][:, 0, :], ACT.Silu).then_inc(st.f.sem, 1)

            with act.Fori(0, B) as b:
                prep(b)
                for f, s, r in order(STEPS1, dict(engine=AC, apply1=xnT1, rel=rel_scores, half0=exp0, half1=exp1,
                                                  pT0=pT0, pT1=pT1,
                                                  band=band_T, apply2=xnT2, gate_up=gate_tanh)):
                    f(s, r)

            for s in range(STREAMS):
                act.wait_ge(streams[s].x_new.sem, streams[s].x_new.at(0, B - 1, 4))
            for kc in range(KC):
                for b in range(B):
                    last = act_copy(ctx_rep[:, kc, b, :].rearrange("p (n j) -> p n j", j=J),
                                    ctx_all[:, kc, b:b + 1, :].to_broadcast([P, REPS, J]))
            last.then_inc(rep_ready, 1)
            act.wait_ge(top_ready, 1)
            nc.scalar.activation(route[:, 1, :], route[:, 0, :], ACT.Exp, scale=-1.0).then_inc(score_exp, 1)
            with act.Fori(0, PASSES[1]) as i:
                for s in range(STREAMS):
                    xn_T(s, 1, i, 1)
                for s in range(STREAMS):
                    gate_act(s, 1, i, 1)

            act.wait_ge(rhs_ps, 1)
            act_copy(rhs_qT[:].rearrange("p c n -> p (c n)"), ps[2][:, 0, 0:D].bitcast(BF16))
            act_copy(rhs_scale_row[:], ps[2][:, 1, 0:D]).then_inc(rhs_sb, 1)

            def xnT_of(n):
                return lambda s, r: xn_T(s, 2, b, 5 * r + n)

            def q_T(l):
                def step(s, r):
                    st = streams[s]
                    act.wait_ge(st.q_ps.sem, st.q_ps.at(2, b, 3 * r + l))
                    if l == 3:
                        last = act_copy(qT[s][:].rearrange("p c n -> p (c n)"), ps[s][:, 0, 0:D])
                    else:
                        for c in range(KC):
                            last = nc.scalar.activation(qT[s][:, c, :], ps[s][:, 0, c * P:c * P + P], ACT.Identity,
                                                        bias=bq2[l][:, c:c + 1])
                    last.then_inc(st.q.sem, 1)
                return step

            def out_T(l):
                def step(s, r):
                    st = streams[s]
                    act.wait_ge(st.oT_ps.sem, st.oT_ps.at(2, b, 3 * r + l))
                    act_copy(xnT[s][:].rearrange("p c n -> p (c n)"), ps[s][:, 1, 0:D]).then_inc(st.oT.sem, 1)
                return step

            def low_copy(n):
                def step(s, r):
                    st = streams[s]
                    act.wait_ge(st.f_ps.sem, st.f_ps.at(2, b, 4 * r + n))
                    act_copy(low_T[s][0:LOW, :], ps[s][0:LOW, 0, 0:P]).then_inc(st.f.sem, 1)
                return step

            def gelu(s, r):
                st = streams[s]
                act.wait_ge(st.f_ps.sem, st.f_ps.at(2, b, 4 * r + 2))
                nc.scalar.activation(probs[s][:, 0:F1], ps[s][:].rearrange("p a n -> p (a n)"), ACT.Gelu_apprx_tanh)\
                    .then_inc(st.f.sem, 1)

            def quant_T(s, r):
                st = streams[s]
                act.wait_ge(st.f_ps.sem, st.f_ps.at(2, b, 4 * r + 4))
                act_copy(x_qT[s][:], ps[s][:, 0, 0:P].bitcast(BF16)).then_inc(st.f.sem, 1)

            own = {"engine": AC}
            for l in LAYERS:
                own |= {f"apply{l}": xnT_of({1: 1, 2: 3, 3: 4}[l]), f"q{l}": q_T(l), f"oT{l}": out_T(l)}
                own |= {f"half{h}_{l}": (lambda s, r, l=l, h=h: exp(s, 2, 6 * r + 2 * l - 1 + h, h)) for h in range(2)}
                own |= {f"pT{h}_{l}": (lambda s, r, l=l, h=h: probs_T(s, 2, 3 * r + l - 1, h)) for h in range(2)}
            own |= dict(fapply1=xnT_of(2), fapply3=xnT_of(5), low1=low_copy(1), gelu1=gelu, low21=low_copy(3), quant2=quant_T)
            with act.Fori(0, B) as b:
                for f, s, r in order(STEPS2, own):
                    f(s, r)

            act.wait_ge(top_ready, 2)
            e1, e2 = (probs[0][:, n * NT * E3:(n + 1) * NT * E3] for n in (2, 3))
            nc.scalar.activation(e1, e1, ACT.Exp, scale=-1.0)
            nc.scalar.activation(e2, e2, ACT.Exp).then_inc(score_exp, 1)
            with act.Fori(0, PASSES[3]) as i:
                for s in range(MS3):
                    st = streams[s]
                    act.wait_ge(st.xnT_ps.sem, st.xnT_ps.at(3, i, 1))
                    act_copy(x_inT[s][:].rearrange("p c n -> p (c n)"), ps[2 * s][:, 0, 0:D]).then_inc(st.xnT.sem, 1)
                for n in range(2):
                    for s in range(MS3):
                        st = streams[s]
                        act.wait_ge(st.f_ps.sem, st.f_ps.at(3, i, n + 1))
                        if n:
                            act.wait_ge(st.fm.sem, st.fm.at(3, i, n))
                        nc.scalar.activation(act3[s][:], ps[2 * s + (n + 1) % 2][:, 0, :], ACT.Silu).then_inc(st.f.sem, 1)

        @block.vector
        def _(dve):
            link = Links(dve, dve_link)
            for s in range(STREAMS):
                dve.sem_inc(streams[s].x_new.sem, 1)
            dve.wait_ge(loaded["k"], 32)
            dve.wait_ge(loaded["v"], 32)
            dve.wait_ge(loaded["rel"], 48)
            nc.vector.tensor_scalar(relk_ext[:], relk_ext[:], relk_0[:], None, ALU.subtract)
            link(nc.vector.memset(relv_m[:], 0.0))
            for par in range(2):
                for r in range(2):
                    at = (2 * par + r) * NREL
                    last = nc.vector.tensor_scalar(relv_m[D0 * r:D0 * r + D0, par, at:at + NREL],
                                                   relv_T[D0 * r:D0 * r + D0, :], relv_0[D0 * r:D0 * r + D0, :],
                                                   None, ALU.subtract)
            last.then_inc(rel_const, 1)
            dve.wait_ge(consts, CONSTS)
            nc.vector.tensor_copy(causal[:], causal_f[:])
            nc.vector.tensor_copy(squareb[:], diag_f[:])
            nc.vector.tensor_copy(onesb[:], onesq[:])

            def ln_stats(s, r):
                if s == 0:
                    dve.wait_ge(loaded["x1" if r else "x0"], 16)
                dve.nop(nofuse=True)
                link(nc.vector.bn_stats(stats[s][:], x_tile(b, s, r)))
                dve.nop(nofuse=True)
                nc.vector.bn_aggr(mean_var[s][:], stats[s][:]).then_inc(streams[s].aggr.sem, 1)

            def ln_apply(s, r, phase, k):
                st = streams[s]
                dve.wait_ge(st.rstd.sem, st.rstd.at(phase, b, k))
                nc.vector.tensor_scalar(xn[s][:], x_tile(b, s, r), mean_var[s][:, 0:1], rstd[s][:, 0:1],
                                        ALU.subtract, ALU.mult).then_inc(st.xn.sem, 1)

            def ln1a(s, r):
                ln_stats(s, r)

            def ln1b(s, r):
                if r:
                    dve.wait_ge(streams[s].xn_stored, 16 * (b * ROUNDS + r))
                ln_apply(s, r, 0, 2 * r + 1)

            def ln2a(s, r):
                ln_stats(s, r)

            def ln2b(s, r):
                ln_apply(s, r, 0, 2 * r + 2)

            def softmax_half(s, r, half):
                st = streams[s]
                for a in range(2):
                    dve.wait_ge(st.s_ps.sem, st.s_ps.at(0, b, 4 * r + 2 * half + a + 1))
                    src, dst = psum_scores(s)[:, a], sbuf_scores(s, half)[:, a]
                    if s == 0 and r == 0:
                        if half == 0:
                            dve.wait_ge(rel_in, 16 * b + 16)
                        rel = heads4(rel_s[:, half * HALF:(half + 1) * HALF].rearrange("p (r n) -> p r n", r=2))[:, a]
                        link(nc.vector.tensor_tensor(dst, src, rel, ALU.add))
                        src = dst
                    m = mx[s][:, 8 * half + 4 * a:8 * half + 4 * a + 4]
                    link(nc.vector.tensor_reduce(out=m, in_=src, axis=X, op=ALU.max))
                    nc.vector.tensor_tensor(dst, src, rep(m, J), ALU.subtract).then_inc(st.p_sub.sem, 1)

            def soft0(s, r):
                softmax_half(s, r, 0)

            def soft1(s, r):
                softmax_half(s, r, 1)

            def normalise(s, r):
                st = streams[s]
                dve.wait_ge(st.p_exp.sem, st.p_exp.at(0, b, 2 * r + 2))
                p3 = probs[s][:].rearrange("p (h j) -> p h j", j=J)
                link(nc.vector.tensor_reduce(out=mx[s][:], in_=p3, axis=X, op=ALU.add))
                link(nc.vector.reciprocal(mx[s][:], mx[s][:]))
                ins = nc.vector.tensor_tensor(p3, p3, rep(mx[s][:], J), ALU.mult)
                ins.then_inc(st.o.sem, 1)
                if s == 0 and r == 0:
                    dve.wait_ge(st.o.sem, st.o.at(0, b, 1))
                    link(nc.vector.memset(band_src, 0.0))
                    nc.vector.tensor_copy(band_src[:, :, MAXREL - 1:MAXREL - 1 + J], p3).then_inc(band_ready, 1)
                    tail = rel_s[:].rearrange("p (h j) -> p h j", j=J)
                    link(nc.vector.tensor_tensor(tail, p3, tail_mask[:].unsqueeze(1).to_broadcast([P, H, J]), ALU.mult))
                    nc.vector.tensor_reduce(out=band[:, :, BAND], in_=tail, axis=X, op=ALU.add).then_inc(band_tail, 1)

            def residual(s, r, u):
                st = streams[s]
                dve.wait_ge(st.y_ps.sem, st.y_ps.at(0, b, 2 * r + u + 1))
                if u:
                    nc.vector.tensor_copy(logits0[:, bass.ds(tile(b, s, r), 1), :].rearrange("p a d -> p (a d)"),
                                          ps[s][:, 1, 0:E0])
                ins = nc.vector.tensor_tensor(x_tile(b, s, r), ps[s][:, 0, 0:D], x_tile(b, s, r), ALU.add)
                ins.then_inc(st.x_new.sem, 1)
                dve.wait_ge(st.x_new.sem, st.x_new.at(0, b, 2 * r + u + 1))

            def res1(s, r):
                residual(s, r, 0)

            def res2(s, r):
                residual(s, r, 1)

            def gate_up(s, r):
                st = streams[s]
                dve.wait_ge(st.f.sem, st.f.at(0, b, r + 1))
                link(nc.vector.scalar_tensor_tensor(out=hid[s][:, 0, :], in0=hid[s][:, 0, :], scalar=1.0, in1=ps[s][:, 0, :],
                                                    op0=ALU.add, op1=ALU.mult))
                nc.vector.scalar_tensor_tensor(out=hid[s][:, 1, :], in0=hid[s][:, 0, :], scalar=0.5, in1=ps[s][:, 1, :],
                                               op0=ALU.mult, op1=ALU.mult).then_inc(st.fm.sem, 1)

            dve.wait_ge(consts, CONSTS)
            nc.vector.tensor_copy(identb[:], ident[:])

            def prep(b):
                dve.wait_ge(kq_sb, 11)
                dve.nop(nofuse=True)
                for c in range(C0):
                    for r in range(2):
                        at = c * 3 * P + (2 * c + r) * J - window(c)
                        last = nc.vector.tensor_copy(
                            vT0[D0 * r:D0 * r + D0, at:at + J],
                            vT_raw[D0 * r:D0 * r + D0, c, bass.ds(b, 1), :].rearrange("p a j -> p (a j)"))
                last.then_inc(vT_ready, 1)

            with dve.Fori(0, B) as b:
                link.enter(b, DVE_LINKS1)
                prep(b)
                for f, s, r in order(STEPS1, dict(engine=DV, stats1=ln1a, apply1=ln1b, half0=soft0, half1=soft1, norm=normalise,
                                                  out1=res1, stats2=ln2a, apply2=ln2b, gate_up=gate_up, out2=res2)):
                    f(s, r)
                for s in range(STREAMS):
                    dve.wait_ge(streams[s].xn_stored, 16 * (b * ROUNDS + ROUNDS))
            link.leave(B)

            def routing(logits, n_exp, top2):
                size = NT * n_exp
                tmp = {0: probs[0][:, 0:size], 7: probs[2][:, 0:size]}
                if top2:
                    tmp |= {n: probs[0][:, n * size:(n + 1) * size] for n in range(8)}
                tmp = {n: x.rearrange("p (n e) -> p n e", e=n_exp) for n, x in tmp.items()}
                tmp.setdefault(5, tmp[7])
                revs = rev[:, E0 - n_exp:E0].unsqueeze(1).to_broadcast([P, NT, n_exp])
                tt, tr = nc.vector.tensor_tensor, nc.vector.tensor_reduce

                def top(scores, best, hot):
                    link(tr(out=best, in_=scores, axis=X, op=ALU.max))
                    link(tt(tmp[7], scores, rep(best, n_exp), ALU.is_equal))
                    link(tt(tmp[7], tmp[7], revs, ALU.mult))
                    link(tr(out=route[:, 7, :], in_=tmp[7], axis=X, op=ALU.max))
                    link(tt(hot, tmp[7], rep(route[:, 7, :], n_exp), ALU.is_equal))

                hots = [tmp[0], tmp[1]] if top2 else [tmp[0]]
                m1, m2 = route[:, 0, :], route[:, 1, :]
                top(logits, route[:, 0, :], hots[0])
                if not top2:
                    nc.vector.tensor_copy(one_hot[:].rearrange("p (n e) -> p n e", e=n_exp), hots[0])\
                        .then_inc(one_hot_ready, 1)
                    nc.vector.tensor_copy(route[:, 5, :], route[:, 0, :]).then_inc(top_ready, 1)
                    dve.wait_ge(score_exp, 1)
                    link(nc.vector.tensor_scalar_add(route[:, 1, :], route[:, 1, :], 1.0))
                    link(nc.vector.reciprocal(route[:, 1, :], route[:, 1, :]))
                else:
                    link(nc.vector.scalar_tensor_tensor(out=tmp[4], in0=hots[0], scalar=NEVER, in1=logits,
                                                        op0=ALU.mult, op1=ALU.add))
                    top(tmp[4], route[:, 1, :], hots[1])
                    oh = one_hot[:, 0:NT * n_exp].rearrange("p (n e) -> p n e", e=n_exp)
                    tt(oh, hots[0], hots[1], ALU.add).then_inc(one_hot_ready, 1)
                    for n, best in ((2, m1), (3, m2)):
                        link(nc.vector.scalar_tensor_tensor(out=tmp[5 + n - 2], in0=logits, scalar=-1.0, in1=logits,
                                                            op0=ALU.mult, op1=ALU.max))
                        link(tt(tmp[5 + n - 2], tmp[5 + n - 2], rep(best, n_exp), ALU.max))
                        link(tt(tmp[7], rep(best, n_exp), logits, ALU.subtract))
                        if n == 2:
                            nc.vector.tensor_copy(tmp[2], tmp[7])
                        link(nc.vector.scalar_tensor_tensor(out=tmp[5 + n - 2], in0=tmp[5 + n - 2], scalar=2 * JITTER,
                                                            in1=tmp[7], op0=ALU.mult, op1=ALU.is_ge))
                    tt(tmp[3], tmp[4], rep(m2, n_exp), ALU.subtract).then_inc(top_ready, 1)
                    dve.wait_ge(score_exp, 2)
                    for n in range(2):
                        link(tt(tmp[2 + n], tmp[2 + n], tmp[5 + n], ALU.mult))
                        link(tr(out=route[:, 2 + n, :], in_=tmp[2 + n], axis=X, op=ALU.add))
                        link(nc.vector.reciprocal(route[:, 2 + n, :], route[:, 2 + n, :]))
                dve.wait_ge(rank_ready, 2 if top2 else 1)
                nblk, end, start = (blocks_of[:, n, 0:n_exp] for n in range(3))
                n_step = B * T // BLK
                big = probs[1][:]
                cmp = big[:, 0:n_exp * n_step].rearrange("p (e k) -> p e k", k=n_step)
                link(tt(cmp, rep(ps[1][:, 0, 0:n_exp], n_step),
                        kstep[:].unsqueeze(1).to_broadcast([P, n_exp, n_step]), ALU.is_gt))
                link(tr(out=nblk, in_=cmp, axis=X, op=ALU.add))
                tri = big[:, 0:n_exp * n_exp].rearrange("p (e f) -> p e f", f=n_exp)
                link(tt(tri, nblk.unsqueeze(1).to_broadcast([P, n_exp, n_exp]), low_tri[:, 0:n_exp, 0:n_exp], ALU.mult))
                link(tr(out=end, in_=tri, axis=X, op=ALU.add))
                link(tt(start, end, nblk, ALU.subtract))
                link(nc.vector.scalar_tensor_tensor(
                    out=tmp[7], in0=start.unsqueeze(1).to_broadcast([P, NT, n_exp]), scalar=float(BLK),
                    in1=ps[0][:, 0, 0:NT * n_exp].rearrange("p (n e) -> p n e", e=n_exp), op0=ALU.mult, op1=ALU.add))
                for n, hot in enumerate(hots):
                    link(tt(tmp[5 + n], tmp[7], hot, ALU.mult))
                    link(tr(out=route[:, 5 + n, :], in_=tmp[5 + n], axis=X, op=ALU.add))
                    last = nc.vector.tensor_copy(slot[:, n, :], route[:, 5 + n, :])
                last.then_inc(routed, 1)

            def loads(n_exp, n_blocks, n_streams):
                tt, tr, end = nc.vector.tensor_tensor, nc.vector.tensor_reduce, blocks_of[:, 1, 0:n_exp]
                big = probs[1][:]
                half = n_blocks // 2
                for n in range(2):
                    out3 = big[:, 0:half * n_exp].rearrange("p (k e) -> p k e", e=n_exp)
                    link(tt(out3, end.unsqueeze(1).to_broadcast([P, half, n_exp]),
                            rep(blks[:, n * half:(n + 1) * half], n_exp), ALU.is_le))
                    link(tr(out=expert[:, n * half:(n + 1) * half], in_=out3, axis=X, op=ALU.add))
                e, ld = expert[:, 0:n_blocks], load_f[:, 0:n_blocks]
                link(tt(ld[:, 1:], e[:, 1:], e[:, 0:n_blocks - 1], ALU.is_equal))
                link(nc.vector.scalar_tensor_tensor(out=ld[:, 1:], in0=ld[:, 1:], scalar=float(n_exp), in1=e[:, 1:],
                                                    op0=ALU.mult, op1=ALU.add))
                first = ld.rearrange("p (s i) -> p s i", i=n_blocks // n_streams)[:, :, 0]
                link(nc.vector.tensor_scalar(first, e.rearrange("p (s i) -> p s i", i=n_blocks // n_streams)[:, :, 0],
                                             float(n_exp - 1), None, ALU.min))
                link(nc.vector.tensor_scalar(ld, ld, float(P), row[:], ALU.mult, ALU.add))
                nc.vector.tensor_copy(load[:, 0:n_blocks], ld).then_inc(loads_ready, 1)

            dve.wait_ge(loaded["shape"], 16 * 7)
            routing(logits0[:], E0, False)
            dve.wait_ge(loaded["xn"], 16 * 4)
            for tl in range(NT):
                nc.vector.tensor_scalar(rows0[tl], rows0[tl], route[:, 1, tl:tl + 1], None, ALU.mult).then_inc(scaled, 1)
            loads(E0, NB0, STREAMS)

            def expert_mul(s, phase, i, k):
                st = streams[s]
                dve.wait_ge(st.f.sem, st.f.at(phase, i, k))
                nc.vector.tensor_tensor(hid[s][:, 1, :], ps[s][:, 1, :], hid[s][:, 0, :], ALU.mult).then_inc(st.fm.sem, 1)

            def expert_pass(i, first):
                for s in range(STREAMS):
                    expert_mul(s, 1, i, 1)
                for s in range(STREAMS):
                    st = streams[s]
                    dve.wait_ge(st.y_ps.sem, st.y_ps.at(1, i, 1))
                    if not first:
                        dve.wait_ge(st.y_out, 16 * i)
                    nc.vector.tensor_copy(y_sb[s], ps[s][:, 0, 0:D]).then_inc(st.x_new.sem, 1)

            expert_pass(0, True)
            with dve.Fori(1, PASSES[1]) as i:
                expert_pass(i, False)
            dve.wait_ge(loaded["p2"], 16 * (12 + 8 + 9))
            nc.vector.tensor_scalar(unmasked[:].rearrange("p n j -> p (n j)"), mask_in[:].bitcast(U8), 0.0, None, ALU.is_equal)
            nc.vector.tensor_copy(v_bd[:, 0].rearrange("p k l (s d) -> p (k l) s d", d=VW)[:, :, :, ATT],
                                  slot_mask[:].rearrange("p k l s -> p (k l) s"))
            nc.vector.tensor_copy(v_bd[:, 1].rearrange("p k l (s d) -> p (k l) s d", d=VW)[:, :, :, ATT],
                                  slot_mask[:].rearrange("p k l s -> p (k l) s"))
            dve.wait_ge(kv_ps, 1)
            for l in LAYERS:
                for c in range(KC):
                    src = kv_bank(l - 1)[:, c * B * J:(c + 1) * B * J].rearrange("p (b j) -> p b j", b=B)
                    dst = k_all[:, :, c, l - 1, :]
                    if l < 3:
                        last = nc.vector.tensor_scalar(dst, src, bk2[l][:, c:c + 1], None, ALU.add)
                    else:
                        last = nc.vector.tensor_copy(dst, src)
            last.then_inc(kv_sb, 1)

            def quantise(out_q, src, scales, tmp2):
                s_, r_ = scales
                link(nc.vector.tensor_reduce(out=s_, in_=src, axis=X, op=ALU.max, apply_absolute_value=True))
                link(nc.vector.tensor_scalar(s_, s_, 1e-12, 1.0 / QMAX, ALU.max, ALU.mult))
                link(nc.vector.reciprocal(r_, s_))
                link(nc.vector.tensor_scalar(tmp2, src, r_, QMAX, ALU.mult, ALU.min))
                link(nc.vector.tensor_scalar(tmp2, tmp2, -QMAX, MAGIC, ALU.max, ALU.add))
                return nc.vector.tensor_scalar(out_q, tmp2, MAGIC, None, ALU.subtract)

            for c in range(KC):
                link(quantise(rhs_q[:, c, :], rhs_T[:, c, :], (rhs_scale[:, c:c + 1], rhs_scale[:, 2 + c:3 + c]),
                              rhs_T[:, c, :]))
                last = nc.vector.tensor_scalar(diag[:, c, :], ident[:], rhs_scale[:, c:c + 1], None, ALU.mult)
            last.then_inc(kv_sb, 1)

            for b in range(B):
                dve.wait_ge(kv_ps, 2 + b)
                for n in range(4):
                    ks = range(3 * n, min(3 * n + 3, NCH))
                    m = len(ks) * len(LAYERS)
                    last = nc.vector.tensor_tensor(
                        v_bd[:, b, ks[0]:ks[-1] + 1].rearrange("p k l (s d) -> p (k l) s d", d=VW)[:, :, :, 0:ATT],
                        kv_bank(4 * (1 - b) + n)[:, 0:m * SLOTS * ATT].rearrange("p (m s d) -> p m s d", s=SLOTS, d=ATT),
                        rep(slot_mask[:, ks[0]:ks[-1] + 1].rearrange("p k l s -> p (k l) s"), ATT), ALU.mult)
                last.then_inc(kv_sb, 1)
            dve.wait_ge(gathered, 16 * NT)
            for tl in range(NT):
                last = nc.vector.tensor_tensor(x_all[:, tl, :], rows0[tl], x_all[:, tl, :], ALU.add)
            link(last)

            def prep2(b):
                dve.nop(nofuse=True)
                for l in LAYERS:
                    for c in range(KC):
                        src = k_all[:, bass.ds(b, 1), c, l - 1, :].to_broadcast([P, 4, J])
                        last = nc.vector.tensor_tensor(k_bd[:, l - 1, c, :].rearrange("p (q j) -> p q j", j=J), src,
                                                       rep(head_mask[:], J), ALU.mult)
                last.then_inc(k_built, 1)

            def stats2(s, r):
                ln_stats(s, r)

            def apply2(k):
                def step(s, r):
                    if k == 1 and r:
                        dve.wait_ge(streams[s].xn_stored, 16 * (b * ROUNDS + (ROUNDS * B + r)))
                    ln_apply(s, r, 2, 6 * r + k)
                return step

            def half2(l, half):
                def step(s, r):
                    st = streams[s]
                    masked = l == 3 or (s == 0 and r == 0)
                    if masked:
                        k = r + 1 if s else (3 + r if l == 3 else l)
                        dve.wait_ge(st.filled.sem, st.filled.at(2, b, k))
                        dve.nop(nofuse=True)
                    for a in range(2):
                        src, dst = psum_scores(s)[:, a], sbuf_scores(s, half)[:, a]
                        dve.wait_ge(st.s_ps.sem, st.s_ps.at(2, b, 12 * r + 4 * l - 4 + 2 * half + a + 1))
                        if masked:
                            dve.nop(nofuse=True)
                            m = (filled_mask[s] if l == 3 else causal)[:]
                            link(nc.vector.copy_predicated(dst, m.unsqueeze(1).to_broadcast([P, 4, J]), src))
                            src = dst
                        m = mx[s][:, 8 * half + 4 * a:8 * half + 4 * a + 4]
                        link(nc.vector.tensor_reduce(out=m, in_=src, axis=X, op=ALU.max))
                        nc.vector.tensor_tensor(dst, src, rep(m, J), ALU.subtract).then_inc(st.p_sub.sem, 1)
                return step

            def attended(l):
                def step(s, r):
                    st = streams[s]
                    dve.wait_ge(st.o_ps.sem, st.o_ps.at(2, b, 3 * r + l))
                    av = ps[s][:, 0, 0:H * VW].rearrange("p (h d) -> p h d", d=VW)
                    link(nc.vector.reciprocal(mx[s][:], av[:, :, ATT]))
                    nc.vector.tensor_tensor(xn[s][:].rearrange("p (h d) -> p h d", d=ATT), av[:, :, 0:ATT],
                                            rep(mx[s][:], ATT), ALU.mult).then_inc(st.o.sem, 1)
                return step

            def residual2(k):
                def step(s, r):
                    st = streams[s]
                    dve.wait_ge(st.y_ps.sem, st.y_ps.at(2, b, 6 * r + k))
                    if k == 6:
                        nc.vector.tensor_copy(logits3[:, bass.ds(tile(b, s, r), 1), :].rearrange("p a d -> p (a d)"),
                                              ps[s][:, 0, 0:E3]).then_inc(st.x_new.sem, 1)
                        return
                    y = ps[s][:, 0, 0:D]
                    if k == 4:
                        link(nc.vector.scalar_tensor_tensor(out=xn[s][:], in0=y, scalar=scale[s][:, 0:1],
                                                            in1=rhs_scale_row[:], op0=ALU.mult, op1=ALU.mult))
                        y = xn[s][:]
                    nc.vector.tensor_tensor(x_tile(b, s, r), y, x_tile(b, s, r), ALU.add).then_inc(st.x_new.sem, 1)
                    dve.wait_ge(st.x_new.sem, st.x_new.at(2, b, 6 * r + k))
                return step

            def quant(s, r):
                st = streams[s]
                dve.wait_ge(st.xn.sem, st.xn.at(2, b, 6 * r + 4))
                quantise(x_q[s][:], xn[s][:], (scale[s][:, 0:1], scale[s][:, 1:2]), xn[s][:]).then_inc(st.fm.sem, 1)

            own = {"engine": DV}
            for l in LAYERS:
                own |= {f"stats{l}": stats2, f"fstats{l}": stats2, f"apply{l}": apply2(2 * l - 1), f"fapply{l}": apply2(2 * l)}
                own |= {f"half0_{l}": half2(l, 0), f"half1_{l}": half2(l, 1), f"av{l}": attended(l),
                        f"out{l}": residual2(2 * l - 1)}
            own |= dict(fout1=residual2(2), fout2=residual2(4), gate3=residual2(6), quant2=quant)
            with dve.Fori(0, B) as b:
                link.enter(b, DVE_LINKS2)
                prep2(b)
                for f, s, r in order(STEPS2, own):
                    f(s, r)
                for s in range(STREAMS):
                    dve.wait_ge(streams[s].xn_stored, 16 * (b * ROUNDS + ROUNDS * (B + 1)))
            link.leave(B)

            for s in range(STREAMS):
                dve.wait_ge(streams[s].x_new.sem, streams[s].x_new.at(2, B - 1, 12))
            routing(logits3[:], E3, True)
            loads(E3, NB3, MS3)

            slots = route[:, 5:7, :].rearrange("p a n -> p (a n)")
            link(nc.vector.tensor_scalar(blk_of[:], slots, 1.0 / BLK, 0.5 / BLK - 0.5, ALU.mult, ALU.add))
            link(nc.vector.tensor_scalar(blk_of[:], blk_of[:], MAGIC, None, ALU.add))
            link(nc.vector.tensor_scalar(blk_of[:], blk_of[:], MAGIC, None, ALU.subtract))
            link(nc.vector.scalar_tensor_tensor(out=place[:], in0=blk_of[:], scalar=-float(BLK), in1=slots,
                                                op0=ALU.mult, op1=ALU.add))
            link(nc.vector.tensor_tensor(block_hot[:], rep(blk_of[:], NB3),
                                         blks[:, 0:NB3].unsqueeze(1).to_broadcast([P, 2 * NT, NB3]), ALU.is_equal))
            nc.vector.tensor_scalar(block_ids[:, :, 0:NB3], block_hot[:], row[:], None, ALU.mult)
            nc.vector.tensor_tensor(block_ids[:, :, NB3:], block_hot[:], rep(nums[:], NB3), ALU.mult)
            for g in range(4):
                part = slice(g * NT // 2, (g + 1) * NT // 2)
                nc.vector.tensor_tensor(place_hot[:, part, :], rep(place[:, part], BLK),
                                        cols[:].unsqueeze(1).to_broadcast([P, NT // 2, BLK]), ALU.is_equal)\
                    .then_inc(one_hot_ready, 1)
            dve.wait_ge(rank_ready, 3)
            low, high = (ps[3][:, 0, n * NB3:(n + 1) * NB3] for n in range(2))
            number, flag, which = (ids[:, n, :] for n in range(3))
            link(nc.vector.tensor_copy(flag, low))
            link(nc.vector.scalar_tensor_tensor(out=number, in0=high, scalar=float(P), in1=flag, op0=ALU.mult, op1=ALU.add))
            link(nc.vector.tensor_scalar(number, number, float(P), None, ALU.subtract))
            link(nc.vector.tensor_scalar(which, number, float(B * T), -float(B * T), ALU.is_ge, ALU.mult))
            link(nc.vector.tensor_tensor(which, which, number, ALU.add))
            link(nc.vector.tensor_scalar(which, which, 0.0, None, ALU.max))
            nc.vector.tensor_copy(row_id[:], which)
            link(nc.vector.tensor_scalar(flag, number, 0.0, float(4 * B * T), ALU.is_lt, ALU.mult))
            link(nc.vector.tensor_tensor(flag, flag, number, ALU.add))
            nc.vector.tensor_copy(row_slot[:], flag).then_inc(loads_ready, 1)
            with dve.Fori(0, PASSES[3]) as i:
                for n in range(2):
                    for s in range(MS3):
                        st = streams[s]
                        dve.wait_ge(st.f.sem, st.f.at(3, i, n + 1))
                        nc.vector.tensor_tensor(
                            hid3[s][:, 4 * n:4 * n + 4, :].rearrange("p a n -> p (a n)"), ps[2 * s + (n + 1) % 2][:, 1, :],
                            act3[s][:], ALU.mult).then_inc(st.fm.sem, 1)
                for s in range(MS3):
                    st = streams[s]
                    dve.wait_ge(st.y_ps.sem, st.y_ps.at(3, i, 1))
                    dve.wait_ge(results3[s], 16 * i + 16 * PASSES[1])
                    nc.vector.tensor_copy(y3[s][:], ps[2 * s + 1][:, 0, 0:D])\
                        .then_inc(st.x_new.sem, 1)
            per = NT // GROUPS
            for g in range(GROUPS):
                dve.wait_ge(gathered3[g], 32)
                for n in range(2):
                    for tl in range(g * per, (g + 1) * per):
                        last = nc.vector.scalar_tensor_tensor(out=x_all[:, tl, :], in0=rows3[n][:, tl, :],
                                                              scalar=route[:, 2 + n, tl:tl + 1], in1=x_all[:, tl, :],
                                                              op0=ALU.mult, op1=ALU.add)
                    if n == 0:
                        link(last)
                last.then_inc(combined, 1)

        @block.tensor
        def _(pe):
            mm = nc.tensor.matmul
            pe.wait_ge(loaded["ctx"], 16)
            for n, (w, arrived) in enumerate(((wk0, "k"), (wv0, "v"))):
                pe.wait_ge(loaded[arrived], 32)
                for c in range(C0):
                    for kc in range(KC):
                        last = mm(ps[2 * n + c // 4][:, c // 2 % 2, c % 2 * B * J:(c % 2 + 1) * B * J],
                                  w[:, kc, c * P:c * P + P], ctx_all[:, kc].rearrange("p b j -> p (b j)"),
                                  start=kc == 0, stop=kc == KC - 1)
                last.then_inc(kq_ps, 1)
            pe.wait_ge(loaded["qT"], 16)
            for n in range(2 * C0 // 2):
                kc, two = n // 4, n % 4
                pe.wait_ge(kq_sb, 1 if n < 2 else 2 if n < 4 else n - 1)
                for par in range(2):
                    for c in range(2):
                        last = mm(ps[n % 4][:, par, c * B * J:(c + 1) * B * J],
                                  wqT0[D0 * par:D0 * par + D0, 2 * two + c, kc * P:kc * P + P],
                                  kT0[D0 * par:D0 * par + D0, 2 * two + c].rearrange("p b j -> p (b j)"),
                                  start=True, stop=True)
                last.then_inc(kq_ps, 1)
            pe.wait_ge(loaded["o"], 16)
            pe.wait_ge(rel_const, 1)
            pe.wait_ge(kq_sb, 7)
            for g in range(4):
                for par in range(2):
                    last = mm(ps[0][:, g // 2, g % 2 * D:g % 2 * D + D], relv_m[:, par, :], wo0[:, 2 * g + par, :],
                              start=par == 0, stop=par == 1)
            last.then_inc(kq_ps, 1)
            pe.wait_ge(kq_sb, 11)

            def prep(b):
                for s in range(STREAMS):
                    pe.wait_ge(streams[s].x_new.sem, streams[s].x_new.at(0, b, 0))
                pe.wait_ge(vT_ready, b + 1)
                for n in range(3):
                    for k in range(4 * n, min(4 * n + 4, NCH)):
                        m = P if k < NCH - 1 else LAST_CH
                        cs = [c for c in range(C0) if c * 2 * J < k * P + P and (c + 1) * 2 * J > k * P]
                        for i, c in enumerate(cs):
                            at = c * 3 * P + k * P - window(c)
                            last = mm(ps[1 + n][0:m, k % 4 // 2, k % 2 * D:k % 2 * D + D], vT0[:, at:at + m],
                                      wo0[:, c, :], start=i == 0, stop=i == len(cs) - 1)
                    last.then_inc(prep_ps.sem, 1)
                pe.wait_ge(prep_sb.sem, prep_sb.at(0, b, 3))

            def xn_T(s, st_sem, value):
                st = streams[s]
                pe.wait_ge(st_sem, value)
                for c in range(KC):
                    last = nc.tensor.transpose(ps[s][:, 0, c * P:c * P + P], xn[s][:, c * P:c * P + P], ident[:])
                last.then_inc(st.xnT_ps.sem, 1)

            def xnT1(s, r):
                xn_T(s, streams[s].xn.sem, streams[s].xn.at(0, b, 2 * r + 1))

            def xnT2(s, r):
                xn_T(s, streams[s].xn.sem, streams[s].xn.at(0, b, 2 * r + 2))

            def rel_scores(s, r):
                if s or r:
                    return
                st = streams[0]
                pe.wait_ge(loaded["rel"], 48)
                pe.wait_ge(st.xnT.sem, st.xnT.at(0, b, 1))
                for c in range(C0):
                    for kc in range(KC):
                        last = mm(ps[0][:, c // 4, c % 4 * P:c % 4 * P + P], wq0[:, kc, c * P:c * P + P],
                                  xnT[0][:, kc, :], start=kc == 0, stop=kc == KC - 1)
                last.then_inc(st.q_ps.sem, 1)
                for g in range(4):
                    pe.wait_ge(st.q.sem, st.q.at(0, b, 1 + g))
                    for par in range(2):
                        for c in range(2):
                            last = mm(ps[0][:, par, c * EXT:c * EXT + EXT],
                                      qT0[D0 * par:D0 * par + D0, 2 * g + c, :],
                                      relk_ext[D0 * par:D0 * par + D0, :], start=True, stop=True)
                    last.then_inc(st.q_ps.sem, 1)
                pe.wait_ge(st.q.sem, st.q.at(0, b, 5))

            def scores(s, r, half):
                st = streams[s]
                if half == 0:
                    pe.wait_ge(st.xnT.sem, st.xnT.at(0, b, 2 * r + 1))
                for a in range(2):
                    if half == 1:
                        pe.wait_ge(st.p_sub.sem, st.p_sub.at(0, b, 4 * r + a + 1))
                    at = half * HALF + a * QUART
                    for kc in range(KC):
                        last = mm(ps[s][:, a, 0:QUART], xnT[s][:, kc, :],
                                  qk0[:, bass.ds(b, 1), kc, at:at + QUART].rearrange("p a n -> p (a n)"),
                                  start=kc == 0, stop=kc == KC - 1)
                    last.then_inc(st.s_ps.sem, 1)

            def scores0(s, r):
                scores(s, r, 0)

            def scores1(s, r):
                scores(s, r, 1)

            def probs_T(s, phase, n, step):
                st = streams[s]
                if step == 1:
                    pe.wait_ge(st.pT.sem, st.pT.at(phase, b, 3 * n + 1))
                elif phase == 0:
                    pe.wait_ge(st.o.sem, st.o.at(0, b, n + 1))
                else:
                    pe.wait_ge(st.p_exp.sem, st.p_exp.at(2, b, 2 * n + 2))
                for part in ((0, 1), (2,))[step]:
                    for k in range(4 * part, min(4 * part + 4, NCH)):
                        m = P if k < NCH - 1 else LAST_CH
                        last = nc.tensor.transpose(ps[s][0:m, part % 2, k % 4 * P:k % 4 * P + P],
                                                   probs[s][:, k * P:k * P + m], ident[:])
                    last.then_inc(st.pT_ps.sem, 1)

            def pT0(s, r):
                probs_T(s, 0, r, 0)

            def pT1(s, r):
                probs_T(s, 0, r, 1)

            def band_T(s, r):
                if s or r:
                    return
                st = streams[0]
                pe.wait_ge(st.pT.sem, st.pT.at(0, b, 3))
                pe.wait_ge(band_in, 16 * b + 16)
                pe.wait_ge(band_tail, b + 1)
                for g in range(4):
                    last = nc.tensor.transpose(ps[0][:, 0, g * P:g * P + P],
                                               band[:, 4 * g:4 * g + 4, :].rearrange("p h e -> p (h e)"), ident[:])
                last.then_inc(st.q_ps.sem, 1)

            def attn_out(s, r):
                st = streams[s]
                first = s == 0 and r == 0
                pe.wait_ge(st.pT.sem, st.pT.at(0, b, 3 * r + 3))
                if first:
                    pe.wait_ge(st.q.sem, st.q.at(0, b, 6))
                    pe.wait_ge(loaded["rest"], 16 * 5)
                y = ps[s][:, 0, 0:D]
                if first:
                    for g in range(4):
                        mm(y, bandT[:, g, :], relvo[:, g, :], start=g == 0, stop=False)
                for k in range(NCH):
                    m = P if k < NCH - 1 else LAST_CH + 1
                    last = mm(y, probsT[s][0:m, k, :], vo0[0:m, k, :], start=k == 0 and not first, stop=k == NCH - 1)
                last.then_inc(st.y_ps.sem, 1)

            def gate_up(s, phase, i, k_in, k, wg, wu):
                st = streams[s]
                pe.wait_ge(st.xnT.sem, st.xnT.at(phase, i, k_in))
                for a, w in enumerate((wg, wu)):
                    for f in range(FC0):
                        for kc in range(KC):
                            last = mm(ps[s][:, a, f * P:f * P + P], w[:, kc, f * P:f * P + P], xnT[s][:, kc, :],
                                      start=kc == 0, stop=kc == KC - 1)
                last.then_inc(st.f_ps.sem, 1)

            def ffn_down(s, phase, i, k, wd):
                st = streams[s]
                pe.wait_ge(st.fm.sem, st.fm.at(phase, i, k))
                for f in range(FC0):
                    last = mm(ps[s][:, 0, 0:D], hid[s][:, 1, f * P:f * P + P], wd[:, f, :], start=f == 0, stop=f == FC0 - 1)
                return last

            def shared_out(s, r):
                ffn_down(s, 0, b, r + 1, sdw)
                for kc in range(KC):
                    last = mm(ps[s][:, 1, 0:E0], xnT[s][:, kc, :], gate0[:, kc, :], start=kc == 0, stop=kc == KC - 1)
                last.then_inc(streams[s].y_ps.sem, 1)

            pe.wait_ge(consts, CONSTS)
            with pe.Fori(0, B) as b:
                prep(b)
                for f, s, r in order(STEPS1, dict(engine=PE, apply1=xnT1, rel=rel_scores, half0=scores0, half1=scores1, pT0=pT0,
                                                  pT1=pT1, band=band_T, out1=attn_out, apply2=xnT2,
                                                  gate_up=lambda s, r: gate_up(s, 0, b, 2 * r + 2, r + 1, sgw, suw),
                                                  out2=shared_out)):
                    f(s, r)

            def ranks(n_exp, ready):
                pe.wait_ge(one_hot_ready, ready)
                hot = one_hot[:, 0:NT * n_exp].rearrange("p (n e) -> p n e", e=n_exp)
                rank = ps[0][:, 0, 0:NT * n_exp].rearrange("p (n e) -> p n e", e=n_exp)
                mm(rank, squareb[:], hot, start=True, stop=True, skip_group_check=True)
                for n in range(NT - 1):
                    mm(rank[:, n + 1:NT, :], onesb[:], hot[:, n:n + 1, :].to_broadcast([P, NT - 1 - n, n_exp]),
                       start=False, stop=True, skip_group_check=True)
                for n in range(NT):
                    last = mm(ps[1][:, 0, 0:n_exp], onesb[:], hot[:, n, :], start=n == 0, stop=n == NT - 1)
                last.then_inc(rank_ready, 1)

            ranks(E0, 1)
            pe.wait_ge(routed, 1)
            with pe.Fori(0, PASSES[1]) as i:
                for s in range(STREAMS):
                    st = streams[s]
                    pe.wait_ge(st.x_new.sem, st.x_new.at(1, i, 0))
                    xn_T(s, st.rows_loaded, 16 * i + 16)
                for s in range(STREAMS):
                    st = streams[s]
                    pe.wait_ge(st.in_loaded, 16 * i + 16)
                    gate_up(s, 1, i, 1, 1, w_in0[s][:, 0], w_in0[s][:, 1])
                for s in range(STREAMS):
                    pe.wait_ge(streams[s].out_loaded, 16 * i + 16)
                    ffn_down(s, 1, i, 1, w_out0[s]).then_inc(streams[s].y_ps.sem, 1)

            pe.wait_ge(loaded["p2"], 16 * (12 + 8 + 9))
            pe.wait_ge(rep_ready, 1)
            for s in range(STREAMS):
                pe.wait_ge(streams[s].x_new.sem, streams[s].x_new.at(2, 0, 0))
            for l in LAYERS:
                for c in range(KC):
                    for kc in range(KC):
                        last = mm(kv_bank(l - 1)[:, c * B * J:(c + 1) * B * J], w2["wk", l][:, kc, c * P:c * P + P],
                                  ctx_all[:, kc].rearrange("p b j -> p (b j)"), start=kc == 0, stop=kc == KC - 1)
            last.then_inc(kv_ps, 1)
            for b in range(B):
                if b:
                    pe.wait_ge(kv_sb, 1)
                for k in range(NCH):
                    at, cols = FIRST[k] * ATT, SLOTS * ATT
                    v = kv_bank(4 * (1 - b) + k // 3)[:, k % 3 * 3 * cols:(k % 3 + 1) * 3 * cols]
                    for kc in range(KC):
                        mm(v, ctx_rep[:, kc, b, k * P:k * P + P], wv2[:, kc, :, at:at + cols],
                           start=kc == 0, stop=True, skip_group_check=True)
                    last = mm(v[:, 0:2 * cols], ones[:], bv2[:, :, at:at + cols], start=False, stop=True,
                              skip_group_check=True)
                last.then_inc(kv_ps, 1)
            pe.wait_ge(kv_sb, 3)
            qps = ps[2][:, 0, 0:D].bitcast(BF16).rearrange("p (c n) -> p c n", c=KC)
            for kc in range(KC):
                for c in range(KC):
                    nc.tensor.transpose(qps[:, kc, c * P:c * P + P], rhs_q[:, c, kc * P:kc * P + P], identb[:])
            for c in range(KC):
                last = mm(ps[2][:, 1, c * P:c * P + P], onesq[:], diag[:, c, :], start=True, stop=True)
            last.then_inc(rhs_ps, 1)
            pe.wait_ge(rhs_sb, 1)
            pe.wait_ge(kv_sb, 4)

            def apply_T(k):
                def step(s, r):
                    xn_T(s, streams[s].xn.sem, streams[s].xn.at(2, b, 6 * r + k))
                return step

            def q_proj(l):
                def step(s, r):
                    st = streams[s]
                    pe.wait_ge(st.xnT.sem, st.xnT.at(2, b, 5 * r + {1: 1, 2: 3, 3: 4}[l]))
                    for c in range(KC):
                        for kc in range(KC):
                            last = mm(ps[s][:, 0, c * P:c * P + P], w2["wq", l][:, kc, c * P:c * P + P],
                                      xnT[s][:, kc, :], start=kc == 0, stop=kc == KC - 1)
                    last.then_inc(st.q_ps.sem, 1)
                return step

            def half_scores(l, half):
                def step(s, r):
                    st = streams[s]
                    if half == 0:
                        pe.wait_ge(st.q.sem, st.q.at(2, b, 3 * r + l))
                        if l == 1 and r == 0:
                            pe.wait_ge(k_built, b + 1)
                    for a in range(2):
                        if half == 1:
                            pe.wait_ge(st.p_sub.sem, st.p_sub.at(2, b, 12 * r + 4 * l - 4 + a + 1))
                        mm(ps[s][:, a, 0:QUART], qT[s][D0 * a:D0 * a + D0, half, :],
                           k_bd[D0 * a:D0 * a + D0, l - 1, half, :], start=True, stop=True).then_inc(st.s_ps.sem, 1)
                return step

            def values(l):
                def step(s, r):
                    st = streams[s]
                    pe.wait_ge(st.pT.sem, st.pT.at(2, b, 9 * r + 3 * l))
                    for k in range(NCH):
                        m = P if k < NCH - 1 else LAST_CH
                        last = mm(ps[s][:, 0, FIRST[k] * VW:(FIRST[k] + SLOTS) * VW], probsT[s][0:m, k, :],
                                  v_bd[0:m, bass.ds(b, 1), k, l - 1, :].rearrange("p a n -> p (a n)"), start=k == 0, stop=True, skip_group_check=True)
                    last.then_inc(st.o_ps.sem, 1)
                return step

            def out_T(l):
                def step(s, r):
                    st = streams[s]
                    pe.wait_ge(st.o.sem, st.o.at(2, b, 3 * r + l))
                    for c in range(KC):
                        last = nc.tensor.transpose(ps[s][:, 1, c * P:c * P + P], xn[s][:, c * P:c * P + P], ident[:])
                    last.then_inc(st.oT_ps.sem, 1)
                return step

            def out_proj(l):
                def step(s, r):
                    st = streams[s]
                    pe.wait_ge(st.oT.sem, st.oT.at(2, b, 3 * r + l))
                    if l < 3:
                        mm(ps[s][:, 0, 0:D], ones[:], bo2[l][:], start=True, stop=False)
                    for c in range(KC):
                        last = mm(ps[s][:, 0, 0:D], xnT[s][:, c, :], w2["wo", l][:, c, :],
                                  start=c == 0 and l == 3, stop=c == KC - 1)
                    last.then_inc(st.y_ps.sem, 1)
                return step

            def low(s, r):
                st = streams[s]
                pe.wait_ge(st.xnT.sem, st.xnT.at(2, b, 5 * r + 2))
                for kc in range(KC):
                    last = mm(ps[s][0:LOW, 0, 0:P], u1[:, kc, :], xnT[s][:, kc, :], start=kc == 0, stop=kc == KC - 1)
                last.then_inc(st.f_ps.sem, 1)

            def up(s, r):
                st = streams[s]
                pe.wait_ge(st.f.sem, st.f.at(2, b, 4 * r + 1))
                for f in range(F1 // P):
                    last = mm(ps[s][:, f // 4, f % 4 * P:f % 4 * P + P], v1[:, f * P:f * P + P], low_T[s][0:LOW + 1, :],
                              start=True, stop=True)
                last.then_inc(st.f_ps.sem, 1)

            def low2(s, r):
                st = streams[s]
                pe.wait_ge(st.f.sem, st.f.at(2, b, 4 * r + 2))
                for f in range(F1 // P):
                    last = mm(ps[s][0:LOW, 0, 0:P], u2[:, f, :], probs[s][:, f * P:f * P + P],
                              start=f == 0, stop=f == F1 // P - 1)
                last.then_inc(st.f_ps.sem, 1)

            def low_out(s, r):
                st = streams[s]
                pe.wait_ge(st.f.sem, st.f.at(2, b, 4 * r + 3))
                mm(ps[s][:, 0, 0:D], low_T[s][0:LOW + 1, :], v2[:], start=True, stop=True).then_inc(st.y_ps.sem, 1)

            def quant_T(s, r):
                st = streams[s]
                pe.wait_ge(st.fm.sem, st.fm.at(2, b, r + 1))
                for c in range(KC):
                    last = nc.tensor.transpose(ps[s][:, 0, 0:P].bitcast(BF16)[:, c * P:c * P + P],
                                               x_q[s][:, c * P:c * P + P], identb[:])
                last.then_inc(st.f_ps.sem, 1)

            def quant_out(s, r):
                st = streams[s]
                pe.wait_ge(st.f.sem, st.f.at(2, b, 4 * r + 4))
                for kc in range(KC):
                    last = mm(ps[s][:, 0, 0:D], x_qT[s][:, kc * P:kc * P + P], rhs_qT[:, kc, :],
                              start=kc == 0, stop=kc == KC - 1)
                last.then_inc(st.y_ps.sem, 1)

            def gate(s, r):
                st = streams[s]
                pe.wait_ge(st.xnT.sem, st.xnT.at(2, b, 5 * r + 5))
                for kc in range(KC):
                    last = mm(ps[s][:, 0, 0:E3], xnT[s][:, kc, :], gate3[:, kc, :], start=kc == 0, stop=kc == KC - 1)
                last.then_inc(st.y_ps.sem, 1)

            own = {"engine": PE}
            for l in LAYERS:
                own |= {f"apply{l}": apply_T(2 * l - 1), f"q{l}": q_proj(l), f"av{l}": values(l), f"oT{l}": out_T(l),
                        f"out{l}": out_proj(l)}
                own |= {f"half{h}_{l}": half_scores(l, h) for h in range(2)}
                own |= {f"pT{h}_{l}": (lambda s, r, l=l, h=h: probs_T(s, 2, 3 * r + l - 1, h)) for h in range(2)}
            own |= dict(fapply1=apply_T(2), fapply3=apply_T(6), low1=low, gelu1=up, low21=low2, fout1=low_out,
                        quant2=quant_T, fout2=quant_out, gate3=gate)
            with pe.Fori(0, B) as b:
                for f, s, r in order(STEPS2, own):
                    f(s, r)

            ranks(E3, 2)
            for u in range(2 * NT):
                if u % (NT // 2) == 0:
                    pe.wait_ge(one_hot_ready, 3 + u // (NT // 2))
                last = mm(ps[3][:, 0, 0:2 * NB3], place_hot[:, u, :], block_ids[:, u, :], start=u == 0, stop=u == 2 * NT - 1)
            last.then_inc(rank_ready, 1)
            with pe.Fori(0, PASSES[3]) as i:
                for s in range(MS3):
                    st = streams[s]
                    pe.wait_ge(st.x_new.sem, st.x_new.at(3, i, 0))
                    pe.wait_ge(rows3_loaded[s], 16 * i + 16 * (PASSES[1] + 1))
                    for c in range(KC):
                        last = nc.tensor.transpose(ps[2 * s][:, 0, c * P:c * P + P], x_in[s][:, c * P:c * P + P], ident[:])
                    last.then_inc(st.xnT_ps.sem, 1)
                for n in range(2):
                    for s in range(MS3):
                        st = streams[s]
                        if n == 0:
                            pe.wait_ge(st.in_loaded, 16 * i + 16 * (PASSES[1] + 1))
                            pe.wait_ge(st.xnT.sem, st.xnT.at(3, i, 1))
                        for a in range(2):
                            for f in range(4):
                                for kc in range(KC):
                                    at = (4 * n + f) * P
                                    last = mm(ps[2 * s + 1 - n][:, a, f * BLK:(f + 1) * BLK],
                                              w_in3[s][:, a, kc, at:at + P], x_inT[s][:, kc, :],
                                              start=kc == 0, stop=kc == KC - 1)
                        last.then_inc(st.f_ps.sem, 1)
                for s in range(MS3):
                    st = streams[s]
                    pe.wait_ge(st.fm.sem, st.fm.at(3, i, 2))
                    pe.wait_ge(st.out_loaded, 16 * i + 16 * (PASSES[1] + 1))
                    for f in range(F3 // P):
                        last = mm(ps[2 * s + 1][:, 0, 0:D], hid3[s][:, f, :], w_out3[s][:, f, :],
                                  start=f == 0, stop=f == F3 // P - 1)
                    last.then_inc(st.y_ps.sem, 1)


def kernel(**inputs):
    import concourse.bacc as bacc
    from concourse.bass_utils import run_bass_kernel_spmd

    a = {k: np.asarray(v) for k, v in inputs.items()}

    def rows_of(*ws):
        e, cp, n = ws[0].shape
        return np.stack(ws, 1).reshape(e, len(ws), cp // P, P, n).transpose(0, 3, 1, 2, 4).reshape(e * P, -1)

    relk, relv = a["L0_xattn_rel_k"], a["L0_xattn_rel_v"]
    dist = np.clip(np.arange(EXT) - (P - 1), -MAXREL, MAXREL) + MAXREL
    arrays = {
        "x": a["x"],
        "ctxT": a["ctx_1024"].transpose(2, 0, 1),
        "Wq0": a["L0_xattn_Wq"], "WqT0": a["L0_xattn_Wq"].T, "Wk0": a["L0_xattn_Wk"], "Wv0": a["L0_xattn_Wv"],
        "Wo0": a["L0_xattn_Wo"], "bo0": a["L0_xattn_bo"][None],
        "relk_ext": np.concatenate([relk[dist].T] * 2), "relk_0": np.concatenate([relk[0]] * 2)[:, None],
        "relv_T": np.concatenate([relv[1:].T] * 2), "relv_0": np.concatenate([relv[0]] * 2)[:, None],
        "sgw": a["L0_ffn_shared_gate_w"], "suw": a["L0_ffn_shared_up_w"], "sdw": a["L0_ffn_shared_down_w"],
        "gate0": a["L0_ffn_gate_w"],
        "w_in0": rows_of(a["L0_ffn_routed_gate_w"], a["L0_ffn_routed_up_w"]), "w_out0": rows_of(a["L0_ffn_routed_down_w"]),
        "w_in3": rows_of(a["L3_ffn_w1"].transpose(0, 2, 1), a["L3_ffn_w3"].transpose(0, 2, 1)),
        "w_out3": rows_of(a["L3_ffn_w2"].transpose(0, 2, 1)), "gate3": a["L3_ffn_gate_w"].T,
        "u1": a["L1_ffn_U1"], "u2": a["L1_ffn_U2"],
        "v1": np.concatenate([a["L1_ffn_V1"], a["L1_ffn_b1"][None]]),
        "v2": np.concatenate([a["L1_ffn_V2"], a["L1_ffn_b2"][None]]),
        "rhsT": a["L2_ffn_rhs"].T,
        "mask": np.ascontiguousarray(a["mask_BxSxS2_bk0"].reshape(NT, P, J).transpose(1, 0, 2)).reshape(P, NT * J)
        .view(np.int32),
    }
    for l in (1, 2):
        arrays |= {f"w{n.lower()}{l}": a[f"L{l}_xattn_W{n}"].T for n in "qkvo"}
        arrays |= {f"b{n}{l}": a[f"L{l}_xattn_b{n}"].reshape(KC, P).T for n in "qk"}
        arrays |= {f"b{n}{l}": a[f"L{l}_xattn_b{n}"][None] for n in "vo"}
    arrays |= {f"w{n}3": a[f"L3_xattn_w_{n}"].T for n in "qkvo"}
    p = np.arange(P)
    arrays["head_mask"] = (p[:, None] % D0 // ATT == np.arange(4)).astype(np.float32)
    mask = (P * np.arange(NCH)[:, None] + p[:, None, None]) // J == np.array(FIRST)[:, None] + np.arange(SLOTS)
    arrays["slot_mask"] = np.repeat(mask[:, :, None].astype(np.float32), len(LAYERS), 2)
    arrays["rev"] = np.broadcast_to(np.arange(E0, 0, -1, dtype=np.float32), (P, E0))
    arrays["kstep"] = np.broadcast_to(BLK * np.arange(B * T // BLK, dtype=np.float32), (P, B * T // BLK))
    arrays["blks"] = np.broadcast_to(np.arange(NB0, dtype=np.float32), (P, NB0))
    arrays["row"] = p[:, None].astype(np.float32)
    arrays["cols"] = np.broadcast_to(np.arange(BLK, dtype=np.float32), (P, BLK))
    arrays["nums"] = np.broadcast_to(np.arange(1, 2 * NT + 1, dtype=np.float32), (P, 2 * NT))
    arrays["low_tri"] = np.broadcast_to(np.tri(E0, dtype=np.float32), (P, E0, E0))
    arrays = {k: np.ascontiguousarray(v) for k, v in arrays.items()}
    nc = bacc.Bacc("TRN2", target_bir_lowering=False, num_devices=1)
    tensors = {k: nc.dram_tensor(k, v.shape, mybir.dt.from_np(v.dtype), kind="ExternalInput").ap()
               for k, v in arrays.items()}
    out = nc.dram_tensor("out", (B, T, D), F32, kind="ExternalOutput")
    build(nc, tensors, out.ap())
    r = run_bass_kernel_spmd(nc, [arrays], core_ids=[0])
    return r.results[0]["out"]
```
